# Optimizing a Trainium2 kernel written in Bass

```python
import numpy as np
import jax
import jax.numpy as jnp

def _softmax(x, axis=-1):
    return jax.nn.softmax(x, axis=axis)

def _gelu(x):
    return jax.nn.gelu(x, approximate=True)

def _silu(x):
    return jax.nn.silu(x)

def _sigmoid(x):
    return jax.nn.sigmoid(x)

def _layernorm(x, axis=-1, eps=1e-05):
    m = jnp.mean(x, axis=axis, keepdims=True)
    v = jnp.var(x, axis=axis, keepdims=True)
    return (x - m) / jnp.sqrt(v + eps)

def _scatter_add(tgt, idx, src, axis=0):
    return tgt.at[idx].add(src)

def _segment_sum(src, seg, n):
    return jax.ops.segment_sum(src, seg, n)
kernel_name = 'mk_decoder_postln_d2_seqx_r4_166b43'

def setup_inputs(seed: int=0):
    np.random.seed(seed)
    _w = jnp.asarray

    def _rec_inputs():
        import jax
        import jax.numpy as jnp
        _rk = jax.random.key(seed)
        x = 7.22e-05 + 1 * jax.random.normal(jax.random.fold_in(_rk, 1), (4, 512, 256), jnp.float32)
        _lenS = 512 - jax.random.randint(jax.random.fold_in(_rk, 7), (4,), 0, max(1, 512 // 4) + 1, jnp.int32)
        _lenS2 = 1024 - jax.random.randint(jax.random.fold_in(_rk, 8), (4,), 0, max(1, 1024 // 4) + 1, jnp.int32)
        _ctx_768P = jax.random.normal(jax.random.fold_in(_rk, 11), (4, 16, 192), jnp.float32)
        _ctx_768c = jax.random.dirichlet(jax.random.fold_in(_rk, 511), 0.3 * jnp.ones((16,), jnp.float32), (4, 1024))
        _ctx_768t = jnp.einsum('bsk,bkd->bsd', _ctx_768c, _ctx_768P)
        _ctx_768t = _ctx_768t * jax.lax.rsqrt(jnp.mean(jnp.square(_ctx_768t)) + 1e-12) * 0.953939
        ctx_768 = 2.09791e-05 + 1.00001 * (_ctx_768t + 0.3 * jax.random.normal(jax.random.fold_in(_rk, 611), (4, 1024, 192), jnp.float32))
        return (x, ctx_768)
    x, ctx_768 = _rec_inputs()

    def _L0_attn_setup():
        import jax, jax.numpy as jnp
        import numpy as np
        N_EMBD = 256
        N_HEAD = 16
        SEQ = 512
        BATCH = 2
        NEG = -1000000000.0
        key = jax.random.key(seed)
        k0, k1, k2 = jax.random.split(key, 3)
        return {'hidden_states': jax.random.normal(k0, (BATCH, SEQ, N_EMBD), dtype=jnp.float32), 'w_attn': jax.random.normal(k1, (3 * N_EMBD, N_EMBD), dtype=jnp.float32) * 0.02, 'b_attn': jnp.zeros((3 * N_EMBD,), dtype=jnp.float32), 'w_proj': jax.random.normal(k2, (N_EMBD, N_EMBD), dtype=jnp.float32) * 0.02, 'b_proj': jnp.zeros((N_EMBD,), dtype=jnp.float32)}
    _L0_attn_all = _L0_attn_setup()
    _L0_attn_in = {k: v for k, v in _L0_attn_all.items() if k in ('w_attn', 'b_attn', 'w_proj', 'b_proj')}
    del _L0_attn_all

    def _L0_xattn_setup():
        import jax, jax.numpy as jnp
        import numpy as np
        IN_DIM = 256
        CTX_DIM = 192
        NUM_HEADS = 16
        HEAD_DIM = IN_DIM // NUM_HEADS
        SCALE = 1.0 / float(np.sqrt(HEAD_DIM))
        key = jax.random.key(seed)
        ks = jax.random.split(key, 10)
        B, NQ, NKV = (8, 256, 128)
        s_in = 1.0 / float(np.sqrt(IN_DIM))
        s_ctx = 1.0 / float(np.sqrt(CTX_DIM))
        return {'x': jax.random.normal(ks[0], (B, NQ, IN_DIM), dtype=jnp.float32), 'context': jax.random.normal(ks[1], (B, NKV, CTX_DIM), dtype=jnp.float32), 'Wq': jax.random.normal(ks[2], (IN_DIM, IN_DIM), dtype=jnp.float32) * s_in, 'bq': jax.random.normal(ks[3], (IN_DIM,), dtype=jnp.float32) * 0.01, 'Wk': jax.random.normal(ks[4], (IN_DIM, CTX_DIM), dtype=jnp.float32) * s_ctx, 'bk': jax.random.normal(ks[5], (IN_DIM,), dtype=jnp.float32) * 0.01, 'Wv': jax.random.normal(ks[6], (IN_DIM, CTX_DIM), dtype=jnp.float32) * s_ctx, 'bv': jax.random.normal(ks[7], (IN_DIM,), dtype=jnp.float32) * 0.01, 'Wo': jax.random.normal(ks[8], (IN_DIM, IN_DIM), dtype=jnp.float32) * s_in, 'bo': jax.random.normal(ks[9], (IN_DIM,), dtype=jnp.float32) * 0.01}
    _L0_xattn_all = _L0_xattn_setup()
    _L0_xattn_in = {k: v for k, v in _L0_xattn_all.items() if k in ('Wq', 'bq', 'Wk', 'bk', 'Wv', 'bv', 'Wo', 'bo')}
    del _L0_xattn_all

    def _L0_ffn_setup():
        import jax, jax.numpy as jnp
        import numpy as np
        B, SEQ, DIM = (2, 1024, 256)
        E, S = (8, 128)
        HID = 4 * DIM
        SCALE = DIM ** 0.5

        def rmsnorm(x, gamma):
            n = jnp.linalg.norm(x, axis=-1, keepdims=True)
            return x / jnp.maximum(n, 1e-12) * SCALE * gamma
        key = jax.random.key(seed)
        ks = jax.random.split(key, 4)
        w_init = lambda k, shape: jax.random.normal(k, shape, dtype=jnp.float32) * 0.02
        return {'x': jax.random.normal(ks[0], (B, SEQ, DIM), dtype=jnp.float32), 'norm_gamma': jnp.ones((DIM,), jnp.float32), 'slot_norm_gamma': jnp.ones((DIM,), jnp.float32), 'slot_embeds': jax.random.normal(ks[1], (E, S, DIM), dtype=jnp.float32), 'w1': w_init(ks[2], (E, DIM, HID)), 'b1': jnp.zeros((E, HID), jnp.float32), 'w2': w_init(ks[3], (E, HID, DIM)), 'b2': jnp.zeros((E, DIM), jnp.float32)}
    _L0_ffn_all = _L0_ffn_setup()
    _L0_ffn_in = {k: v for k, v in _L0_ffn_all.items() if k in ('norm_gamma', 'slot_norm_gamma', 'slot_embeds', 'w1', 'b1', 'w2', 'b2')}
    del _L0_ffn_all

    def _L1_attn_setup():
        import jax, jax.numpy as jnp
        import numpy as np
        B, T, D, H = (4, 512, 256, 16)
        HD = D // H
        key = jax.random.key(seed)
        k1, k2, k3 = jax.random.split(key, 3)
        scale = 1.0 / np.sqrt(D)
        x = jax.random.normal(k1, (B, T, D), dtype=jnp.float32)
        w_qkv = jax.random.normal(k2, (D, 3 * D), dtype=jnp.float32) * scale
        w_o = jax.random.normal(k3, (D, D), dtype=jnp.float32) * scale
        return {'x': x, 'w_qkv': w_qkv, 'w_o': w_o}
    _L1_attn_all = _L1_attn_setup()
    _L1_attn_in = {k: v for k, v in _L1_attn_all.items() if k in ('w_qkv', 'w_o')}
    del _L1_attn_all

    def _L1_xattn_setup():
        import jax, jax.numpy as jnp
        import numpy as np
        N_HEADS = 16
        DIM_EMBED = 256
        DIM_CROSS = 192
        DIM_HEAD = DIM_EMBED // N_HEADS
        key = jax.random.key(seed)
        ks = jax.random.split(key, 10)
        B, Sq, Sk = (8, 1024, 77)
        s_e = 1.0 / np.sqrt(DIM_EMBED)
        s_c = 1.0 / np.sqrt(DIM_CROSS)
        return {'x': jax.random.normal(ks[0], (B, Sq, DIM_EMBED), jnp.float32), 'y': jax.random.normal(ks[1], (B, Sk, DIM_CROSS), jnp.float32), 'wq': jax.random.normal(ks[2], (DIM_EMBED, DIM_EMBED), jnp.float32) * s_e, 'bq': jax.random.normal(ks[3], (DIM_EMBED,), jnp.float32) * 0.01, 'wk': jax.random.normal(ks[4], (DIM_CROSS, DIM_EMBED), jnp.float32) * s_c, 'bk': jax.random.normal(ks[5], (DIM_EMBED,), jnp.float32) * 0.01, 'wv': jax.random.normal(ks[6], (DIM_CROSS, DIM_EMBED), jnp.float32) * s_c, 'bv': jax.random.normal(ks[7], (DIM_EMBED,), jnp.float32) * 0.01, 'wo': jax.random.normal(ks[8], (DIM_EMBED, DIM_EMBED), jnp.float32) * s_e, 'bo': jax.random.normal(ks[9], (DIM_EMBED,), jnp.float32) * 0.01}
    _L1_xattn_all = _L1_xattn_setup()
    _L1_xattn_in = {k: v for k, v in _L1_xattn_all.items() if k in ('wq', 'bq', 'wk', 'bk', 'wv', 'bv', 'wo', 'bo')}
    del _L1_xattn_all

    def _L1_ffn_setup():
        import jax, jax.numpy as jnp
        import numpy as np
        N_HEAD = 16
        NUM_EXPERTS = 8
        TOP_K = 2
        LN_EPS = 1e-05

        def _layernorm(x, g, b):
            mu = jnp.mean(x, axis=-1, keepdims=True)
            var = jnp.mean(jnp.square(x - mu), axis=-1, keepdims=True)
            return (x - mu) * jax.lax.rsqrt(var + LN_EPS) * g + b

        def _attention(h, Wq, bq, Wk, bk, Wv, bv, Wp, bp):
            B, T, D = h.shape
            hd = D // N_HEAD

            def split(z):
                return z.reshape(B, T, N_HEAD, hd).transpose(0, 2, 1, 3)
            q = split(h @ Wq + bq)
            k = split(h @ Wk + bk)
            v = split(h @ Wv + bv)
            att = jnp.einsum('bhqd,bhkd->bhqk', q, k) / jnp.sqrt(jnp.float32(hd))
            causal = jnp.tril(jnp.ones((T, T), bool))
            att = jnp.where(causal, att, -jnp.inf)
            att = jax.nn.softmax(att, axis=-1)
            y = jnp.einsum('bhqk,bhkd->bhqd', att, v)
            y = y.transpose(0, 2, 1, 3).reshape(B, T, D)
            return y @ Wp + bp

        def _token_moe(h, gate_W, gate_b, exp_W1, exp_b1, exp_W2, exp_b2):
            B, T, D = h.shape
            flat = h.reshape(-1, D)
            N = flat.shape[0]
            logits = flat @ gate_W + gate_b
            top_v, top_i = jax.lax.top_k(logits, TOP_K)
            w = jax.nn.softmax(top_v, axis=-1)
            w_full = jnp.zeros((N, NUM_EXPERTS), flat.dtype)
            w_full = w_full.at[jnp.arange(N)[:, None], top_i].add(w)
            out = jnp.zeros_like(flat)
            for e in range(NUM_EXPERTS):
                mid = jax.nn.gelu(flat @ exp_W1[e] + exp_b1[e], approximate=False)
                y_e = mid @ exp_W2[e] + exp_b2[e]
                out = out + w_full[:, e:e + 1] * y_e
            return out.reshape(B, T, D)
        key = jax.random.key(seed)
        B, T, D = (8, 256, 256)
        H = 4 * D
        E = NUM_EXPERTS
        ks = jax.random.split(key, 24)
        s = 0.02
        inp = {'x': jax.random.normal(ks[0], (B, T, D), jnp.float32), 'ln1_g': jnp.ones((D,), jnp.float32), 'ln1_b': jnp.zeros((D,), jnp.float32), 'ln2_g': jnp.ones((D,), jnp.float32), 'ln2_b': jnp.zeros((D,), jnp.float32), 'Wq': jax.random.normal(ks[1], (D, D), jnp.float32) * s, 'bq': jnp.zeros((D,), jnp.float32), 'Wk': jax.random.normal(ks[2], (D, D), jnp.float32) * s, 'bk': jnp.zeros((D,), jnp.float32), 'Wv': jax.random.normal(ks[3], (D, D), jnp.float32) * s, 'bv': jnp.zeros((D,), jnp.float32), 'Wp': jax.random.normal(ks[4], (D, D), jnp.float32) * s, 'bp': jnp.zeros((D,), jnp.float32), 'gate_W': jax.random.normal(ks[5], (D, E), jnp.float32) * s, 'gate_b': jnp.zeros((E,), jnp.float32), 'exp_W1': jax.random.normal(ks[6], (E, D, H), jnp.float32) * s, 'exp_b1': jnp.zeros((E, H), jnp.float32), 'exp_W2': jax.random.normal(ks[7], (E, H, D), jnp.float32) * s, 'exp_b2': jnp.zeros((E, D), jnp.float32)}
        return inp
    _L1_ffn_all = _L1_ffn_setup()
    _L1_ffn_in = {k: v for k, v in _L1_ffn_all.items() if k in ('ln1_g', 'ln1_b', 'ln2_g', 'ln2_b', 'Wq', 'bq', 'Wk', 'bk', 'Wv', 'bv', 'Wp', 'bp', 'gate_W', 'gate_b', 'exp_W1', 'exp_b1', 'exp_W2', 'exp_b2')}
    del _L1_ffn_all
    return {'x': x, 'ctx_768': ctx_768, 'L0_attn_w_attn': _L0_attn_in['w_attn'], 'L0_attn_b_attn': _L0_attn_in['b_attn'], 'L0_attn_w_proj': _L0_attn_in['w_proj'], 'L0_attn_b_proj': _L0_attn_in['b_proj'], 'L0_xattn_Wq': _L0_xattn_in['Wq'], 'L0_xattn_bq': _L0_xattn_in['bq'], 'L0_xattn_Wk': _L0_xattn_in['Wk'], 'L0_xattn_bk': _L0_xattn_in['bk'], 'L0_xattn_Wv': _L0_xattn_in['Wv'], 'L0_xattn_bv': _L0_xattn_in['bv'], 'L0_xattn_Wo': _L0_xattn_in['Wo'], 'L0_xattn_bo': _L0_xattn_in['bo'], 'L0_ffn_norm_gamma': _L0_ffn_in['norm_gamma'], 'L0_ffn_slot_norm_gamma': _L0_ffn_in['slot_norm_gamma'], 'L0_ffn_slot_embeds': _L0_ffn_in['slot_embeds'], 'L0_ffn_w1': _L0_ffn_in['w1'], 'L0_ffn_b1': _L0_ffn_in['b1'], 'L0_ffn_w2': _L0_ffn_in['w2'], 'L0_ffn_b2': _L0_ffn_in['b2'], 'L1_attn_w_qkv': _L1_attn_in['w_qkv'], 'L1_attn_w_o': _L1_attn_in['w_o'], 'L1_xattn_wq': _L1_xattn_in['wq'], 'L1_xattn_bq': _L1_xattn_in['bq'], 'L1_xattn_wk': _L1_xattn_in['wk'], 'L1_xattn_bk': _L1_xattn_in['bk'], 'L1_xattn_wv': _L1_xattn_in['wv'], 'L1_xattn_bv': _L1_xattn_in['bv'], 'L1_xattn_wo': _L1_xattn_in['wo'], 'L1_xattn_bo': _L1_xattn_in['bo'], 'L1_ffn_ln1_g': _L1_ffn_in['ln1_g'], 'L1_ffn_ln1_b': _L1_ffn_in['ln1_b'], 'L1_ffn_ln2_g': _L1_ffn_in['ln2_g'], 'L1_ffn_ln2_b': _L1_ffn_in['ln2_b'], 'L1_ffn_Wq': _L1_ffn_in['Wq'], 'L1_ffn_bq': _L1_ffn_in['bq'], 'L1_ffn_Wk': _L1_ffn_in['Wk'], 'L1_ffn_bk': _L1_ffn_in['bk'], 'L1_ffn_Wv': _L1_ffn_in['Wv'], 'L1_ffn_bv': _L1_ffn_in['bv'], 'L1_ffn_Wp': _L1_ffn_in['Wp'], 'L1_ffn_bp': _L1_ffn_in['bp'], 'L1_ffn_gate_W': _L1_ffn_in['gate_W'], 'L1_ffn_gate_b': _L1_ffn_in['gate_b'], 'L1_ffn_exp_W1': _L1_ffn_in['exp_W1'], 'L1_ffn_exp_b1': _L1_ffn_in['exp_b1'], 'L1_ffn_exp_W2': _L1_ffn_in['exp_W2'], 'L1_ffn_exp_b2': _L1_ffn_in['exp_b2']}

def reference(x, ctx_768, L0_attn_w_attn, L0_attn_b_attn, L0_attn_w_proj, L0_attn_b_proj, L0_xattn_Wq, L0_xattn_bq, L0_xattn_Wk, L0_xattn_bk, L0_xattn_Wv, L0_xattn_bv, L0_xattn_Wo, L0_xattn_bo, L0_ffn_norm_gamma, L0_ffn_slot_norm_gamma, L0_ffn_slot_embeds, L0_ffn_w1, L0_ffn_b1, L0_ffn_w2, L0_ffn_b2, L1_attn_w_qkv, L1_attn_w_o, L1_xattn_wq, L1_xattn_bq, L1_xattn_wk, L1_xattn_bk, L1_xattn_wv, L1_xattn_bv, L1_xattn_wo, L1_xattn_bo, L1_ffn_ln1_g, L1_ffn_ln1_b, L1_ffn_ln2_g, L1_ffn_ln2_b, L1_ffn_Wq, L1_ffn_bq, L1_ffn_Wk, L1_ffn_bk, L1_ffn_Wv, L1_ffn_bv, L1_ffn_Wp, L1_ffn_bp, L1_ffn_gate_W, L1_ffn_gate_b, L1_ffn_exp_W1, L1_ffn_exp_b1, L1_ffn_exp_W2, L1_ffn_exp_b2):
    import jax
    import jax.numpy as jnp

    def _L0_attn_ref(hidden_states, w_attn, b_attn, w_proj, b_proj):
        import jax, jax.numpy as jnp
        import numpy as np
        N_EMBD = 256
        N_HEAD = 16
        SEQ = 512
        BATCH = 2
        NEG = -1000000000.0
        B, S, E = hidden_states.shape
        H = N_HEAD
        D = E // H
        qkv = hidden_states @ w_attn.T + b_attn
        q, k, v = jnp.split(qkv, 3, axis=-1)
        split = lambda t: t.reshape(B, S, H, D).transpose(0, 2, 1, 3)
        q, k, v = (split(q), split(k), split(v))
        w = jnp.einsum('bhnd,bhmd->bhnm', q, k) * jax.lax.rsqrt(float(D))
        mask = jnp.tril(jnp.ones((S, S), dtype=jnp.float32))
        w = jnp.where(mask > 0, w, NEG)
        w = jax.nn.softmax(w, axis=-1)
        attn = jnp.einsum('bhnm,bhmd->bhnd', w, v)
        attn = attn.transpose(0, 2, 1, 3).reshape(B, S, E)
        return attn @ w_proj.T + b_proj

    def _L0_xattn_ref(x, context, Wq, bq, Wk, bk, Wv, bv, Wo, bo):
        import jax, jax.numpy as jnp
        import numpy as np
        IN_DIM = 256
        CTX_DIM = 192
        NUM_HEADS = 16
        HEAD_DIM = IN_DIM // NUM_HEADS
        SCALE = 1.0 / float(np.sqrt(HEAD_DIM))
        q = x @ Wq.T + bq
        k = context @ Wk.T + bk
        v = context @ Wv.T + bv
        B, NQ, _ = q.shape
        NKV = k.shape[1]
        q = q.reshape(B, NQ, NUM_HEADS, HEAD_DIM)
        k = k.reshape(B, NKV, NUM_HEADS, HEAD_DIM)
        v = v.reshape(B, NKV, NUM_HEADS, HEAD_DIM)
        attn = jnp.einsum('bihd,bjhd->bhij', q, k) * SCALE
        attn = jax.nn.softmax(attn, axis=-1)
        out = jnp.einsum('bhij,bjhd->bihd', attn, v)
        out = out.reshape(B, NQ, IN_DIM)
        return out @ Wo.T + bo

    def _L0_ffn_ref(x, norm_gamma, slot_norm_gamma, slot_embeds, w1, b1, w2, b2):
        import jax, jax.numpy as jnp
        import numpy as np
        B, SEQ, DIM = (2, 1024, 256)
        E, S = (8, 128)
        HID = 4 * DIM
        SCALE = DIM ** 0.5

        def rmsnorm(x, gamma):
            n = jnp.linalg.norm(x, axis=-1, keepdims=True)
            return x / jnp.maximum(n, 1e-12) * SCALE * gamma
        xn = rmsnorm(x, norm_gamma)
        sn = rmsnorm(slot_embeds, slot_norm_gamma)
        logits = jnp.einsum('bnd,esd->bnes', xn, sn)
        dispatch = jax.nn.softmax(logits, axis=1)
        b, n, e, s = logits.shape
        combine = jax.nn.softmax(logits.reshape(b, n, e * s), axis=-1)
        slots = jnp.einsum('bnd,bnes->besd', xn, dispatch)
        h = jnp.einsum('besd,edh->besh', slots, w1) + b1[None, :, None, :]
        h = jax.nn.gelu(h, approximate=False)
        eo = jnp.einsum('besh,ehd->besd', h, w2) + b2[None, :, None, :]
        eo = eo.reshape(b, e * s, DIM)
        out = jnp.einsum('bmd,bnm->bnd', eo, combine)
        return out

    def _L1_attn_ref(x, w_qkv, w_o):
        import jax, jax.numpy as jnp
        import numpy as np
        B, T, D, H = (4, 512, 256, 16)
        HD = D // H
        b, t, d = x.shape
        qkv = jnp.einsum('btd,de->bte', x, w_qkv)
        q, k, v = jnp.split(qkv, 3, axis=-1)
        q = q.reshape(b, t, H, HD).transpose(0, 2, 1, 3)
        k = k.reshape(b, t, H, HD).transpose(0, 2, 1, 3)
        v = v.reshape(b, t, H, HD).transpose(0, 2, 1, 3)
        scores = jnp.einsum('bhqd,bhkd->bhqk', q, k) * (1.0 / jnp.sqrt(jnp.asarray(HD, x.dtype)))
        causal = jnp.tril(jnp.ones((t, t), dtype=bool))
        scores = jnp.where(causal[None, None, :, :], scores, -jnp.inf)
        weights = jax.nn.softmax(scores, axis=-1)
        out = jnp.einsum('bhqk,bhkd->bhqd', weights, v)
        out = out.transpose(0, 2, 1, 3).reshape(b, t, d)
        return jnp.einsum('btd,de->bte', out, w_o)

    def _L1_xattn_ref(x, y, wq, bq, wk, bk, wv, bv, wo, bo):
        import jax, jax.numpy as jnp
        import numpy as np
        N_HEADS = 16
        DIM_EMBED = 256
        DIM_CROSS = 192
        DIM_HEAD = DIM_EMBED // N_HEADS
        B, Sq, E = x.shape
        H, D = (N_HEADS, DIM_HEAD)
        q = (x @ wq + bq).reshape(B, Sq, H, D).transpose(0, 2, 1, 3)
        k = (y @ wk + bk).reshape(B, -1, H, D).transpose(0, 2, 1, 3)
        v = (y @ wv + bv).reshape(B, -1, H, D).transpose(0, 2, 1, 3)
        scores = jnp.einsum('bhqd,bhkd->bhqk', q, k) / jnp.sqrt(jnp.asarray(D, x.dtype))
        attn = jax.nn.softmax(scores, axis=-1)
        out = jnp.einsum('bhqk,bhkd->bhqd', attn, v)
        out = out.transpose(0, 2, 1, 3).reshape(B, Sq, E)
        return out @ wo + bo

    def _L1_ffn_ref(x, ln1_g, ln1_b, ln2_g, ln2_b, Wq, bq, Wk, bk, Wv, bv, Wp, bp, gate_W, gate_b, exp_W1, exp_b1, exp_W2, exp_b2):
        import jax, jax.numpy as jnp
        import numpy as np
        N_HEAD = 16
        NUM_EXPERTS = 8
        TOP_K = 2
        LN_EPS = 1e-05

        def _layernorm(x, g, b):
            mu = jnp.mean(x, axis=-1, keepdims=True)
            var = jnp.mean(jnp.square(x - mu), axis=-1, keepdims=True)
            return (x - mu) * jax.lax.rsqrt(var + LN_EPS) * g + b

        def _attention(h, Wq, bq, Wk, bk, Wv, bv, Wp, bp):
            B, T, D = h.shape
            hd = D // N_HEAD

            def split(z):
                return z.reshape(B, T, N_HEAD, hd).transpose(0, 2, 1, 3)
            q = split(h @ Wq + bq)
            k = split(h @ Wk + bk)
            v = split(h @ Wv + bv)
            att = jnp.einsum('bhqd,bhkd->bhqk', q, k) / jnp.sqrt(jnp.float32(hd))
            causal = jnp.tril(jnp.ones((T, T), bool))
            att = jnp.where(causal, att, -jnp.inf)
            att = jax.nn.softmax(att, axis=-1)
            y = jnp.einsum('bhqk,bhkd->bhqd', att, v)
            y = y.transpose(0, 2, 1, 3).reshape(B, T, D)
            return y @ Wp + bp

        def _token_moe(h, gate_W, gate_b, exp_W1, exp_b1, exp_W2, exp_b2):
            B, T, D = h.shape
            flat = h.reshape(-1, D)
            N = flat.shape[0]
            logits = flat @ gate_W + gate_b
            top_v, top_i = jax.lax.top_k(logits, TOP_K)
            w = jax.nn.softmax(top_v, axis=-1)
            w_full = jnp.zeros((N, NUM_EXPERTS), flat.dtype)
            w_full = w_full.at[jnp.arange(N)[:, None], top_i].add(w)
            out = jnp.zeros_like(flat)
            for e in range(NUM_EXPERTS):
                mid = jax.nn.gelu(flat @ exp_W1[e] + exp_b1[e], approximate=False)
                y_e = mid @ exp_W2[e] + exp_b2[e]
                out = out + w_full[:, e:e + 1] * y_e
            return out.reshape(B, T, D)
        x = x + _attention(_layernorm(x, ln1_g, ln1_b), Wq, bq, Wk, bk, Wv, bv, Wp, bp)
        x = x + _token_moe(_layernorm(x, ln2_g, ln2_b), gate_W, gate_b, exp_W1, exp_b1, exp_W2, exp_b2)
        return x
    x = _layernorm(x + _L0_attn_ref(x, L0_attn_w_attn, L0_attn_b_attn, L0_attn_w_proj, L0_attn_b_proj), axis=-1)
    x = _layernorm(x + _L0_xattn_ref(x, ctx_768, L0_xattn_Wq, L0_xattn_bq, L0_xattn_Wk, L0_xattn_bk, L0_xattn_Wv, L0_xattn_bv, L0_xattn_Wo, L0_xattn_bo), axis=-1)
    x = _layernorm(x + _L0_ffn_ref(x, L0_ffn_norm_gamma, L0_ffn_slot_norm_gamma, L0_ffn_slot_embeds, L0_ffn_w1, L0_ffn_b1, L0_ffn_w2, L0_ffn_b2), axis=-1)
    x = _layernorm(x + _L1_attn_ref(x, L1_attn_w_qkv, L1_attn_w_o), axis=-1)
    x = _layernorm(x + _L1_xattn_ref(x, ctx_768, L1_xattn_wq, L1_xattn_bq, L1_xattn_wk, L1_xattn_bk, L1_xattn_wv, L1_xattn_bv, L1_xattn_wo, L1_xattn_bo), axis=-1)
    x = _layernorm(x + _L1_ffn_ref(x, L1_ffn_ln1_g, L1_ffn_ln1_b, L1_ffn_ln2_g, L1_ffn_ln2_b, L1_ffn_Wq, L1_ffn_bq, L1_ffn_Wk, L1_ffn_bk, L1_ffn_Wv, L1_ffn_bv, L1_ffn_Wp, L1_ffn_bp, L1_ffn_gate_W, L1_ffn_gate_b, L1_ffn_exp_W1, L1_ffn_exp_b1, L1_ffn_exp_W2, L1_ffn_exp_b2), axis=-1)
    return x

_drawn_inputs = setup_inputs


def setup_inputs(seed=0):
    import zlib

    import numpy as np

    out = dict(_drawn_inputs(seed))
    spreads = {'L0_attn_b_attn': (0.0, 0.1),
     'L0_attn_b_proj': (0.0, 0.1),
     'L0_ffn_norm_gamma': (1.0, 0.2),
     'L0_ffn_slot_norm_gamma': (1.0, 0.2),
     'L0_ffn_b1': (0.0, 0.1),
     'L0_ffn_b2': (0.0, 0.1),
     'L1_ffn_ln1_g': (1.0, 0.6),
     'L1_ffn_ln1_b': (0.0, 0.8),
     'L1_ffn_ln2_g': (1.0, 0.6),
     'L1_ffn_ln2_b': (0.0, 0.45),
     'L1_ffn_bq': (0.0, 0.8),
     'L1_ffn_bk': (0.0, 2.0),
     'L1_ffn_bv': (0.0, 0.452),
     'L1_ffn_bp': (0.0, 0.1),
     'L1_ffn_gate_b': (0.0, 0.31),
     'L1_ffn_exp_b1': (0.0, 0.622),
     'L1_ffn_exp_b2': (0.0, 0.1)}
    factors = {'L0_attn_w_attn': 3.659,
     'L0_xattn_bq': 22.764,
     'L0_xattn_bk': 64.0,
     'L0_xattn_bv': 5.137,
     'L0_xattn_bo': 4.761,
     'L1_xattn_bq': 24.023,
     'L1_xattn_bk': 64.0,
     'L1_xattn_bv': 6.084,
     'L1_xattn_bo': 5.805,
     'L1_ffn_Wq': 8.0,
     'L1_ffn_Wk': 8.0}
    for name, (base, spread) in spreads.items():
        noise = np.random.default_rng([zlib.crc32(name.encode()), seed]).standard_normal(out[name].shape)
        drawn = base * np.exp(spread * noise) if base else spread * noise
        out[name] = jnp.asarray(drawn.astype(out[name].dtype))
    for name, factor in factors.items():
        out[name] = (out[name] * factor).astype(out[name].dtype)
    return out
```

```python
from contextlib import ExitStack, contextmanager

import concourse.bass as bass
from concourse import mybir
import numpy as np

F32 = mybir.dt.float32
F32R = mybir.dt.float32r
BF16 = mybir.dt.bfloat16
U32 = mybir.dt.uint32
ALU = mybir.AluOpType
ACT = mybir.ActivationFunctionType
AX_X = mybir.AxisListType.X

P = 128
BATCH, SEQ, D = 4, 512, 256
T = BATCH * SEQ
NT = T // P
QT = SEQ // P
DK = D // P
CTX_SEQ, CTX_D = 1024, 192
CP = CTX_D // 2
CT = BATCH * CTX_SEQ
HEADS, HD = 16, 16
GH = 4
GROUPS = HEADS // GH
GD = GH * HD
NG = BATCH * GROUPS
EXPERTS, SLOTS, HID = 8, 128, 1024
HM = HID // P
BANK = 512
NEG_BIG = -1.0e30
LN_EPS = 1e-5
SHIFT_ROW = 96
SHIFT_END = SHIFT_ROW + 3
STACK = P


def wait_for(eng, sem, count):
    if isinstance(count, int) and count <= 0:
        return
    eng.wait_ge(sem, count)


class Core:

    def __init__(self, nc, ctx, args, out):
        self.nc, self.ctx, self.args, self.out = nc, ctx, args, out
        self.slot_stored = [ctx.enter_context(nc.semaphore(f"slot_stored{i}")) for i in range(8)]
        self.slot_count = [0] * 8
        self.psum = ctx.enter_context(nc.psum_tensor("psum", [P, 8, BANK], F32))

    def sem(self, name):
        sem = self.stage_ctx.enter_context(self.nc.semaphore(name))
        self.stage_sems.append(sem)
        return sem

    @contextmanager
    def stage(self):
        self.stage_sems = []
        with ExitStack() as self.stage_ctx:
            yield
            with self.nc.Block() as block:
                @block.gpsimd
                def _(pool):
                    for sem in self.stage_sems:
                        pool.sem_clear(sem)

    def keep(self, name, shape, dt=F32):
        return self.ctx.enter_context(self.nc.sbuf_tensor(name, shape, dt))

    def dram(self, name, shape, dt=F32):
        return self.nc.dram_tensor(name, shape, dt, kind="Internal").ap()


def staged(build_stage):
    def run(c, *args, **named):
        with c.stage():
            build_stage(c, *args, **named)
    return run


@staged
def stage_load(c):
    nc = c.nc
    c.x_tok = c.keep("x_tok", [P, NT, D])
    c.xT = c.keep("xT", [P, DK, T])
    c.ident = c.keep("ident", [P, P])
    c.ident_bf = c.keep("ident_bf", [P, P], BF16)
    c.mask_qk = c.keep("mask_qk", [P, P], BF16)
    c.mask_kq = c.keep("mask_kq", [P, P], BF16)
    c.eps = c.keep("eps", [P, 1])
    loaded, filled, made = c.sem("x_loaded"), c.sem("const_filled"), c.sem("const_made")
    with nc.Block() as block:
        @block.sync
        def _(sp):
            sp.dma_start(c.x_tok[:, :, :], c.args["x"].rearrange("b (q p) d -> p (b q) d", p=P)).then_inc(loaded, 16)
            sp.wait_ge(loaded, 16)

        @block.gpsimd
        def _(pool):
            for t in (c.ident, c.ident_bf, c.mask_qk, c.mask_kq):
                pool.memset(t[:, :], 0.0).then_inc(filled, 1)
            pool.memset(c.eps[:, :], LN_EPS).then_inc(made, 1)
            pool.wait_ge(filled, 4)
            for t in (c.ident, c.ident_bf):
                pool.affine_select(out=t[:, :], in_=t[:, :], compare_op=ALU.not_equal, fill=1.0, base=0,
                                   pattern=[[-1, P]], channel_multiplier=1).then_inc(made, 1)
            pool.affine_select(out=c.mask_qk[:, :], in_=c.mask_qk[:, :], compare_op=ALU.is_ge, fill=NEG_BIG,
                               base=0, pattern=[[-1, P]], channel_multiplier=1).then_inc(made, 1)
            pool.affine_select(out=c.mask_kq[:, :], in_=c.mask_kq[:, :], compare_op=ALU.is_ge, fill=NEG_BIG,
                               base=0, pattern=[[1, P]], channel_multiplier=-1).then_inc(made, 1)
            pool.wait_ge(made, 5)


@staged
def stage_fetch(c, name, pairs):
    loaded = c.sem(name)
    with c.nc.Block() as block:
        @block.sync
        def _(sp):
            for dst, src in pairs:
                sp.dma_start(dst, src).then_inc(loaded, 16)
            sp.wait_ge(loaded, 16 * len(pairs))


@staged
def stage_norm(c, name, src, tiles, layernorm=False, affine=None, rms=None, keep_tok=None, dstT=None, out=None):
    nc = c.nc
    with ExitStack() as ctx:
        def sb(n, shape, dt=F32):
            return ctx.enter_context(nc.sbuf_tensor(f"{name}_{n}", shape, dt))

        stats = sb("stats", [P, tiles, 6])
        mean_var = sb("mean_var", [P, 2, tiles, 2])
        root = sb("root", [P, 2, tiles])
        rstd = sb("rstd", [P, 2, tiles])
        squares = sb("squares", [P, 2, D])
        gain = sb("gain", [P, D])
        bias = sb("bias", [P, D])
        if keep_tok is None and (affine or rms):
            keep_tok = sb("rows", [P, tiles, D])
        coef_in, dve, rooted = c.sem(f"{name}_coef_in"), c.sem(f"{name}_dve"), c.sem(f"{name}_rooted")
        rows_ready, turned, evacuated = c.sem(f"{name}_rows_ready"), c.sem(f"{name}_turned"), c.sem(f"{name}_evacuated")
        stored = c.sem(f"{name}_stored")
        passes = int(layernorm) + int(affine is not None)
        rows = keep_tok if (affine or rms) else src
        coefs = list(affine or ()) + ([rms] if rms else [])

        with nc.Block() as block:
            @block.sync
            def _(sp):
                for tile, ap in zip((gain, bias), coefs):
                    sp.dma_start(tile[:, :], ap.partition_broadcast(P)).then_inc(coef_in, 16)
                if coefs:
                    sp.wait_ge(coef_in, 16 * len(coefs))
                if out is not None:
                    for b in range(tiles // QT):
                        sp.wait_ge(rows_ready, QT * (b + 1))
                        sp.dma_start(out[b].rearrange("(q p) d -> p q d", p=P),
                                     rows[:, b * QT:(b + 1) * QT, :]).then_inc(stored, 16)
                    sp.wait_ge(stored, 16 * (tiles // QT))

            @block.vector
            def _(v):
                done = 0

                def step(ins, wait=True):
                    nonlocal done
                    ins.then_inc(dve, 1)
                    done += 1
                    if wait:
                        v.wait_ge(dve, done)

                def statistics(n, which):
                    for t in range(tiles):
                        step(v.bn_stats(stats[:, t, :], which[:, t, :]), wait=t == tiles - 1)
                    for t in range(tiles):
                        step(v.bn_aggr(mean_var[:, n, t, :], stats[:, t, :]), wait=t == tiles - 1)
                    v.wait_ge(rooted, n + 1)
                    step(v.reciprocal(rstd[:, n, :], root[:, n, :]))

                n = 0
                if layernorm:
                    statistics(n, src)
                    for t in range(tiles):
                        ins = v.tensor_scalar(src[:, t, :], src[:, t, :], mean_var[:, n, t, 0:1], rstd[:, n, t:t + 1],
                                              ALU.subtract, ALU.mult)
                        if affine or rms:
                            step(ins, wait=t == tiles - 1)
                        else:
                            ins.then_inc(rows_ready, 1)
                    n += 1
                if affine:
                    statistics(n, src)
                    v.wait_ge(coef_in, 32)
                    for t in range(tiles):
                        step(v.tensor_scalar(rows[:, t, :], src[:, t, :], mean_var[:, n, t, 0:1], rstd[:, n, t:t + 1],
                                             ALU.subtract, ALU.mult), wait=t == tiles - 1)
                    for t in range(tiles):
                        step(v.tensor_tensor(rows[:, t, :], rows[:, t, :], gain[:, :], ALU.mult), wait=t == tiles - 1)
                    for t in range(tiles):
                        v.tensor_tensor(rows[:, t, :], rows[:, t, :], bias[:, :], ALU.add).then_inc(rows_ready, 1)
                if rms:
                    v.wait_ge(rooted, n + 1)
                    step(v.tensor_scalar(root[:, n, :], root[:, n, :], 1e-12, None, ALU.max))
                    step(v.reciprocal(rstd[:, n, :], root[:, n, :]))
                    step(v.tensor_scalar(rstd[:, n, :], rstd[:, n, :], float(D) ** 0.5, None, ALU.mult))
                    v.wait_ge(coef_in, 16)
                    for t in range(tiles):
                        v.scalar_tensor_tensor(rows[:, t, :], src[:, t, :], rstd[:, n, t:t + 1], gain[:, :],
                                               ALU.mult, ALU.mult).then_inc(rows_ready, 1)

            if dstT is not None:
                @block.tensor
                def _(pe):
                    if not (layernorm or affine or rms):
                        pass
                    else:
                        pe.wait_ge(rows_ready, tiles)
                    for t in range(0, tiles, QT):
                        for k in range(DK):
                            u = t // QT * DK + k
                            wait_for(pe, evacuated, u - 7)
                            for q in range(QT):
                                ins = pe.transpose(c.psum[:, u % 8, q * P:(q + 1) * P],
                                                   rows[:, t + q, k * P:(k + 1) * P], c.ident[:, :])
                            ins.then_inc(turned, 1)

            @block.scalar
            def _(act):
                squared = 0
                n = 0
                for _ in range(passes):
                    act.wait_ge(dve, 2 * tiles + n * (3 * tiles + 1))
                    act.activation(root[:, n, :], mean_var[:, n, :, 1], ACT.Sqrt, bias=c.eps[:, :]).then_inc(rooted, 1)
                    n += 1
                if rms:
                    if layernorm:
                        act.wait_ge(dve, 3 * tiles + 1)
                    for t in range(tiles):
                        if t >= 2:
                            act.wait_ge(evacuated, t - 1)
                        act.activation(squares[:, t % 2, :], src[:, t, :], ACT.Square,
                                       accum_out=root[:, n, t:t + 1]).then_inc(evacuated, 1)
                    act.wait_ge(evacuated, tiles)
                    act.activation(rstd[:, n, :], root[:, n, :], ACT.Sqrt).then_inc(evacuated, 1)
                    act.wait_ge(evacuated, tiles + 1)
                    act.activation(root[:, n, :], rstd[:, n, :], ACT.Copy).then_inc(rooted, 1)
                    squared = tiles + 1
                if dstT is not None:
                    for u in range(tiles // QT * DK):
                        act.wait_ge(turned, u + 1)
                        act.activation(dstT[:, u % DK, u // DK * SEQ:u // DK * SEQ + SEQ], c.psum[:, u % 8, :],
                                       ACT.Copy).then_inc(evacuated, 1)
                    act.wait_ge(evacuated, squared + tiles // QT * DK)


@staged
def stage_project(c, name, src, rows, tokens, split=(), values=None):
    nc = c.nc
    per = tokens // BATCH
    with ExitStack() as ctx:
        def sb(n, shape, dt=F32):
            return ctx.enter_context(nc.sbuf_tensor(f"{name}_{n}", shape, dt))

        weights = [sb(f"w{i}", [rows, 2, D]) for i in range(len(split))]
        biases = [sb(f"b{i}", [P, DK]) for i in range(len(split))]
        staged = sb("staged", [P, 8, 2, BANK])
        w_in, bank_full = c.sem(f"{name}_w_in"), c.sem(f"{name}_bank_full")
        head_done, bank_read = c.sem(f"{name}_head_done"), c.sem(f"{name}_bank_read")
        zeroed = c.sem(f"{name}_zeroed")
        stored, base = c.slot_stored, list(c.slot_count)
        if values:
            wv = sb("wv", [rows, 2, D])
        loads = len(split) + sum(x[1] is not None for x in split) + (values is not None)
        jobs = []
        for ch in range(tokens // BANK):
            jobs += [("split", i, m, ch) for i in range(len(split)) for m in range(DK)]
            if values:
                jobs += [("value", h, 0, ch) for h in range(2)]

        with nc.Block() as block:
            @block.sync
            def _(sp):
                for i, (w, b, _) in enumerate(split):
                    sp.dma_start(weights[i][:, :, :], w.rearrange("(k p) n -> p k n", p=rows)).then_inc(w_in, 16)
                    if b is not None:
                        sp.dma_start(biases[i][:, :], b.rearrange("(k p) -> p k", p=P),
                                     allow_slow_non_contiguous=True).then_inc(w_in, 16)
                if values:
                    sp.dma_start(wv[:, :, :], values[0].rearrange("(k p) n -> p k n", p=rows)).then_inc(w_in, 16)
                for u, (kind, i, m, ch) in enumerate(jobs):
                    sp.wait_ge(bank_read, u + 1)
                    b, at = ch * BANK // per, ch * BANK % per
                    if kind == "split":
                        row = b * D + m * P
                        sp.dma_start(split[i][2][:, row:row + P, at:at + BANK].rearrange("a p t -> p a t"),
                                     staged[:, u % 8, :, :]).then_inc(stored[u % 8], 16)
                    else:
                        kt = at // P + 2 * i
                        sp.dma_start(values[1][b * GROUPS:(b + 1) * GROUPS, :, kt:kt + 2, :].rearrange("g p t d -> p g (t d)"),
                                     staged[:, u % 8, 0, :].rearrange("p (g m) -> p g m", g=GROUPS)
                                     ).then_inc(stored[u % 8], 16)
                for s in range(8):
                    c.slot_count[s] += 16 * len(range(s, len(jobs), 8))
                    wait_for(sp, stored[s], c.slot_count[s])

            @block.gpsimd
            def _(pool):
                for i, (_, b, _) in enumerate(split):
                    if b is None:
                        pool.memset(biases[i][:, :], 0.0).then_inc(zeroed, 1)

            zeros = sum(x[1] is None for x in split)

            @block.tensor
            def _(pe):
                pe.wait_ge(w_in, 16 * loads)
                for u, (kind, i, m, ch) in enumerate(jobs):
                    wait_for(pe, bank_read, u - 7)
                    for half in range(1 if kind == "split" else 2):
                        for k in range(2):
                            if kind == "split":
                                ins = pe.matmul(c.psum[:, u % 8, :], weights[i][:, k, m * P:(m + 1) * P],
                                                src[:, k, ch * BANK:(ch + 1) * BANK], start=k == 0, stop=k == 1)
                            else:
                                t = ch * BANK + (2 * i + half) * P
                                ins = pe.matmul(c.psum[:, u % 8, half * D:(half + 1) * D], src[:, k, t:t + P],
                                                wv[:, k, :], start=k == 0, stop=k == 1)
                    ins.then_inc(bank_full, 1)

            @block.scalar
            def _(act):
                act.wait_ge(w_in, 16 * loads)
                wait_for(act, zeroed, zeros)
                for u, (kind, i, m, ch) in enumerate(jobs):
                    if kind == "split":
                        act.wait_ge(bank_full, u + 1)
                        if u >= 8:
                            act.wait_ge(stored[u % 8], base[u % 8] + 16 * (u // 8))
                        act.activation(staged[:, u % 8, 0, :].bitcast(F32R), c.psum[:, u % 8, :], ACT.Identity,
                                       bias=biases[i][:, m:m + 1]).then_inc(head_done, 1)

            @block.vector
            def _(v):
                heads = 0
                v.wait_ge(w_in, 16 * loads)
                wait_for(v, zeroed, zeros)
                for u, (kind, i, m, ch) in enumerate(jobs):
                    if kind == "split":
                        heads += 1
                        v.wait_ge(head_done, heads)
                        v.scalar_tensor_tensor(staged[:, u % 8, 1, :].bitcast(F32R), c.psum[:, u % 8, :],
                                               biases[i][:, m:m + 1], staged[:, u % 8, 0, :],
                                               ALU.add, ALU.subtract).then_inc(bank_read, 1)
                    else:
                        v.wait_ge(bank_full, u + 1)
                        if u >= 8:
                            v.wait_ge(stored[u % 8], base[u % 8] + 16 * (u // 8))
                        v.tensor_copy(staged[:, u % 8, 0, :].rearrange("p (g t d) -> p t g d", g=GROUPS, t=2),
                                      c.psum[:, u % 8, :].rearrange("p (t g d) -> p t g d", t=2, g=GROUPS)
                                      ).then_inc(bank_read, 1)


def attention_plan(KT, units, causal):
    def queries(t):
        return SEQ - t * P if causal else SEQ

    slots = [(t, h) for t in range(KT) for h in range(2)]
    load = [2 * queries(t) + (queries(t) if h else 0) for t, h in slots]
    cost = [unit[3] + P for unit in units]
    plan, u = [], 0
    for s, (t, h) in enumerate(slots):
        while u < len(units) and sum(cost[:u]) * sum(load) <= sum(load[:s]) * sum(cost):
            plan.append(("unit", 2, u))
            u += 1
        if KT - 1 <= s < KT - 1 + GH:
            plan.append(("shift", 1, s - KT + 1))
        plan.append(("scores", 0, s))
        if h == 1:
            plan += [("values", 0, t - 1)] if t else [("values", -1, KT - 1), ("drain", -1, 0)]
        if s == 4:
            plan.append(("turn", -1, 0))
    return plan + [("unit", 2, v) for v in range(u, len(units))]


@staged
def stage_attention(c, name, q_dram, k_dram, v_dram, v_bias, o_tok, keys, causal):
    nc = c.nc
    KT = keys // P
    units = [(j, qt, k0, (qt + 1) * P if causal else BANK)
             for j in range(GH) for qt in range(QT) for k0 in range(0, keys, BANK)]
    U = len(units)
    parts = U // (GH * QT)
    scale = 1.0 / float(HD) ** 0.5
    NB = 4
    SHIFT_STEPS = 6
    PV_BANK, RING = 6, (4, 5, 7)
    plan = attention_plan(KT, units, causal)
    ring_uses = [x for x in plan if x[0] in ("unit", "shift", "turn")]

    def exists(n, event):
        return 0 <= n + event[1] < NG

    def bank_before(n, event):
        at = ring_uses.index(event)
        for body in (n, n - 1, n - 2):
            same = [x for i, x in enumerate(ring_uses) if i % 3 == at % 3 and (body < n or i < at)]
            same = [x for x in same if exists(body, x)]
            if same:
                what, ahead, index = same[-1]
                return what, ahead + body - n, index
        return None

    with ExitStack() as ctx:
        def sb(n, shape, dt=F32):
            return ctx.enter_context(nc.sbuf_tensor(f"{name}_{n}", shape, dt))

        qs = [sb(f"q{i}", [STACK, GH, SEQ], F32R) for i in range(NB)]
        ks = [sb(f"k{i}", [STACK, GH, keys], F32R) for i in range(NB)]
        v_raw = [sb(f"v_raw{i}", [P, KT, GD]) for i in range(2)]
        v_aug = [sb(f"v_aug{i}", [P, KT, GH, 32]) for i in range(2)]
        bias = sb("v_bias", [P, D])
        probs = [sb(f"p{i}", [P, GH, SEQ]) for i in range(2)]
        max_parts = sb("max_parts", [P, U])
        row_max = sb("row_max", [P, GH * QT])
        rest = sb("rest", [P, 2, GH * QT])
        shift = sb("shift", [P, GH * QT, 3], BF16)
        o_sum = sb("o_sum", [P, SEQ])
        recip = sb("recip", [P, QT * GH])
        s_set = c.sem(f"{name}_set")
        s_bias = c.sem(f"{name}_v_bias")
        s_qk = [c.sem(f"{name}_qk_in{i}") for i in range(NB)]
        s_vin = [c.sem(f"{name}_v_in{i}") for i in range(2)]
        s_vaug = c.sem(f"{name}_v_aug")
        s_unit_full, s_unit_read = c.sem(f"{name}_unit_full"), c.sem(f"{name}_unit_read")
        s_shift = c.sem(f"{name}_shift")
        s_row_full, s_row = c.sem(f"{name}_row_full"), c.sem(f"{name}_row")
        s_score, s_exp = c.sem(f"{name}_score"), c.sem(f"{name}_exp")
        s_pv = c.sem(f"{name}_pv")
        s_osum, s_turn, s_norm = c.sem(f"{name}_o_sum"), c.sem(f"{name}_turn"), c.sem(f"{name}_norm")

        def first_query(t):
            return t * P if causal else 0

        def ring_bank(event):
            return RING[ring_uses.index(event) % 3]

        with nc.Block() as block:
            def for_groups(eng, body):
                for r in range(GROUPS):
                    body(r, 0, r, r)
                with eng.Fori(1, BATCH - 1) as b:
                    for r in range(GROUPS):
                        body(b * GROUPS + r, b, r, GROUPS + r)
                for r in range(GROUPS):
                    body((BATCH - 1) * GROUPS + r, BATCH - 1, r, (BATCH - 1) * GROUPS + r)

            def run_plan(eng, handlers):
                def body(n, b, r, like):
                    for event in plan:
                        what, ahead, index = event
                        if what in handlers and exists(like, event):
                            g = (r + ahead) % GROUPS
                            batch = b + (r + ahead - g) // GROUPS
                            handlers[what](n + ahead, batch, g, index, n, like, event)

                body(-2, -1, 2, -2)
                body(-1, -1, 3, -1)
                for_groups(eng, body)
                body(NG, BATCH, 0, NG)

            @block.sync
            def _(sp):
                def body(n, b, r, like):
                    wait_for(sp, s_score, 2 * KT * (n - NB + 1))
                    for blk, (qp, kp) in enumerate(((0, 0), (0, 1), (1, 0), (1, 1))):
                        at = slice(HD * blk, HD * (blk + 1))
                        sp.dma_start(qs[r][at, :, :].bitcast(F32),
                                     q_dram[qp, bass.ds(n * GD, GD), :].rearrange("(j d) t -> d j t", d=HD)
                                     ).then_inc(s_qk[r], 16)
                        sp.dma_start(ks[r][at, :, :].bitcast(F32),
                                     k_dram[kp, bass.ds(n * GD, GD), :].rearrange("(j d) t -> d j t", d=HD)
                                     ).then_inc(s_qk[r], 16)
                    wait_for(sp, s_vaug, n - 1)
                    sp.dma_start(v_raw[r % 2][:, :, :], v_dram[bass.ds(n, 1), :, :, :].rearrange("o p t d -> p (o t) d")
                                 ).then_inc(s_vin[r % 2], 16)

                if v_bias is not None:
                    sp.dma_start(bias[:, :], v_bias.partition_broadcast(P)).then_inc(s_bias, 16)
                for_groups(sp, body)

            @block.gpsimd
            def _(pool):
                steps = 0
                if v_bias is None:
                    pool.memset(bias[:, :], 0.0).then_inc(s_bias, 1)
                pool.wait_ge(s_bias, 1 if v_bias is None else 16)
                for i in range(NB):
                    fills = [(qs[i][64:STACK, :, :].bitcast(F32), 0.0), (ks[i][64:STACK, :, :].bitcast(F32), 1.0)]
                    fills += [(t[:, :, :, :], 1.0) for t in v_aug] if i == 1 else []
                    for ap, value in fills:
                        pool.memset(ap, value).then_inc(s_set, 1)
                        steps += 1
                        pool.wait_ge(s_set, steps)

                def body(n, b, r, like):
                    pool.wait_ge(s_vin[r % 2], 16 * (b * (GROUPS // 2) + r // 2 + 1))
                    wait_for(pool, s_pv, KT * (n - 1))
                    own = bias[:, r * GD:(r + 1) * GD].rearrange("p (j d) -> p j d", d=HD).unsqueeze(1)
                    pool.tensor_tensor(v_aug[r % 2][:, :, :, 0:HD],
                                       v_raw[r % 2][:, :, :].rearrange("p t (j d) -> p t j d", d=HD),
                                       own.to_broadcast([P, KT, GH, HD]), ALU.add).then_inc(s_vaug, 1)

                for_groups(pool, body)

            @block.tensor
            def _(pe):
                def wait_bank(n, like, event):
                    found = bank_before(like, event)
                    if found is None:
                        return
                    what, ahead, index = found
                    if what == "unit":
                        pe.wait_ge(s_unit_read, (n + ahead) * U + index + 1)
                    elif what == "turn":
                        pe.wait_ge(s_norm, 2 * (n + ahead + 1))
                    else:
                        pe.wait_ge(s_row, GH * (n + ahead) + index + 1)

                def unit(g, b, r, u, n, like, event):
                    if u == 0:
                        if like + 2 < NB:
                            pe.wait_ge(s_set, (2, 4, 8, 10)[like + 2])
                        pe.wait_ge(s_qk[r], 128 * (b + 1))
                    wait_bank(n, like, event)
                    j, qt, k0, width = units[u]
                    bank = ring_bank(event)
                    ins = pe.matmul(c.psum[:, bank, 0:width], qs[r][0:SHIFT_ROW, j, qt * P:(qt + 1) * P],
                                    ks[r][0:SHIFT_ROW, j, k0:k0 + width], start=True, stop=not causal)
                    if causal:
                        ins = pe.matmul(c.psum[:, bank, qt * P:(qt + 1) * P], c.ident_bf[:, :],
                                        c.mask_qk[:, :], start=False, stop=True)
                    ins.then_inc(s_unit_full, 1)

                def shift_row(g, b, r, j, n, like, event):
                    if j == 0:
                        pe.wait_ge(s_shift, SHIFT_STEPS * (g + 1))
                    wait_bank(n, like, event)
                    for qt in range(QT):
                        ins = pe.matmul(c.psum[SHIFT_ROW:SHIFT_END, ring_bank(event), qt * P:(qt + 1) * P],
                                        shift[:, j * QT + qt, :], c.ident_bf[:, :], start=True, stop=True)
                    ins.then_inc(s_row_full, 1)

                def scores(g, b, r, s, n, like, event):
                    t, h = s // 2, s % 2
                    if t == 0:
                        pe.wait_ge(s_row, GH * g + 2 * h + 2)
                    wait_for(pe, s_exp, 2 * KT * g + s - 1)
                    q0 = first_query(t)
                    for j in range(2 * h, 2 * h + 2):
                        bank = 2 * (s % 2) + j % 2
                        ins = pe.matmul(c.psum[:, bank, q0:SEQ], ks[r][0:STACK, j, t * P:(t + 1) * P],
                                        qs[r][0:STACK, j, q0:SEQ], start=True, stop=not causal)
                        if causal:
                            ins = pe.matmul(c.psum[:, bank, q0:q0 + P], c.ident_bf[:, :], c.mask_kq[:, :],
                                            start=False, stop=True)
                    ins.then_inc(s_score, 1)

                def values(g, b, r, t, n, like, event):
                    pe.wait_ge(s_exp, 2 * KT * g + 2 * t + 2)
                    if t == 0:
                        pe.wait_ge(s_vaug, g + 1)
                        wait_for(pe, s_osum, g)
                    q0 = first_query(t)
                    for j in range(GH):
                        ins = pe.matmul(c.psum[32 * j:32 * j + 32, PV_BANK, q0:SEQ], v_aug[r % 2][:, t, j, :],
                                        probs[t % 2][:, j, q0:SEQ], start=t == 0, stop=t == KT - 1)
                    ins.then_inc(s_pv, 1)

                def turn(g, b, r, _, n, like, event):
                    pe.wait_ge(s_osum, g + 1)
                    wait_bank(n, like, event)
                    for qt in range(QT):
                        ins = pe.transpose(c.psum[:, ring_bank(event), qt * P:(qt + 1) * P],
                                           o_sum[:, qt * P:(qt + 1) * P], c.ident[:, :])
                    ins.then_inc(s_turn, 1)

                run_plan(pe, {"unit": unit, "shift": shift_row, "scores": scores, "values": values, "turn": turn})

            @block.scalar
            def _(act):
                def shift_row(g, b, r, j, n, like, event):
                    act.wait_ge(s_row_full, GH * g + j + 1)
                    act.activation(qs[r][SHIFT_ROW:SHIFT_END, j, :], c.psum[SHIFT_ROW:SHIFT_END, ring_bank(event), :],
                                   ACT.Copy).then_inc(s_row, 1)

                def exps(g, b, r, s, n, like, event):
                    t, h = s // 2, s % 2
                    q0 = first_query(t)
                    act.wait_ge(s_score, 2 * KT * g + s + 1)
                    wait_for(act, s_pv, KT * g + t - 1)
                    act.activation(probs[t % 2][:, 2 * h:2 * h + 2, q0:SEQ],
                                   c.psum[:, 2 * (s % 2):2 * (s % 2) + 2, q0:SEQ], ACT.Exp,
                                   scale=scale).then_inc(s_exp, 1)

                def drain_outputs(g, b, r, _, n, like, event):
                    act.wait_ge(s_pv, KT * (g + 1))
                    wait_for(act, s_turn, g)
                    act.activation(o_sum[:, :], c.psum[:, PV_BANK, :], ACT.Copy).then_inc(s_osum, 1)

                run_plan(act, {"shift": shift_row, "scores": exps, "drain": drain_outputs})

            @block.vector
            def _(v):
                def unit(g, b, r, u, n, like, event):
                    v.wait_ge(s_unit_full, g * U + u + 1)
                    if u == 0:
                        wait_for(v, s_shift, SHIFT_STEPS * g)
                    v.reduce_max(max_parts[:, u:u + 1], c.psum[:, ring_bank(event), 0:units[u][3]],
                                 axis=AX_X).then_inc(s_unit_read, 1)
                    if u == U - 1:
                        shift_parts(g)

                def shift_parts(g):
                    at = SHIFT_STEPS * g
                    v.wait_ge(s_unit_read, U * (g + 1))
                    wait_for(v, s_row_full, GH * g)
                    v.tensor_reduce(row_max[:, :], max_parts[:, :].rearrange("p (u k) -> p u k", k=parts),
                                    axis=AX_X, op=ALU.max).then_inc(s_shift, 1)
                    v.wait_ge(s_shift, at + 1)
                    v.tensor_scalar(shift[:, :, 0], row_max[:, :], -1.0, None, ALU.mult).then_inc(s_shift, 1)
                    v.wait_ge(s_shift, at + 2)
                    v.scalar_tensor_tensor(rest[:, 0, :], row_max[:, :], -1.0, shift[:, :, 0], ALU.mult,
                                           ALU.subtract).then_inc(s_shift, 1)
                    v.wait_ge(s_shift, at + 3)
                    v.tensor_copy(shift[:, :, 1], rest[:, 0, :]).then_inc(s_shift, 1)
                    v.wait_ge(s_shift, at + 4)
                    v.tensor_tensor(rest[:, 1, :], rest[:, 0, :], shift[:, :, 1], ALU.subtract).then_inc(s_shift, 1)
                    v.wait_ge(s_shift, at + 5)
                    v.tensor_copy(shift[:, :, 2], rest[:, 1, :]).then_inc(s_shift, 1)

                def normalise(g, b, r, _, n, like, event):
                    v.wait_ge(s_turn, g + 1)
                    turned = c.psum[:, ring_bank(event), :].rearrange("p (a c) -> p a c", c=32)
                    wait_for(v, s_norm, 2 * g)
                    v.reciprocal(recip[:, :].unsqueeze(2), turned[:, :, HD:HD + 1]).then_inc(s_norm, 1)
                    v.wait_ge(s_norm, 2 * g + 1)
                    dst = o_tok[:, bass.ds(b * QT, QT), r * GD:(r + 1) * GD].rearrange("p q (j d) -> p q j d", d=HD)
                    v.tensor_tensor(dst, turned[:, :, 0:HD].rearrange("p (q j) d -> p q j d", j=GH),
                                    recip[:, :].rearrange("p (q j) -> p q j", j=GH).unsqueeze(3)
                                    .to_broadcast([P, QT, GH, HD]), ALU.mult).then_inc(s_norm, 1)

                run_plan(v, {"unit": unit, "turn": normalise})


@staged
def stage_output(c, name, o_tok, w, b):
    nc = c.nc
    with ExitStack() as ctx:
        def sb(n, shape, dt=F32):
            return ctx.enter_context(nc.sbuf_tensor(f"{name}_{n}", shape, dt))

        wo = sb("wo", [P, DK, D])
        bo = sb("bo", [P, D])
        oT = sb("oT", [P, 4, DK, P])
        w_in, turned, evacuated = c.sem(f"{name}_w_in"), c.sem(f"{name}_turned"), c.sem(f"{name}_evacuated")
        projected, added, biased = c.sem(f"{name}_projected"), c.sem(f"{name}_added"), c.sem(f"{name}_biased")
        loads = 1 + (b is not None)

        with nc.Block() as block:
            @block.sync
            def _(sp):
                sp.dma_start(wo[:, :, :], w.rearrange("(k p) n -> p k n", p=P)).then_inc(w_in, 16)
                if b is not None:
                    sp.dma_start(bo[:, :], b.partition_broadcast(P)).then_inc(w_in, 16)
                sp.wait_ge(w_in, 16 * loads)

            @block.tensor
            def _(pe):
                def turn(t):
                    wait_for(pe, evacuated, t - 3)
                    for k in range(DK):
                        ins = pe.transpose(c.psum[:, t % 4, k * P:(k + 1) * P],
                                           o_tok[:, t, k * P:(k + 1) * P], c.ident[:, :])
                    ins.then_inc(turned, 1)

                turn(0)
                turn(1)
                pe.wait_ge(w_in, 16 * loads)
                for t in range(NT):
                    if t + 2 < NT:
                        turn(t + 2)
                    pe.wait_ge(evacuated, t + 1)
                    wait_for(pe, added, t - 3)
                    for k in range(DK):
                        ins = pe.matmul(c.psum[:, 4 + t % 4, 0:D], oT[:, t % 4, k, :], wo[:, k, :],
                                        start=k == 0, stop=k == DK - 1)
                    ins.then_inc(projected, 1)

            @block.scalar
            def _(act):
                for t in range(NT):
                    act.wait_ge(turned, t + 1)
                    wait_for(act, projected, t - 3)
                    act.activation(oT[:, t % 4, :, :], c.psum[:, t % 4, 0:DK * P].rearrange("p (k n) -> p k n", k=DK),
                                   ACT.Copy).then_inc(evacuated, 1)

            @block.gpsimd
            def _(pool):
                if b is not None:
                    pool.wait_ge(w_in, 16 * loads)
                    for t in range(NT):
                        pool.tensor_tensor(c.x_tok[:, t, :], c.x_tok[:, t, :], bo[:, :], ALU.add).then_inc(biased, 1)

            @block.vector
            def _(v):
                for t in range(NT):
                    v.wait_ge(projected, t + 1)
                    if b is not None:
                        v.wait_ge(biased, t + 1)
                    v.tensor_tensor(c.x_tok[:, t, :], c.psum[:, 4 + t % 4, 0:D], c.x_tok[:, t, :],
                                    ALU.add).then_inc(added, 1)


@staged
def stage_experts(c, name, w1, b1, w2, b2, chunks, tokens_of, eo=None, token_weight=None):
    nc = c.nc
    with ExitStack() as ctx:
        def sb(n, shape, dt=F32):
            return ctx.enter_context(nc.sbuf_tensor(f"{name}_{n}", shape, dt))

        up = [sb(f"up{i}", [P, DK, HID]) for i in range(2)]
        down = [sb(f"down{i}", [P, HM, D]) for i in range(2)]
        up_bias = [sb(f"up_bias{i}", [P, HM]) for i in range(2)]
        down_bias = [sb(f"down_bias{i}", [P, D]) for i in range(2)] if eo is not None else None
        weight = [sb(f"weight{i}", [P, NT]) for i in range(2)] if eo is None else None
        hidden = sb("hidden", [P, HM, BANK])
        w_in = [c.sem(f"{name}_w_in{i}") for i in range(2)]
        s_up, s_gelu = c.sem(f"{name}_up"), c.sem(f"{name}_gelu")
        s_down, s_read, s_weight = c.sem(f"{name}_down"), c.sem(f"{name}_read"), c.sem(f"{name}_weight")
        per_load = 16 * (3 + (eo is not None))
        tiles = BANK // P
        UP_BANKS = 4

        with nc.Block() as block:
            def for_experts(eng, body):
                for r in range(2):
                    body(r, 0, r)
                with eng.Fori(1, EXPERTS // 2) as pair:
                    for r in range(2):
                        body(pair * 2 + r, pair, r)

            @block.sync
            def _(sp):
                def body(e, pair, r):
                    wait_for(sp, s_down, tiles * chunks * (e - 1))
                    one = bass.ds(e, 1)
                    sp.dma_start(up[r][:, :, :], w1[one, :, :].rearrange("o (k p) n -> p (o k) n", p=P)).then_inc(w_in[r], 16)
                    sp.dma_start(up_bias[r][:, :], b1[one, :, :].rearrange("o p m -> p (o m)")).then_inc(w_in[r], 16)
                    sp.dma_start(down[r][:, :, :], w2[one, :, :].rearrange("o (m p) n -> p (o m) n", p=P)).then_inc(w_in[r], 16)
                    if eo is not None:
                        wait_for(sp, s_read, tiles * chunks * (e - 1))
                        sp.dma_start(down_bias[r][:, :], b2[one, :].rearrange("o n -> (o n)").partition_broadcast(P)
                                     ).then_inc(w_in[r], 16)

                for_experts(sp, body)

            @block.tensor
            def _(pe):
                def body(e, pair, r):
                    pe.wait_ge(w_in[r], (pair + 1) * per_load)
                    for ch in range(chunks):
                        q = e * chunks + ch
                        for m in range(HM):
                            wait_for(pe, s_gelu, q * HM + m - UP_BANKS + 1)
                            for k in range(DK):
                                ins = pe.matmul(c.psum[:, m % UP_BANKS, :], up[r][:, k, m * P:(m + 1) * P],
                                                tokens_of(e, k, ch), start=k == 0, stop=k == DK - 1)
                            ins.then_inc(s_up, 1)
                        for t in range(tiles):
                            wait_for(pe, s_read, (q - 1) * tiles + t + 1)
                            for m in range(HM):
                                if t == 0:
                                    pe.wait_ge(s_gelu, q * HM + m + 1)
                                ins = pe.matmul(c.psum[:, 4 + t, 0:D], hidden[:, m, t * P:(t + 1) * P],
                                                down[r][:, m, :], start=m == 0, stop=m == HM - 1)
                            ins.then_inc(s_down, 1)

                for_experts(pe, body)

            @block.scalar
            def _(act):
                def body(e, pair, r):
                    act.wait_ge(w_in[r], (pair + 1) * per_load)
                    for ch in range(chunks):
                        q = e * chunks + ch
                        wait_for(act, s_down, q * tiles)
                        for m in range(HM):
                            act.wait_ge(s_up, q * HM + m + 1)
                            act.activation(hidden[:, m, :], c.psum[:, m % UP_BANKS, :], ACT.Gelu,
                                           bias=up_bias[r][:, m:m + 1]).then_inc(s_gelu, 1)

                for_experts(act, body)

            @block.vector
            def _(v):
                def body(e, pair, r):
                    if eo is not None:
                        v.wait_ge(w_in[r], (pair + 1) * per_load)
                    else:
                        wait_for(v, s_read, tiles * chunks * (e - 1))
                        v.tensor_copy(weight[r][:, :].unsqueeze(2), token_weight[:, :, bass.ds(e, 1)]).then_inc(s_weight, 1)
                        v.wait_ge(s_weight, e + 1)
                    for ch in range(chunks):
                        q = e * chunks + ch
                        for t in range(tiles):
                            v.wait_ge(s_down, q * tiles + t + 1)
                            if eo is not None:
                                v.tensor_tensor(eo[:, bass.ds(e, 1), t, :], c.psum[:, 4 + t, 0:D].unsqueeze(1),
                                                down_bias[r][:, :].unsqueeze(1), ALU.add).then_inc(s_read, 1)
                            else:
                                x = ch * tiles + t
                                wait_for(v, s_read, (q - chunks) * tiles + t + 1)
                                v.scalar_tensor_tensor(c.x_tok[:, x, :], c.psum[:, 4 + t, 0:D], weight[r][:, x:x + 1],
                                                       c.x_tok[:, x, :], ALU.mult, ALU.add).then_inc(s_read, 1)

                for_experts(v, body)


def soft_moe(c):
    nc, a = c.nc, c.args
    ES = EXPERTS * SLOTS
    with ExitStack() as ctx:
        def keep(n, shape):
            return ctx.enter_context(nc.sbuf_tensor(f"soft_{n}", shape, F32))

        slots_T = keep("slots_T", [P, EXPERTS, DK, BATCH * SLOTS])
        combine = keep("combine", [P, EXPERTS, NT, P])
        with ExitStack() as inner:
            h_tok = inner.enter_context(nc.sbuf_tensor("soft_h_tok", [P, NT, D], F32))
            slot_T = inner.enter_context(nc.sbuf_tensor("soft_slot_T", [P, DK, ES], F32))
            with nc.sbuf_tensor("soft_embeds", [P, EXPERTS, D], F32) as embeds:
                stage_fetch(c, "soft_embeds_in", [(embeds[:, :, :], a["L0_ffn_slot_embeds"].rearrange("e s d -> s e d"))])
                stage_norm(c, "slot", embeds, EXPERTS, rms=a["L0_ffn_slot_norm_gamma"], dstT=slot_T)
            stage_norm(c, "n1", c.x_tok, NT, layernorm=True, rms=a["L0_ffn_norm_gamma"], keep_tok=h_tok, dstT=c.xT)
            stage_soft_routes(c, h_tok, slot_T, slots_T, combine)
        outputs = slots_T[:, :, :, :].rearrange("p e k (h n) -> p e (k h) n", n=D)
        stage_experts(c, "soft_experts", a["L0_ffn_w1"], a["L0_ffn_b1"], a["L0_ffn_w2"], a["L0_ffn_b2"], 1,
                      lambda e, k, ch: slots_T[:, bass.ds(e, 1), k, :].rearrange("p o n -> p (o n)"), eo=outputs)
        stage_combine(c, combine, outputs)


@staged
def stage_soft_routes(c, h_tok, slot_T, slots_T, combine):
    nc = c.nc
    with ExitStack() as ctx:
        def sb(n, shape, dt=F32):
            return ctx.enter_context(nc.sbuf_tensor(f"route_{n}", shape, dt))

        def sem(n):
            return c.sem(f"route_{n}")

        jobs = []
        for b in range(BATCH):
            jobs += [("dispatch", b, e) for e in range(EXPERTS)] + [("combine", b, q) for q in range(QT)]
            jobs += [("slots", b, k) for k in range(DK)]
        soft = [i for i, job in enumerate(jobs) if job[0] != "slots"]
        place = {i: n for n, i in enumerate(soft)}
        probs = sb("probs", [P, 2, 2, BANK])
        dispatch = sb("dispatch", [P, QT, EXPERTS * SLOTS])
        low, total, inverse = sb("low", [P, len(soft)]), sb("total", [P, len(soft)]), sb("inverse", [P, len(soft)])
        s_full, s_low, s_exp, s_inverse = sem("full"), sem("low"), sem("exp"), sem("inverse")
        s_scaled, s_turned, s_out, s_slots = sem("scaled"), sem("turned"), sem("out"), sem("slots")

        def banks(i):
            return 2 if jobs[i][0] != "dispatch" else 1

        def slots_before(i):
            return sum(job[0] == "slots" for job in jobs[:i])

        with nc.Block() as block:
            @block.tensor
            def _(pe):
                def fill(i):
                    kind, b, n = jobs[i]
                    if i >= 2:
                        if i - 2 in place:
                            pe.wait_ge(s_exp, place[i - 2] + 1)
                        else:
                            pe.wait_ge(s_slots, slots_before(i - 2) + 1)
                    if kind == "slots":
                        pe.wait_ge(s_out, max(place[x] for x in soft if jobs[x][:2] == ("dispatch", b)) + 1)
                    for h in range(banks(i)):
                        bank = c.psum[:, 2 * (i % 2) + h, :]
                        if kind == "dispatch":
                            for k in range(DK):
                                ins = pe.matmul(bank, slot_T[:, k, n * SLOTS:(n + 1) * SLOTS],
                                                c.xT[:, k, b * SEQ:(b + 1) * SEQ], start=k == 0, stop=k == DK - 1)
                        elif kind == "combine":
                            t = b * SEQ + n * P
                            for k in range(DK):
                                ins = pe.matmul(bank, c.xT[:, k, t:t + P], slot_T[:, k, h * BANK:(h + 1) * BANK],
                                                start=k == 0, stop=k == DK - 1)
                        else:
                            for q in range(QT):
                                ins = pe.matmul(bank, h_tok[:, b * QT + q, n * P:(n + 1) * P],
                                                dispatch[:, q, h * BANK:(h + 1) * BANK], start=q == 0, stop=q == QT - 1)
                    ins.then_inc(s_full, 1)

                def turn(i):
                    n = place[i]
                    pe.wait_ge(s_scaled, n + 1)
                    if n >= 2:
                        pe.wait_ge(s_out, n - 1)
                    for h in range(banks(i)):
                        for q in range(BANK // P):
                            ins = pe.transpose(c.psum[:, 4 + 2 * (n % 2) + h, q * P:(q + 1) * P],
                                               probs[:, n % 2, h, q * P:(q + 1) * P], c.ident[:, :])
                    ins.then_inc(s_turned, 1)

                for i in range(len(jobs)):
                    fill(i)
                    if i >= 1 and i - 1 in place:
                        turn(i - 1)

            @block.vector
            def _(v):
                def lows(i):
                    n = place[i]
                    v.wait_ge(s_full, i + 1)
                    src = c.psum[:, 2 * (i % 2):2 * (i % 2) + banks(i), :]
                    v.tensor_reduce(low[:, n:n + 1], src, axis=mybir.AxisListType.XY, op=ALU.max,
                                    negate=True).then_inc(s_low, 1)

                def scale(i):
                    n = place[i]
                    v.wait_ge(s_exp, n + 1)
                    v.reciprocal(inverse[:, n:n + 1], total[:, n:n + 1]).then_inc(s_inverse, 1)
                    v.wait_ge(s_inverse, n + 1)
                    own = probs[:, n % 2, 0:banks(i), :]
                    v.tensor_scalar(own, own, inverse[:, n:n + 1], None, ALU.mult).then_inc(s_scaled, 1)

                for i in range(len(jobs) + 1):
                    if i < len(jobs) and i in place:
                        lows(i)
                    if i >= 1 and i - 1 in place:
                        scale(i - 1)

            @block.scalar
            def _(act):
                def exps(i):
                    n = place[i]
                    act.wait_ge(s_low, n + 1)
                    if n >= 2:
                        act.wait_ge(s_turned, n - 1)
                    act.activation(probs[:, n % 2, 0:banks(i), :], c.psum[:, 2 * (i % 2):2 * (i % 2) + banks(i), :],
                                   ACT.Exp, bias=low[:, n:n + 1], accum_out=total[:, n:n + 1]).then_inc(s_exp, 1)

                def evacuate(i):
                    kind, b, x = jobs[i]
                    n = place[i]
                    act.wait_ge(s_turned, n + 1)
                    pair = 4 + 2 * (n % 2)
                    if kind == "dispatch":
                        act.activation(dispatch[:, :, x * SLOTS:(x + 1) * SLOTS],
                                       c.psum[:, pair, :].rearrange("p (q s) -> p q s", q=QT), ACT.Copy).then_inc(s_out, 1)
                    else:
                        act.activation(combine[:, :, b * QT + x, :],
                                       c.psum[:, pair:pair + 2, :].rearrange("p h (e n) -> p (h e) n", n=P),
                                       ACT.Copy).then_inc(s_out, 1)

                def slots(i):
                    _, b, k = jobs[i]
                    act.wait_ge(s_full, i + 1)
                    pair = 2 * (i % 2)
                    act.activation(slots_T[:, :, k, b * SLOTS:(b + 1) * SLOTS],
                                   c.psum[:, pair:pair + 2, :].rearrange("p h (e n) -> p (h e) n", n=SLOTS),
                                   ACT.Copy).then_inc(s_slots, 1)

                for i in range(len(jobs)):
                    if i in place:
                        exps(i)
                    if i >= 1 and i - 1 in place:
                        evacuate(i - 1)
                    if i not in place:
                        slots(i)


@staged
def stage_combine(c, combine, outputs):
    s_full, s_read = c.sem("combine_full"), c.sem("combine_read")
    with c.nc.Block() as block:
        @block.tensor
        def _(pe):
            for t in range(NT):
                wait_for(pe, s_read, t - 7)
                for e in range(EXPERTS):
                    ins = pe.matmul(c.psum[:, t % 8, 0:D], combine[:, e, t, :], outputs[:, e, t // QT, :],
                                    start=e == 0, stop=e == EXPERTS - 1)
                ins.then_inc(s_full, 1)

        @block.vector
        def _(v):
            for t in range(NT):
                v.wait_ge(s_full, t + 1)
                v.tensor_tensor(c.x_tok[:, t, :], c.psum[:, t % 8, 0:D], c.x_tok[:, t, :], ALU.add).then_inc(s_read, 1)


def token_moe(c, block_in):
    a = c.args
    with c.nc.sbuf_tensor("gate_weight", [P, NT, EXPERTS], F32) as weight:
        stage_gate(c, weight, block_in)
        stage_experts(c, "token_experts", a["L1_ffn_exp_W1"], a["L1_ffn_exp_b1"], a["L1_ffn_exp_W2"], None, NT // QT,
                      lambda e, k, ch: c.xT[:, k, ch * BANK:(ch + 1) * BANK], token_weight=weight)


@staged
def stage_gate(c, weight, block_in):
    nc, a = c.nc, c.args
    E = EXPERTS
    with ExitStack() as ctx:
        def sb(n, shape, dt=F32):
            return ctx.enter_context(nc.sbuf_tensor(f"gate_{n}", shape, dt))

        def sem(n):
            return c.sem(f"gate_{n}")

        weight_T = sb("weight_T", [E, T])
        gate_w, gate_b, down_b = sb("w", [P, DK, E]), sb("b", [P, E]), sb("down_b", [E, D])
        logits, top = sb("logits", [P, NT, E]), sb("top", [P, NT, 8])
        at, at_f = sb("at", [P, NT, 8], U32), sb("at_f", [P, NT, 8])
        number = sb("number", [P, E])
        lead, ratio = sb("lead", [P, NT]), sb("ratio", [P, NT])
        share = sb("share", [P, NT, 2])
        pick = sb("pick", [P, 2, NT, E])
        s_in, s_full, s_dve, s_exp = sem("in"), sem("full"), sem("dve"), sem("exp")
        s_number, s_turned, s_out, s_bias = sem("number"), sem("turned"), sem("out"), sem("bias")
        s_bias_full, s_twice = sem("bias_full"), sem("twice")
        LOGIT_BANK = 7
        with nc.Block() as block:
            @block.sync
            def _(sp):
                sp.dma_start(gate_w[:, :, :], a["L1_ffn_gate_W"].rearrange("(k p) e -> p k e", p=P)).then_inc(s_in, 16)
                sp.dma_start(gate_b[:, :], a["L1_ffn_gate_b"].partition_broadcast(P)).then_inc(s_in, 16)
                sp.dma_start(down_b[:, :], a["L1_ffn_exp_b2"]).then_inc(s_in, 16)
                sp.wait_ge(s_in, 48)

            @block.gpsimd
            def _(pool):
                for e in range(E):
                    pool.memset(number[:, e:e + 1], float(e)).then_inc(s_number, 1)
                    pool.wait_ge(s_number, e + 1)
                for t in range(NT):
                    pool.tensor_tensor(c.x_tok[:, t, :], c.x_tok[:, t, :], block_in[:, t, :], ALU.add).then_inc(s_twice, 1)

            @block.tensor
            def _(pe):
                pe.wait_ge(s_in, 48)
                for t in range(NT):
                    for k in range(DK):
                        ins = pe.matmul(c.psum[:, LOGIT_BANK, t * E:(t + 1) * E], c.xT[:, k, t * P:(t + 1) * P],
                                        gate_w[:, k, :], start=k == 0, stop=k == DK - 1)
                ins.then_inc(s_full, 1)
                pe.wait_ge(s_dve, 2 * NT + 11)
                for t in range(NT):
                    ins = pe.transpose(c.psum[0:E, t // QT, t % QT * P:(t % QT + 1) * P], weight[:, t, :], c.ident[:, :])
                    ins.then_inc(s_turned, 1)
                for t in range(NT):
                    pe.wait_ge(s_out, t // QT + 1)
                    wait_for(pe, s_bias, t - 3)
                    pe.matmul(c.psum[:, 4 + t % 4, 0:D], weight_T[:, t * P:(t + 1) * P], down_b[:, :],
                              start=True, stop=True).then_inc(s_bias_full, 1)

            @block.scalar
            def _(act):
                act.wait_ge(s_dve, 2 * NT + 3)
                act.activation(ratio[:, :], lead[:, :], ACT.Exp).then_inc(s_exp, 1)
                for q in range(NT // QT):
                    act.wait_ge(s_turned, QT * (q + 1))
                    act.activation(weight_T[:, q * SEQ:(q + 1) * SEQ], c.psum[0:E, q, :], ACT.Copy).then_inc(s_out, 1)

            @block.vector
            def _(v):
                done = 0

                def step(ins, wait=True):
                    nonlocal done
                    ins.then_inc(s_dve, 1)
                    done += 1
                    if wait:
                        v.wait_ge(s_dve, done)

                v.wait_ge(s_in, 48)
                v.wait_ge(s_full, 1)
                step(v.tensor_tensor(logits[:, :, :], c.psum[:, LOGIT_BANK, 0:NT * E].rearrange("p (t e) -> p t e", e=E),
                                     gate_b[:, :].unsqueeze(1).to_broadcast([P, NT, E]), ALU.add))
                for t in range(NT):
                    step(v.max(top[:, t, :], logits[:, t, :]), wait=t == NT - 1)
                for t in range(NT):
                    step(v.max_index(at[:, t, :], top[:, t, :], logits[:, t, :]), wait=t == NT - 1)
                step(v.tensor_copy(at_f[:, :, :], at[:, :, :]))
                step(v.tensor_tensor(lead[:, :], top[:, :, 1], top[:, :, 0], ALU.subtract))
                v.wait_ge(s_exp, 1)
                step(v.tensor_scalar(lead[:, :], ratio[:, :], 1.0, None, ALU.add))
                step(v.reciprocal(share[:, :, 0], lead[:, :]))
                step(v.tensor_tensor(share[:, :, 1], ratio[:, :], share[:, :, 0], ALU.mult))
                v.wait_ge(s_number, E)
                for x in range(2):
                    numbers = number[:, :].unsqueeze(1).to_broadcast([P, NT, E])
                    step(v.tensor_tensor(pick[:, x, :, :], numbers, at_f[:, :, x:x + 1].to_broadcast([P, NT, E]), ALU.is_equal))
                    step(v.tensor_tensor(pick[:, x, :, :], pick[:, x, :, :], share[:, :, x:x + 1].to_broadcast([P, NT, E]), ALU.mult))
                step(v.tensor_tensor(weight[:, :, :], pick[:, 0, :, :], pick[:, 1, :, :], ALU.add))
                assert done == 2 * NT + 11, done
                for t in range(NT):
                    v.wait_ge(s_bias_full, t + 1)
                    v.wait_ge(s_twice, t + 1)
                    v.tensor_tensor(c.x_tok[:, t, :], c.psum[:, 4 + t % 4, 0:D], c.x_tok[:, t, :], ALU.add).then_inc(s_bias, 1)


def build(nc, args, out):
    with ExitStack() as ctx:
        c = Core(nc, ctx, args, out)
        a = args
        stage_load(c)
        stage_norm(c, "x0", c.x_tok, NT, dstT=c.xT)
        q_dram = c.dram("q_parts", (2, BATCH * D, SEQ))
        k_self = c.dram("k_parts_self", (2, BATCH * D, SEQ))
        k_cross = c.dram("k_parts_cross", (2, BATCH * D, CTX_SEQ))
        v_self = c.dram("v_self", (NG, P, SEQ // P, GD))
        v_cross = c.dram("v_cross", (NG, P, CTX_SEQ // P, GD))

        def self_attention(name, wq, wk, wv, bq, bk, bv, wo, bo):
            stage_project(c, f"{name}_qkv", c.xT, P, T, split=((wq, bq, q_dram), (wk, bk, k_self)),
                          values=(wv, v_self))
            attend(name, k_self, v_self, bv, SEQ, True, wo, bo)

        def cross_attention(name, wq, wk, wv, bq, bk, bv, wo, bo):
            stage_project(c, f"{name}_q", c.xT, P, T, split=((wq, bq, q_dram),))
            with nc.sbuf_tensor(f"{name}_ctx", [CP, 2, CT], F32) as ctx_T:
                stage_fetch(c, f"{name}_ctx_in", [(ctx_T[:, k, :], a["ctxT"][k * CP:(k + 1) * CP, :]) for k in range(2)])
                stage_project(c, f"{name}_kv", ctx_T, CP, CT, split=((wk, bk, k_cross),), values=(wv, v_cross))
            attend(name, k_cross, v_cross, bv, CTX_SEQ, False, wo, bo)

        def attend(name, k_dram, v_dram, bv, keys, causal, wo, bo):
            with nc.sbuf_tensor(f"{name}_o_tok", [P, NT, D], F32) as o_tok:
                stage_attention(c, name, q_dram, k_dram, v_dram, bv, o_tok, keys, causal)
                stage_output(c, f"{name}_out", o_tok, wo, bo)

        w, b = a["L0_attn_w_attn"], a["L0_attn_b_attn"]
        self_attention("a0", w[:, 0:D], w[:, D:2 * D], w[:, 2 * D:], b[0:D], b[D:2 * D], b[2 * D:],
                       a["L0_attn_w_proj"], a["L0_attn_b_proj"])
        stage_norm(c, "n0", c.x_tok, NT, layernorm=True, dstT=c.xT)
        cross_attention("c0", *(a[f"L0_xattn_{x}"] for x in ("Wq", "Wk", "Wv", "bq", "bk", "bv", "Wo", "bo")))
        soft_moe(c)
        stage_norm(c, "n2", c.x_tok, NT, layernorm=True, dstT=c.xT)
        w = a["L1_attn_w_qkv"]
        self_attention("a1", w[:, 0:D], w[:, D:2 * D], w[:, 2 * D:], None, None, None, a["L1_attn_w_o"], None)
        stage_norm(c, "n3", c.x_tok, NT, layernorm=True, dstT=c.xT)
        cross_attention("c1", *(a[f"L1_xattn_{x}"] for x in ("wq", "wk", "wv", "bq", "bk", "bv", "wo", "bo")))
        stage_norm(c, "n4", c.x_tok, NT, layernorm=True, affine=(a["L1_ffn_ln1_g"], a["L1_ffn_ln1_b"]), dstT=c.xT)
        block_in = c.keep("block_in", [P, NT, D])
        stage_fetch(c, "block_in", [(block_in[:, :, :], c.x_tok[:, :, :])])
        self_attention("a2", *(a[f"L1_ffn_{x}"] for x in ("Wq", "Wk", "Wv", "bq", "bk", "bv", "Wp", "bp")))
        stage_norm(c, "n5", c.x_tok, NT, affine=(a["L1_ffn_ln2_g"], a["L1_ffn_ln2_b"]), dstT=c.xT)
        token_moe(c, block_in)
        stage_norm(c, "n6", c.x_tok, NT, layernorm=True, out=out)


TRANSPOSED = ("L0_attn_w_attn", "L0_attn_w_proj", "L0_xattn_Wq", "L0_xattn_Wk", "L0_xattn_Wv", "L0_xattn_Wo")


def kernel(**inputs):
    import concourse.bacc as bacc
    from concourse.bass_utils import run_bass_kernel_spmd

    nc = bacc.Bacc("TRN2", target_bir_lowering=False, num_devices=1)
    arrays, args = {}, {}
    for name, value in inputs.items():
        a = np.asarray(value)
        if name in TRANSPOSED:
            a = a.T
        if name == "ctx_768":
            name, a = "ctxT", a.reshape(CT, CTX_D).T
        if name in ("L0_ffn_b1", "L1_ffn_exp_b1"):
            a = a.reshape(EXPERTS, HM, P).transpose(0, 2, 1)
        a = np.ascontiguousarray(a)
        arrays[f"in_{name}"] = a
        args[name] = nc.dram_tensor(f"in_{name}", a.shape, mybir.dt.from_np(a.dtype), kind="ExternalInput").ap()
    out = nc.dram_tensor("out", (BATCH, SEQ, D), F32, kind="ExternalOutput").ap()
    build(nc, args, out)
    r = run_bass_kernel_spmd(nc, [arrays], core_ids=[0])
    return r.results[0]["out"]
```

```python
from contextlib import ExitStack, contextmanager

import concourse.bass as bass
from concourse import mybir
import numpy as np

F32 = mybir.dt.float32
F32R = mybir.dt.float32r
BF16 = mybir.dt.bfloat16
U32 = mybir.dt.uint32
ALU = mybir.AluOpType
ACT = mybir.ActivationFunctionType
AX_X = mybir.AxisListType.X

P = 128
BATCH, SEQ, D = 4, 512, 256
T = BATCH * SEQ
NT = T // P
QT = SEQ // P
DK = D // P
CTX_SEQ, CTX_D = 1024, 192
CP = CTX_D // 2
CT = BATCH * CTX_SEQ
HEADS, HD = 16, 16
GH = 4
GROUPS = HEADS // GH
GD = GH * HD
NG = BATCH * GROUPS
EXPERTS, SLOTS, HID = 8, 128, 1024
HM = HID // P
TILES = 2 * T // P + EXPERTS - 1
BANK = 512
NEG_BIG = -1.0e30
LN_EPS = 1e-5
SHIFT_ROW = 96
SHIFT_END = SHIFT_ROW + 3
STACK = P


def wait_for(eng, sem, count):
    if isinstance(count, int) and count <= 0:
        return
    eng.wait_ge(sem, count)


class Core:

    def __init__(self, nc, ctx, args, out):
        self.nc, self.ctx, self.args, self.out = nc, ctx, args, out
        self.slot_stored = [ctx.enter_context(nc.semaphore(f"slot_stored{i}")) for i in range(8)]
        self.slot_count = [0] * 8
        self.psum = ctx.enter_context(nc.psum_tensor("psum", [P, 8, BANK], F32))

    def sem(self, name):
        sem = self.stage_ctx.enter_context(self.nc.semaphore(name))
        self.stage_sems.append(sem)
        return sem

    @contextmanager
    def stage(self):
        self.stage_sems = []
        with ExitStack() as self.stage_ctx:
            yield
            with self.nc.Block() as block:
                @block.gpsimd
                def _(pool):
                    for sem in self.stage_sems:
                        pool.sem_clear(sem)

    def keep(self, name, shape, dt=F32):
        return self.ctx.enter_context(self.nc.sbuf_tensor(name, shape, dt))

    def dram(self, name, shape, dt=F32):
        return self.nc.dram_tensor(name, shape, dt, kind="Internal").ap()


def staged(build_stage):
    def run(c, *args, **named):
        with c.stage():
            build_stage(c, *args, **named)
    return run


@staged
def stage_load(c, rows_dram, rows_filled):
    nc = c.nc
    c.x_tok = c.keep("x_tok", [P, NT, D])
    c.xT = c.keep("xT", [P, DK, T])
    c.ident = c.keep("ident", [P, P])
    c.ident_bf = c.keep("ident_bf", [P, P], BF16)
    c.mask_qk = c.keep("mask_qk", [P, P], BF16)
    c.mask_kq = c.keep("mask_kq", [P, P], BF16)
    c.eps = c.keep("eps", [P, 1])
    loaded, filled, made = c.sem("x_loaded"), c.sem("const_filled"), c.sem("const_made")
    with nc.Block() as block:
        @block.sync
        def _(sp):
            sp.dma_start(c.x_tok[:, :, :], c.args["x"].rearrange("b (q p) d -> p (b q) d", p=P)).then_inc(loaded, 16)
            sp.wait_ge(loaded, 16)

        @block.scalar
        def _(act):
            for first in range(0, TILES * P, T):
                n = min(T, TILES * P - first)
                act.dma_start(rows_dram[first:first + n, :],
                              c.args["x"].rearrange("b s d -> (b s) d")[0:n, :]).then_inc(rows_filled, 16)

        @block.gpsimd
        def _(pool):
            for t in (c.ident, c.ident_bf, c.mask_qk, c.mask_kq):
                pool.memset(t[:, :], 0.0).then_inc(filled, 1)
            pool.memset(c.eps[:, :], LN_EPS).then_inc(made, 1)
            pool.wait_ge(filled, 4)
            for t in (c.ident, c.ident_bf):
                pool.affine_select(out=t[:, :], in_=t[:, :], compare_op=ALU.not_equal, fill=1.0, base=0,
                                   pattern=[[-1, P]], channel_multiplier=1).then_inc(made, 1)
            pool.affine_select(out=c.mask_qk[:, :], in_=c.mask_qk[:, :], compare_op=ALU.is_ge, fill=NEG_BIG,
                               base=0, pattern=[[-1, P]], channel_multiplier=1).then_inc(made, 1)
            pool.affine_select(out=c.mask_kq[:, :], in_=c.mask_kq[:, :], compare_op=ALU.is_ge, fill=NEG_BIG,
                               base=0, pattern=[[1, P]], channel_multiplier=-1).then_inc(made, 1)
            pool.wait_ge(made, 5)


@staged
def stage_fetch(c, name, pairs):
    loaded = c.sem(name)
    with c.nc.Block() as block:
        @block.sync
        def _(sp):
            for dst, src in pairs:
                sp.dma_start(dst, src).then_inc(loaded, 16)
            sp.wait_ge(loaded, 16 * len(pairs))


@staged
def stage_norm(c, name, src, tiles, layernorm=False, affine=None, rms=None, keep_tok=None, dstT=None, out=None):
    nc = c.nc
    with ExitStack() as ctx:
        def sb(n, shape, dt=F32):
            return ctx.enter_context(nc.sbuf_tensor(f"{name}_{n}", shape, dt))

        stats = sb("stats", [P, tiles, 6])
        mean_var = sb("mean_var", [P, 2, tiles, 2])
        root = sb("root", [P, 2, tiles])
        rstd = sb("rstd", [P, 2, tiles])
        squares = sb("squares", [P, 2, D])
        gain = sb("gain", [P, D])
        bias = sb("bias", [P, D])
        if keep_tok is None and (affine or rms):
            keep_tok = sb("rows", [P, tiles, D])
        coef_in, dve, rooted = c.sem(f"{name}_coef_in"), c.sem(f"{name}_dve"), c.sem(f"{name}_rooted")
        rows_ready, turned, evacuated = c.sem(f"{name}_rows_ready"), c.sem(f"{name}_turned"), c.sem(f"{name}_evacuated")
        stored = c.sem(f"{name}_stored")
        passes = int(layernorm) + int(affine is not None)
        rows = keep_tok if (affine or rms) else src
        coefs = list(affine or ()) + ([rms] if rms else [])

        with nc.Block() as block:
            @block.sync
            def _(sp):
                for tile, ap in zip((gain, bias), coefs):
                    sp.dma_start(tile[:, :], ap.partition_broadcast(P)).then_inc(coef_in, 16)
                if coefs:
                    sp.wait_ge(coef_in, 16 * len(coefs))
                if out is not None:
                    for b in range(tiles // QT):
                        sp.wait_ge(rows_ready, QT * (b + 1))
                        sp.dma_start(out[b].rearrange("(q p) d -> p q d", p=P),
                                     rows[:, b * QT:(b + 1) * QT, :]).then_inc(stored, 16)
                    sp.wait_ge(stored, 16 * (tiles // QT))

            @block.vector
            def _(v):
                done = 0

                def step(ins, wait=True):
                    nonlocal done
                    ins.then_inc(dve, 1)
                    done += 1
                    if wait:
                        v.wait_ge(dve, done)

                def statistics(n, which):
                    for t in range(tiles):
                        step(v.bn_stats(stats[:, t, :], which[:, t, :]), wait=t == tiles - 1)
                    for t in range(tiles):
                        step(v.bn_aggr(mean_var[:, n, t, :], stats[:, t, :]), wait=t == tiles - 1)
                    v.wait_ge(rooted, n + 1)
                    step(v.reciprocal(rstd[:, n, :], root[:, n, :]))

                n = 0
                if layernorm:
                    statistics(n, src)
                    for t in range(tiles):
                        ins = v.tensor_scalar(src[:, t, :], src[:, t, :], mean_var[:, n, t, 0:1], rstd[:, n, t:t + 1],
                                              ALU.subtract, ALU.mult)
                        if affine or rms:
                            step(ins, wait=t == tiles - 1)
                        else:
                            ins.then_inc(rows_ready, 1)
                    n += 1
                if affine:
                    statistics(n, src)
                    v.wait_ge(coef_in, 32)
                    for t in range(tiles):
                        step(v.tensor_scalar(rows[:, t, :], src[:, t, :], mean_var[:, n, t, 0:1], rstd[:, n, t:t + 1],
                                             ALU.subtract, ALU.mult), wait=t == tiles - 1)
                    for t in range(tiles):
                        step(v.tensor_tensor(rows[:, t, :], rows[:, t, :], gain[:, :], ALU.mult), wait=t == tiles - 1)
                    for t in range(tiles):
                        v.tensor_tensor(rows[:, t, :], rows[:, t, :], bias[:, :], ALU.add).then_inc(rows_ready, 1)
                if rms:
                    v.wait_ge(rooted, n + 1)
                    step(v.tensor_scalar(root[:, n, :], root[:, n, :], 1e-12, None, ALU.max))
                    step(v.reciprocal(rstd[:, n, :], root[:, n, :]))
                    step(v.tensor_scalar(rstd[:, n, :], rstd[:, n, :], float(D) ** 0.5, None, ALU.mult))
                    v.wait_ge(coef_in, 16)
                    for t in range(tiles):
                        v.scalar_tensor_tensor(rows[:, t, :], src[:, t, :], rstd[:, n, t:t + 1], gain[:, :],
                                               ALU.mult, ALU.mult).then_inc(rows_ready, 1)

            if dstT is not None:
                @block.tensor
                def _(pe):
                    if not (layernorm or affine or rms):
                        pass
                    else:
                        pe.wait_ge(rows_ready, tiles)
                    for t in range(0, tiles, QT):
                        for k in range(DK):
                            u = t // QT * DK + k
                            wait_for(pe, evacuated, u - 7)
                            for q in range(QT):
                                ins = pe.transpose(c.psum[:, u % 8, q * P:(q + 1) * P],
                                                   rows[:, t + q, k * P:(k + 1) * P], c.ident[:, :])
                            ins.then_inc(turned, 1)

            @block.scalar
            def _(act):
                squared = 0
                n = 0
                for _ in range(passes):
                    act.wait_ge(dve, 2 * tiles + n * (3 * tiles + 1))
                    act.activation(root[:, n, :], mean_var[:, n, :, 1], ACT.Sqrt, bias=c.eps[:, :]).then_inc(rooted, 1)
                    n += 1
                if rms:
                    if layernorm:
                        act.wait_ge(dve, 3 * tiles + 1)
                    for t in range(tiles):
                        if t >= 2:
                            act.wait_ge(evacuated, t - 1)
                        act.activation(squares[:, t % 2, :], src[:, t, :], ACT.Square,
                                       accum_out=root[:, n, t:t + 1]).then_inc(evacuated, 1)
                    act.wait_ge(evacuated, tiles)
                    act.activation(rstd[:, n, :], root[:, n, :], ACT.Sqrt).then_inc(evacuated, 1)
                    act.wait_ge(evacuated, tiles + 1)
                    act.activation(root[:, n, :], rstd[:, n, :], ACT.Copy).then_inc(rooted, 1)
                    squared = tiles + 1
                if dstT is not None:
                    for u in range(tiles // QT * DK):
                        act.wait_ge(turned, u + 1)
                        act.activation(dstT[:, u % DK, u // DK * SEQ:u // DK * SEQ + SEQ], c.psum[:, u % 8, :],
                                       ACT.Copy).then_inc(evacuated, 1)
                    act.wait_ge(evacuated, squared + tiles // QT * DK)


@staged
def stage_project(c, name, src, rows, tokens, split=(), values=None):
    nc = c.nc
    per = tokens // BATCH
    with ExitStack() as ctx:
        def sb(n, shape, dt=F32):
            return ctx.enter_context(nc.sbuf_tensor(f"{name}_{n}", shape, dt))

        weights = [sb(f"w{i}", [rows, 2, D]) for i in range(len(split))]
        biases = [sb(f"b{i}", [P, DK]) for i in range(len(split))]
        staged = sb("staged", [P, 8, 2, BANK])
        w_in, bank_full = c.sem(f"{name}_w_in"), c.sem(f"{name}_bank_full")
        head_done, bank_read = c.sem(f"{name}_head_done"), c.sem(f"{name}_bank_read")
        zeroed = c.sem(f"{name}_zeroed")
        stored, base = c.slot_stored, list(c.slot_count)
        if values:
            wv = sb("wv", [rows, 2, D])
        loads = len(split) + sum(x[1] is not None for x in split) + (values is not None)
        jobs = []
        for ch in range(tokens // BANK):
            jobs += [("split", i, m, ch) for i in range(len(split)) for m in range(DK)]
            if values:
                jobs += [("value", h, 0, ch) for h in range(2)]

        with nc.Block() as block:
            @block.sync
            def _(sp):
                for i, (w, b, _) in enumerate(split):
                    sp.dma_start(weights[i][:, :, :], w.rearrange("(k p) n -> p k n", p=rows)).then_inc(w_in, 16)
                    if b is not None:
                        sp.dma_start(biases[i][:, :], b.rearrange("(k p) -> p k", p=P),
                                     allow_slow_non_contiguous=True).then_inc(w_in, 16)
                if values:
                    sp.dma_start(wv[:, :, :], values[0].rearrange("(k p) n -> p k n", p=rows)).then_inc(w_in, 16)
                for u, (kind, i, m, ch) in enumerate(jobs):
                    sp.wait_ge(bank_read, u + 1)
                    b, at = ch * BANK // per, ch * BANK % per
                    if kind == "split":
                        row = b * D + m * P
                        sp.dma_start(split[i][2][:, row:row + P, at:at + BANK].rearrange("a p t -> p a t"),
                                     staged[:, u % 8, :, :]).then_inc(stored[u % 8], 16)
                    else:
                        kt = at // P + 2 * i
                        sp.dma_start(values[1][b * GROUPS:(b + 1) * GROUPS, :, kt:kt + 2, :].rearrange("g p t d -> p g (t d)"),
                                     staged[:, u % 8, 0, :].rearrange("p (g m) -> p g m", g=GROUPS)
                                     ).then_inc(stored[u % 8], 16)
                for s in range(8):
                    c.slot_count[s] += 16 * len(range(s, len(jobs), 8))
                    wait_for(sp, stored[s], c.slot_count[s])

            @block.gpsimd
            def _(pool):
                for i, (_, b, _) in enumerate(split):
                    if b is None:
                        pool.memset(biases[i][:, :], 0.0).then_inc(zeroed, 1)

            zeros = sum(x[1] is None for x in split)

            @block.tensor
            def _(pe):
                pe.wait_ge(w_in, 16 * loads)
                for u, (kind, i, m, ch) in enumerate(jobs):
                    wait_for(pe, bank_read, u - 7)
                    for half in range(1 if kind == "split" else 2):
                        for k in range(2):
                            if kind == "split":
                                ins = pe.matmul(c.psum[:, u % 8, :], weights[i][:, k, m * P:(m + 1) * P],
                                                src[:, k, ch * BANK:(ch + 1) * BANK], start=k == 0, stop=k == 1)
                            else:
                                t = ch * BANK + (2 * i + half) * P
                                ins = pe.matmul(c.psum[:, u % 8, half * D:(half + 1) * D], src[:, k, t:t + P],
                                                wv[:, k, :], start=k == 0, stop=k == 1)
                    ins.then_inc(bank_full, 1)

            @block.scalar
            def _(act):
                act.wait_ge(w_in, 16 * loads)
                wait_for(act, zeroed, zeros)
                for u, (kind, i, m, ch) in enumerate(jobs):
                    if kind == "split":
                        act.wait_ge(bank_full, u + 1)
                        if u >= 8:
                            act.wait_ge(stored[u % 8], base[u % 8] + 16 * (u // 8))
                        act.activation(staged[:, u % 8, 0, :].bitcast(F32R), c.psum[:, u % 8, :], ACT.Identity,
                                       bias=biases[i][:, m:m + 1]).then_inc(head_done, 1)

            @block.vector
            def _(v):
                heads = 0
                v.wait_ge(w_in, 16 * loads)
                wait_for(v, zeroed, zeros)
                for u, (kind, i, m, ch) in enumerate(jobs):
                    if kind == "split":
                        heads += 1
                        v.wait_ge(head_done, heads)
                        v.scalar_tensor_tensor(staged[:, u % 8, 1, :].bitcast(F32R), c.psum[:, u % 8, :],
                                               biases[i][:, m:m + 1], staged[:, u % 8, 0, :],
                                               ALU.add, ALU.subtract).then_inc(bank_read, 1)
                    else:
                        v.wait_ge(bank_full, u + 1)
                        if u >= 8:
                            v.wait_ge(stored[u % 8], base[u % 8] + 16 * (u // 8))
                        v.tensor_copy(staged[:, u % 8, 0, :].rearrange("p (g t d) -> p t g d", g=GROUPS, t=2),
                                      c.psum[:, u % 8, :].rearrange("p (t g d) -> p t g d", t=2, g=GROUPS)
                                      ).then_inc(bank_read, 1)


def attention_plan(KT, units, causal):
    def queries(t):
        return SEQ - t * P if causal else SEQ

    slots = [(t, h) for t in range(KT) for h in range(2)]
    load = [2 * queries(t) + (queries(t) if h else 0) for t, h in slots]
    cost = [unit[3] + P for unit in units]
    plan, u = [], 0
    for s, (t, h) in enumerate(slots):
        while u < len(units) and sum(cost[:u]) * sum(load) <= sum(load[:s]) * sum(cost):
            plan.append(("unit", 2, u))
            u += 1
        if KT - 1 <= s < KT - 1 + GH:
            plan.append(("shift", 1, s - KT + 1))
        plan.append(("scores", 0, s))
        if h == 1:
            plan += [("values", 0, t - 1)] if t else [("values", -1, KT - 1), ("drain", -1, 0)]
        if s == 4:
            plan.append(("turn", -1, 0))
    return plan + [("unit", 2, v) for v in range(u, len(units))]


@staged
def stage_attention(c, name, q_dram, k_dram, v_dram, v_bias, o_tok, keys, causal):
    nc = c.nc
    KT = keys // P
    units = [(j, qt, k0, (qt + 1) * P if causal else BANK)
             for j in range(GH) for qt in range(QT) for k0 in range(0, keys, BANK)]
    U = len(units)
    parts = U // (GH * QT)
    scale = 1.0 / float(HD) ** 0.5
    NB = 4
    SHIFT_STEPS = 6
    PV_BANK, RING = 6, (4, 5, 7)
    plan = attention_plan(KT, units, causal)
    ring_uses = [x for x in plan if x[0] in ("unit", "shift", "turn")]

    def exists(n, event):
        return 0 <= n + event[1] < NG

    def bank_before(n, event):
        at = ring_uses.index(event)
        for body in (n, n - 1, n - 2):
            same = [x for i, x in enumerate(ring_uses) if i % 3 == at % 3 and (body < n or i < at)]
            same = [x for x in same if exists(body, x)]
            if same:
                what, ahead, index = same[-1]
                return what, ahead + body - n, index
        return None

    with ExitStack() as ctx:
        def sb(n, shape, dt=F32):
            return ctx.enter_context(nc.sbuf_tensor(f"{name}_{n}", shape, dt))

        qs = [sb(f"q{i}", [STACK, GH, SEQ], F32R) for i in range(NB)]
        ks = [sb(f"k{i}", [STACK, GH, keys], F32R) for i in range(NB)]
        v_raw = [sb(f"v_raw{i}", [P, KT, GD]) for i in range(2)]
        v_aug = [sb(f"v_aug{i}", [P, KT, GH, 32]) for i in range(2)]
        bias = sb("v_bias", [P, D])
        probs = [sb(f"p{i}", [P, GH, SEQ]) for i in range(2)]
        max_parts = sb("max_parts", [P, U])
        row_max = sb("row_max", [P, GH * QT])
        rest = sb("rest", [P, 2, GH * QT])
        shift = sb("shift", [P, GH * QT, 3], BF16)
        o_sum = sb("o_sum", [P, SEQ])
        recip = sb("recip", [P, QT * GH])
        s_set = c.sem(f"{name}_set")
        s_bias = c.sem(f"{name}_v_bias")
        s_qk = [c.sem(f"{name}_qk_in{i}") for i in range(NB)]
        s_vin = [c.sem(f"{name}_v_in{i}") for i in range(2)]
        s_vaug = c.sem(f"{name}_v_aug")
        s_unit_full, s_unit_read = c.sem(f"{name}_unit_full"), c.sem(f"{name}_unit_read")
        s_shift = c.sem(f"{name}_shift")
        s_row_full, s_row = c.sem(f"{name}_row_full"), c.sem(f"{name}_row")
        s_score, s_exp = c.sem(f"{name}_score"), c.sem(f"{name}_exp")
        s_pv = c.sem(f"{name}_pv")
        s_osum, s_turn, s_norm = c.sem(f"{name}_o_sum"), c.sem(f"{name}_turn"), c.sem(f"{name}_norm")

        def first_query(t):
            return t * P if causal else 0

        def ring_bank(event):
            return RING[ring_uses.index(event) % 3]

        with nc.Block() as block:
            def for_groups(eng, body):
                for r in range(GROUPS):
                    body(r, 0, r, r)
                with eng.Fori(1, BATCH - 1) as b:
                    for r in range(GROUPS):
                        body(b * GROUPS + r, b, r, GROUPS + r)
                for r in range(GROUPS):
                    body((BATCH - 1) * GROUPS + r, BATCH - 1, r, (BATCH - 1) * GROUPS + r)

            def run_plan(eng, handlers):
                def body(n, b, r, like):
                    for event in plan:
                        what, ahead, index = event
                        if what in handlers and exists(like, event):
                            g = (r + ahead) % GROUPS
                            batch = b + (r + ahead - g) // GROUPS
                            handlers[what](n + ahead, batch, g, index, n, like, event)

                body(-2, -1, 2, -2)
                body(-1, -1, 3, -1)
                for_groups(eng, body)
                body(NG, BATCH, 0, NG)

            @block.sync
            def _(sp):
                def body(n, b, r, like):
                    wait_for(sp, s_score, 2 * KT * (n - NB + 1))
                    for blk, (qp, kp) in enumerate(((0, 0), (0, 1), (1, 0), (1, 1))):
                        at = slice(HD * blk, HD * (blk + 1))
                        sp.dma_start(qs[r][at, :, :].bitcast(F32),
                                     q_dram[qp, bass.ds(n * GD, GD), :].rearrange("(j d) t -> d j t", d=HD)
                                     ).then_inc(s_qk[r], 16)
                        sp.dma_start(ks[r][at, :, :].bitcast(F32),
                                     k_dram[kp, bass.ds(n * GD, GD), :].rearrange("(j d) t -> d j t", d=HD)
                                     ).then_inc(s_qk[r], 16)
                    wait_for(sp, s_vaug, n - 1)
                    sp.dma_start(v_raw[r % 2][:, :, :], v_dram[bass.ds(n, 1), :, :, :].rearrange("o p t d -> p (o t) d")
                                 ).then_inc(s_vin[r % 2], 16)

                if v_bias is not None:
                    sp.dma_start(bias[:, :], v_bias.partition_broadcast(P)).then_inc(s_bias, 16)
                for_groups(sp, body)

            @block.gpsimd
            def _(pool):
                steps = 0
                if v_bias is None:
                    pool.memset(bias[:, :], 0.0).then_inc(s_bias, 1)
                pool.wait_ge(s_bias, 1 if v_bias is None else 16)
                for i in range(NB):
                    fills = [(qs[i][64:STACK, :, :].bitcast(F32), 0.0), (ks[i][64:STACK, :, :].bitcast(F32), 1.0)]
                    fills += [(t[:, :, :, :], 1.0) for t in v_aug] if i == 1 else []
                    for ap, value in fills:
                        pool.memset(ap, value).then_inc(s_set, 1)
                        steps += 1
                        pool.wait_ge(s_set, steps)

                def body(n, b, r, like):
                    pool.wait_ge(s_vin[r % 2], 16 * (b * (GROUPS // 2) + r // 2 + 1))
                    wait_for(pool, s_pv, KT * (n - 1))
                    own = bias[:, r * GD:(r + 1) * GD].rearrange("p (j d) -> p j d", d=HD).unsqueeze(1)
                    pool.tensor_tensor(v_aug[r % 2][:, :, :, 0:HD],
                                       v_raw[r % 2][:, :, :].rearrange("p t (j d) -> p t j d", d=HD),
                                       own.to_broadcast([P, KT, GH, HD]), ALU.add).then_inc(s_vaug, 1)

                for_groups(pool, body)

            @block.tensor
            def _(pe):
                def wait_bank(n, like, event):
                    found = bank_before(like, event)
                    if found is None:
                        return
                    what, ahead, index = found
                    if what == "unit":
                        pe.wait_ge(s_unit_read, (n + ahead) * U + index + 1)
                    elif what == "turn":
                        pe.wait_ge(s_norm, 2 * (n + ahead + 1))
                    else:
                        pe.wait_ge(s_row, GH * (n + ahead) + index + 1)

                def unit(g, b, r, u, n, like, event):
                    if u == 0:
                        if like + 2 < NB:
                            pe.wait_ge(s_set, (2, 4, 8, 10)[like + 2])
                        pe.wait_ge(s_qk[r], 128 * (b + 1))
                    wait_bank(n, like, event)
                    j, qt, k0, width = units[u]
                    bank = ring_bank(event)
                    ins = pe.matmul(c.psum[:, bank, 0:width], qs[r][0:SHIFT_ROW, j, qt * P:(qt + 1) * P],
                                    ks[r][0:SHIFT_ROW, j, k0:k0 + width], start=True, stop=not causal)
                    if causal:
                        ins = pe.matmul(c.psum[:, bank, qt * P:(qt + 1) * P], c.ident_bf[:, :],
                                        c.mask_qk[:, :], start=False, stop=True)
                    ins.then_inc(s_unit_full, 1)

                def shift_row(g, b, r, j, n, like, event):
                    if j == 0:
                        pe.wait_ge(s_shift, SHIFT_STEPS * (g + 1))
                    wait_bank(n, like, event)
                    for qt in range(QT):
                        ins = pe.matmul(c.psum[SHIFT_ROW:SHIFT_END, ring_bank(event), qt * P:(qt + 1) * P],
                                        shift[:, j * QT + qt, :], c.ident_bf[:, :], start=True, stop=True)
                    ins.then_inc(s_row_full, 1)

                def scores(g, b, r, s, n, like, event):
                    t, h = s // 2, s % 2
                    if t == 0:
                        pe.wait_ge(s_row, GH * g + 2 * h + 2)
                    wait_for(pe, s_exp, 2 * KT * g + s - 1)
                    q0 = first_query(t)
                    for j in range(2 * h, 2 * h + 2):
                        bank = 2 * (s % 2) + j % 2
                        ins = pe.matmul(c.psum[:, bank, q0:SEQ], ks[r][0:STACK, j, t * P:(t + 1) * P],
                                        qs[r][0:STACK, j, q0:SEQ], start=True, stop=not causal)
                        if causal:
                            ins = pe.matmul(c.psum[:, bank, q0:q0 + P], c.ident_bf[:, :], c.mask_kq[:, :],
                                            start=False, stop=True)
                    ins.then_inc(s_score, 1)

                def values(g, b, r, t, n, like, event):
                    pe.wait_ge(s_exp, 2 * KT * g + 2 * t + 2)
                    if t == 0:
                        pe.wait_ge(s_vaug, g + 1)
                        wait_for(pe, s_osum, g)
                    q0 = first_query(t)
                    for j in range(GH):
                        ins = pe.matmul(c.psum[32 * j:32 * j + 32, PV_BANK, q0:SEQ], v_aug[r % 2][:, t, j, :],
                                        probs[t % 2][:, j, q0:SEQ], start=t == 0, stop=t == KT - 1)
                    ins.then_inc(s_pv, 1)

                def turn(g, b, r, _, n, like, event):
                    pe.wait_ge(s_osum, g + 1)
                    wait_bank(n, like, event)
                    for qt in range(QT):
                        ins = pe.transpose(c.psum[:, ring_bank(event), qt * P:(qt + 1) * P],
                                           o_sum[:, qt * P:(qt + 1) * P], c.ident[:, :])
                    ins.then_inc(s_turn, 1)

                run_plan(pe, {"unit": unit, "shift": shift_row, "scores": scores, "values": values, "turn": turn})

            @block.scalar
            def _(act):
                def shift_row(g, b, r, j, n, like, event):
                    act.wait_ge(s_row_full, GH * g + j + 1)
                    act.activation(qs[r][SHIFT_ROW:SHIFT_END, j, :], c.psum[SHIFT_ROW:SHIFT_END, ring_bank(event), :],
                                   ACT.Copy).then_inc(s_row, 1)

                def exps(g, b, r, s, n, like, event):
                    t, h = s // 2, s % 2
                    q0 = first_query(t)
                    act.wait_ge(s_score, 2 * KT * g + s + 1)
                    wait_for(act, s_pv, KT * g + t - 1)
                    act.activation(probs[t % 2][:, 2 * h:2 * h + 2, q0:SEQ],
                                   c.psum[:, 2 * (s % 2):2 * (s % 2) + 2, q0:SEQ], ACT.Exp,
                                   scale=scale).then_inc(s_exp, 1)

                def drain_outputs(g, b, r, _, n, like, event):
                    act.wait_ge(s_pv, KT * (g + 1))
                    wait_for(act, s_turn, g)
                    act.activation(o_sum[:, :], c.psum[:, PV_BANK, :], ACT.Copy).then_inc(s_osum, 1)

                run_plan(act, {"shift": shift_row, "scores": exps, "drain": drain_outputs})

            @block.vector
            def _(v):
                def unit(g, b, r, u, n, like, event):
                    v.wait_ge(s_unit_full, g * U + u + 1)
                    if u == 0:
                        wait_for(v, s_shift, SHIFT_STEPS * g)
                    v.reduce_max(max_parts[:, u:u + 1], c.psum[:, ring_bank(event), 0:units[u][3]],
                                 axis=AX_X).then_inc(s_unit_read, 1)
                    if u == U - 1:
                        shift_parts(g)

                def shift_parts(g):
                    at = SHIFT_STEPS * g
                    v.wait_ge(s_unit_read, U * (g + 1))
                    wait_for(v, s_row_full, GH * g)
                    v.tensor_reduce(row_max[:, :], max_parts[:, :].rearrange("p (u k) -> p u k", k=parts),
                                    axis=AX_X, op=ALU.max).then_inc(s_shift, 1)
                    v.wait_ge(s_shift, at + 1)
                    v.tensor_scalar(shift[:, :, 0], row_max[:, :], -1.0, None, ALU.mult).then_inc(s_shift, 1)
                    v.wait_ge(s_shift, at + 2)
                    v.scalar_tensor_tensor(rest[:, 0, :], row_max[:, :], -1.0, shift[:, :, 0], ALU.mult,
                                           ALU.subtract).then_inc(s_shift, 1)
                    v.wait_ge(s_shift, at + 3)
                    v.tensor_copy(shift[:, :, 1], rest[:, 0, :]).then_inc(s_shift, 1)
                    v.wait_ge(s_shift, at + 4)
                    v.tensor_tensor(rest[:, 1, :], rest[:, 0, :], shift[:, :, 1], ALU.subtract).then_inc(s_shift, 1)
                    v.wait_ge(s_shift, at + 5)
                    v.tensor_copy(shift[:, :, 2], rest[:, 1, :]).then_inc(s_shift, 1)

                def normalise(g, b, r, _, n, like, event):
                    v.wait_ge(s_turn, g + 1)
                    turned = c.psum[:, ring_bank(event), :].rearrange("p (a c) -> p a c", c=32)
                    wait_for(v, s_norm, 2 * g)
                    v.reciprocal(recip[:, :].unsqueeze(2), turned[:, :, HD:HD + 1]).then_inc(s_norm, 1)
                    v.wait_ge(s_norm, 2 * g + 1)
                    dst = o_tok[:, bass.ds(b * QT, QT), r * GD:(r + 1) * GD].rearrange("p q (j d) -> p q j d", d=HD)
                    v.tensor_tensor(dst, turned[:, :, 0:HD].rearrange("p (q j) d -> p q j d", j=GH),
                                    recip[:, :].rearrange("p (q j) -> p q j", j=GH).unsqueeze(3)
                                    .to_broadcast([P, QT, GH, HD]), ALU.mult).then_inc(s_norm, 1)

                run_plan(v, {"unit": unit, "turn": normalise})


@staged
def stage_output(c, name, o_tok, w, b):
    nc = c.nc
    with ExitStack() as ctx:
        def sb(n, shape, dt=F32):
            return ctx.enter_context(nc.sbuf_tensor(f"{name}_{n}", shape, dt))

        wo = sb("wo", [P, DK, D])
        bo = sb("bo", [P, D])
        oT = sb("oT", [P, 4, DK, P])
        w_in, turned, evacuated = c.sem(f"{name}_w_in"), c.sem(f"{name}_turned"), c.sem(f"{name}_evacuated")
        projected, added, biased = c.sem(f"{name}_projected"), c.sem(f"{name}_added"), c.sem(f"{name}_biased")
        loads = 1 + (b is not None)

        with nc.Block() as block:
            @block.sync
            def _(sp):
                sp.dma_start(wo[:, :, :], w.rearrange("(k p) n -> p k n", p=P)).then_inc(w_in, 16)
                if b is not None:
                    sp.dma_start(bo[:, :], b.partition_broadcast(P)).then_inc(w_in, 16)
                sp.wait_ge(w_in, 16 * loads)

            @block.tensor
            def _(pe):
                def turn(t):
                    wait_for(pe, evacuated, t - 3)
                    for k in range(DK):
                        ins = pe.transpose(c.psum[:, t % 4, k * P:(k + 1) * P],
                                           o_tok[:, t, k * P:(k + 1) * P], c.ident[:, :])
                    ins.then_inc(turned, 1)

                turn(0)
                turn(1)
                pe.wait_ge(w_in, 16 * loads)
                for t in range(NT):
                    if t + 2 < NT:
                        turn(t + 2)
                    pe.wait_ge(evacuated, t + 1)
                    wait_for(pe, added, t - 3)
                    for k in range(DK):
                        ins = pe.matmul(c.psum[:, 4 + t % 4, 0:D], oT[:, t % 4, k, :], wo[:, k, :],
                                        start=k == 0, stop=k == DK - 1)
                    ins.then_inc(projected, 1)

            @block.scalar
            def _(act):
                for t in range(NT):
                    act.wait_ge(turned, t + 1)
                    wait_for(act, projected, t - 3)
                    act.activation(oT[:, t % 4, :, :], c.psum[:, t % 4, 0:DK * P].rearrange("p (k n) -> p k n", k=DK),
                                   ACT.Copy).then_inc(evacuated, 1)

            @block.gpsimd
            def _(pool):
                if b is not None:
                    pool.wait_ge(w_in, 16 * loads)
                    for t in range(NT):
                        pool.tensor_tensor(c.x_tok[:, t, :], c.x_tok[:, t, :], bo[:, :], ALU.add).then_inc(biased, 1)

            @block.vector
            def _(v):
                for t in range(NT):
                    v.wait_ge(projected, t + 1)
                    if b is not None:
                        v.wait_ge(biased, t + 1)
                    v.tensor_tensor(c.x_tok[:, t, :], c.psum[:, 4 + t % 4, 0:D], c.x_tok[:, t, :],
                                    ALU.add).then_inc(added, 1)


@staged
def stage_experts(c, name, w1, b1, w2, b2, tokens_of, eo):
    nc = c.nc
    with ExitStack() as ctx:
        def sb(n, shape, dt=F32):
            return ctx.enter_context(nc.sbuf_tensor(f"{name}_{n}", shape, dt))

        up = [sb(f"up{i}", [P, DK, HID]) for i in range(2)]
        down = [sb(f"down{i}", [P, HM, D]) for i in range(2)]
        up_bias = [sb(f"up_bias{i}", [P, HM]) for i in range(2)]
        down_bias = [sb(f"down_bias{i}", [P, D]) for i in range(2)]
        hidden = sb("hidden", [P, HM, BANK])
        w_in = [c.sem(f"{name}_w_in{i}") for i in range(2)]
        s_up, s_gelu = c.sem(f"{name}_up"), c.sem(f"{name}_gelu")
        s_down, s_read = c.sem(f"{name}_down"), c.sem(f"{name}_read")
        per_load = 16 * 4
        tiles = BANK // P
        UP_BANKS = 4

        with nc.Block() as block:
            def for_experts(eng, body):
                for r in range(2):
                    body(r, 0, r)
                with eng.Fori(1, EXPERTS // 2) as pair:
                    for r in range(2):
                        body(pair * 2 + r, pair, r)

            @block.sync
            def _(sp):
                def body(e, pair, r):
                    wait_for(sp, s_down, tiles * (e - 1))
                    one = bass.ds(e, 1)
                    sp.dma_start(up[r][:, :, :], w1[one, :, :].rearrange("o (k p) n -> p (o k) n", p=P)).then_inc(w_in[r], 16)
                    sp.dma_start(up_bias[r][:, :], b1[one, :, :].rearrange("o p m -> p (o m)")).then_inc(w_in[r], 16)
                    sp.dma_start(down[r][:, :, :], w2[one, :, :].rearrange("o (m p) n -> p (o m) n", p=P)).then_inc(w_in[r], 16)
                    wait_for(sp, s_read, tiles * (e - 1))
                    sp.dma_start(down_bias[r][:, :], b2[one, :].rearrange("o n -> (o n)").partition_broadcast(P)
                                 ).then_inc(w_in[r], 16)

                for_experts(sp, body)

            @block.tensor
            def _(pe):
                def body(e, pair, r):
                    pe.wait_ge(w_in[r], (pair + 1) * per_load)
                    for m in range(HM):
                        wait_for(pe, s_gelu, e * HM + m - UP_BANKS + 1)
                        for k in range(DK):
                            ins = pe.matmul(c.psum[:, m % UP_BANKS, :], up[r][:, k, m * P:(m + 1) * P],
                                            tokens_of(e, k), start=k == 0, stop=k == DK - 1)
                        ins.then_inc(s_up, 1)
                    for t in range(tiles):
                        wait_for(pe, s_read, (e - 1) * tiles + t + 1)
                        for m in range(HM):
                            if t == 0:
                                pe.wait_ge(s_gelu, e * HM + m + 1)
                            ins = pe.matmul(c.psum[:, 4 + t, 0:D], hidden[:, m, t * P:(t + 1) * P],
                                            down[r][:, m, :], start=m == 0, stop=m == HM - 1)
                        ins.then_inc(s_down, 1)

                for_experts(pe, body)

            @block.scalar
            def _(act):
                def body(e, pair, r):
                    act.wait_ge(w_in[r], (pair + 1) * per_load)
                    wait_for(act, s_down, e * tiles)
                    for m in range(HM):
                        act.wait_ge(s_up, e * HM + m + 1)
                        act.activation(hidden[:, m, :], c.psum[:, m % UP_BANKS, :], ACT.Gelu,
                                       bias=up_bias[r][:, m:m + 1]).then_inc(s_gelu, 1)

                for_experts(act, body)

            @block.vector
            def _(v):
                def body(e, pair, r):
                    v.wait_ge(w_in[r], (pair + 1) * per_load)
                    for t in range(tiles):
                        v.wait_ge(s_down, e * tiles + t + 1)
                        v.tensor_tensor(eo[:, bass.ds(e, 1), t, :], c.psum[:, 4 + t, 0:D].unsqueeze(1),
                                        down_bias[r][:, :].unsqueeze(1), ALU.add).then_inc(s_read, 1)

                for_experts(v, body)


def soft_moe(c):
    nc, a = c.nc, c.args
    ES = EXPERTS * SLOTS
    with ExitStack() as ctx:
        def keep(n, shape):
            return ctx.enter_context(nc.sbuf_tensor(f"soft_{n}", shape, F32))

        slots_T = keep("slots_T", [P, EXPERTS, DK, BATCH * SLOTS])
        combine = keep("combine", [P, EXPERTS, NT, P])
        with ExitStack() as inner:
            h_tok = inner.enter_context(nc.sbuf_tensor("soft_h_tok", [P, NT, D], F32))
            slot_T = inner.enter_context(nc.sbuf_tensor("soft_slot_T", [P, DK, ES], F32))
            with nc.sbuf_tensor("soft_embeds", [P, EXPERTS, D], F32) as embeds:
                stage_fetch(c, "soft_embeds_in", [(embeds[:, :, :], a["L0_ffn_slot_embeds"].rearrange("e s d -> s e d"))])
                stage_norm(c, "slot", embeds, EXPERTS, rms=a["L0_ffn_slot_norm_gamma"], dstT=slot_T)
            stage_norm(c, "n1", c.x_tok, NT, layernorm=True, rms=a["L0_ffn_norm_gamma"], keep_tok=h_tok, dstT=c.xT)
            stage_soft_routes(c, h_tok, slot_T, slots_T, combine)
        outputs = slots_T[:, :, :, :].rearrange("p e k (h n) -> p e (k h) n", n=D)
        stage_experts(c, "soft_experts", a["L0_ffn_w1"], a["L0_ffn_b1"], a["L0_ffn_w2"], a["L0_ffn_b2"],
                      lambda e, k: slots_T[:, bass.ds(e, 1), k, :].rearrange("p o n -> p (o n)"), eo=outputs)
        stage_combine(c, combine, outputs)


@staged
def stage_soft_routes(c, h_tok, slot_T, slots_T, combine):
    nc = c.nc
    with ExitStack() as ctx:
        def sb(n, shape, dt=F32):
            return ctx.enter_context(nc.sbuf_tensor(f"route_{n}", shape, dt))

        def sem(n):
            return c.sem(f"route_{n}")

        jobs = []
        for b in range(BATCH):
            jobs += [("dispatch", b, e) for e in range(EXPERTS)] + [("combine", b, q) for q in range(QT)]
            jobs += [("slots", b, k) for k in range(DK)]
        soft = [i for i, job in enumerate(jobs) if job[0] != "slots"]
        place = {i: n for n, i in enumerate(soft)}
        probs = sb("probs", [P, 2, 2, BANK])
        dispatch = sb("dispatch", [P, QT, EXPERTS * SLOTS])
        low, total, inverse = sb("low", [P, len(soft)]), sb("total", [P, len(soft)]), sb("inverse", [P, len(soft)])
        s_full, s_low, s_exp, s_inverse = sem("full"), sem("low"), sem("exp"), sem("inverse")
        s_scaled, s_turned, s_out, s_slots = sem("scaled"), sem("turned"), sem("out"), sem("slots")

        def banks(i):
            return 2 if jobs[i][0] != "dispatch" else 1

        def slots_before(i):
            return sum(job[0] == "slots" for job in jobs[:i])

        with nc.Block() as block:
            @block.tensor
            def _(pe):
                def fill(i):
                    kind, b, n = jobs[i]
                    if i >= 2:
                        if i - 2 in place:
                            pe.wait_ge(s_exp, place[i - 2] + 1)
                        else:
                            pe.wait_ge(s_slots, slots_before(i - 2) + 1)
                    if kind == "slots":
                        pe.wait_ge(s_out, max(place[x] for x in soft if jobs[x][:2] == ("dispatch", b)) + 1)
                    for h in range(banks(i)):
                        bank = c.psum[:, 2 * (i % 2) + h, :]
                        if kind == "dispatch":
                            for k in range(DK):
                                ins = pe.matmul(bank, slot_T[:, k, n * SLOTS:(n + 1) * SLOTS],
                                                c.xT[:, k, b * SEQ:(b + 1) * SEQ], start=k == 0, stop=k == DK - 1)
                        elif kind == "combine":
                            t = b * SEQ + n * P
                            for k in range(DK):
                                ins = pe.matmul(bank, c.xT[:, k, t:t + P], slot_T[:, k, h * BANK:(h + 1) * BANK],
                                                start=k == 0, stop=k == DK - 1)
                        else:
                            for q in range(QT):
                                ins = pe.matmul(bank, h_tok[:, b * QT + q, n * P:(n + 1) * P],
                                                dispatch[:, q, h * BANK:(h + 1) * BANK], start=q == 0, stop=q == QT - 1)
                    ins.then_inc(s_full, 1)

                def turn(i):
                    n = place[i]
                    pe.wait_ge(s_scaled, n + 1)
                    if n >= 2:
                        pe.wait_ge(s_out, n - 1)
                    for h in range(banks(i)):
                        for q in range(BANK // P):
                            ins = pe.transpose(c.psum[:, 4 + 2 * (n % 2) + h, q * P:(q + 1) * P],
                                               probs[:, n % 2, h, q * P:(q + 1) * P], c.ident[:, :])
                    ins.then_inc(s_turned, 1)

                for i in range(len(jobs)):
                    fill(i)
                    if i >= 1 and i - 1 in place:
                        turn(i - 1)

            @block.vector
            def _(v):
                def lows(i):
                    n = place[i]
                    v.wait_ge(s_full, i + 1)
                    src = c.psum[:, 2 * (i % 2):2 * (i % 2) + banks(i), :]
                    v.tensor_reduce(low[:, n:n + 1], src, axis=mybir.AxisListType.XY, op=ALU.max,
                                    negate=True).then_inc(s_low, 1)

                def scale(i):
                    n = place[i]
                    v.wait_ge(s_exp, n + 1)
                    v.reciprocal(inverse[:, n:n + 1], total[:, n:n + 1]).then_inc(s_inverse, 1)
                    v.wait_ge(s_inverse, n + 1)
                    own = probs[:, n % 2, 0:banks(i), :]
                    v.tensor_scalar(own, own, inverse[:, n:n + 1], None, ALU.mult).then_inc(s_scaled, 1)

                for i in range(len(jobs) + 1):
                    if i < len(jobs) and i in place:
                        lows(i)
                    if i >= 1 and i - 1 in place:
                        scale(i - 1)

            @block.scalar
            def _(act):
                def exps(i):
                    n = place[i]
                    act.wait_ge(s_low, n + 1)
                    if n >= 2:
                        act.wait_ge(s_turned, n - 1)
                    act.activation(probs[:, n % 2, 0:banks(i), :], c.psum[:, 2 * (i % 2):2 * (i % 2) + banks(i), :],
                                   ACT.Exp, bias=low[:, n:n + 1], accum_out=total[:, n:n + 1]).then_inc(s_exp, 1)

                def evacuate(i):
                    kind, b, x = jobs[i]
                    n = place[i]
                    act.wait_ge(s_turned, n + 1)
                    pair = 4 + 2 * (n % 2)
                    if kind == "dispatch":
                        act.activation(dispatch[:, :, x * SLOTS:(x + 1) * SLOTS],
                                       c.psum[:, pair, :].rearrange("p (q s) -> p q s", q=QT), ACT.Copy).then_inc(s_out, 1)
                    else:
                        act.activation(combine[:, :, b * QT + x, :],
                                       c.psum[:, pair:pair + 2, :].rearrange("p h (e n) -> p (h e) n", n=P),
                                       ACT.Copy).then_inc(s_out, 1)

                def slots(i):
                    _, b, k = jobs[i]
                    act.wait_ge(s_full, i + 1)
                    pair = 2 * (i % 2)
                    act.activation(slots_T[:, :, k, b * SLOTS:(b + 1) * SLOTS],
                                   c.psum[:, pair:pair + 2, :].rearrange("p h (e n) -> p (h e) n", n=SLOTS),
                                   ACT.Copy).then_inc(s_slots, 1)

                for i in range(len(jobs)):
                    if i in place:
                        exps(i)
                    if i >= 1 and i - 1 in place:
                        evacuate(i - 1)
                    if i not in place:
                        slots(i)


@staged
def stage_combine(c, combine, outputs):
    s_full, s_read = c.sem("combine_full"), c.sem("combine_read")
    with c.nc.Block() as block:
        @block.tensor
        def _(pe):
            for t in range(NT):
                wait_for(pe, s_read, t - 7)
                for e in range(EXPERTS):
                    ins = pe.matmul(c.psum[:, t % 8, 0:D], combine[:, e, t, :], outputs[:, e, t // QT, :],
                                    start=e == 0, stop=e == EXPERTS - 1)
                ins.then_inc(s_full, 1)

        @block.vector
        def _(v):
            for t in range(NT):
                v.wait_ge(s_full, t + 1)
                v.tensor_tensor(c.x_tok[:, t, :], c.psum[:, t % 8, 0:D], c.x_tok[:, t, :], ALU.add).then_inc(s_read, 1)


def token_moe(c, block_in, rows_dram, rows_filled):
    nc, a = c.nc, c.args
    results_dram = c.dram("expert_results", (TILES * P, D))
    with ExitStack() as ctx:
        def keep(n, shape, dt=F32):
            return ctx.enter_context(nc.sbuf_tensor(f"routed_{n}", shape, dt))

        up_in = ctx.enter_context(nc.semaphore("routed_up_in"))
        down_in = ctx.enter_context(nc.semaphore("routed_down_in"))
        share = keep("share", [P, NT, 2])
        place = keep("place", [P, 2, NT], U32)
        expert_of = keep("expert_of", [P, TILES], U32)
        with nc.sbuf_tensor("routed_up", [P, EXPERTS, DK, HID], F32) as up:
            stage_start_weights(c, up, a["L1_ffn_exp_W1"], up_in)
            with nc.sbuf_tensor("routed_h_tok", [P, NT, D], F32) as h_tok:
                stage_norm(c, "n5", c.x_tok, NT, affine=(a["L1_ffn_ln2_g"], a["L1_ffn_ln2_b"]), keep_tok=h_tok, dstT=c.xT)
                stage_gate(c, share, place, expert_of, block_in, h_tok, rows_dram, rows_filled)
            with nc.sbuf_tensor("routed_down", [P, EXPERTS, HM, D], F32) as down:
                stage_routed_experts(c, up, up_in, down, down_in, expert_of, rows_dram, results_dram)
        stage_gather(c, share, place, results_dram)


@staged
def stage_start_weights(c, up, w1, up_in):
    with c.nc.Block() as block:
        @block.sync
        def _(sp):
            for e in range(EXPERTS):
                sp.dma_start(up[:, e, :, :], w1[e].rearrange("(k p) n -> p k n", p=P)).then_inc(up_in, 16)


@staged
def stage_routed_experts(c, up, up_in, down, down_in, expert_of, rows_dram, results_dram):
    nc, a = c.nc, c.args
    HALVES = HID // BANK
    PER = BANK // P
    X_BANK, UP_BANK, TURN_BANK, DOWN_BANK = 0, 1, 3, 5
    with ExitStack() as ctx:
        def sb(n, shape, dt=F32):
            return ctx.enter_context(nc.sbuf_tensor(f"routed_{n}", shape, dt))

        def sem(n):
            return c.sem(f"routed_{n}")

        bias = sb("bias", [P, EXPERTS * HM])
        rows = [sb(f"rows{i}", [P, D]) for i in range(2)]
        rows_T = [sb(f"rows_T{i}", [P, DK, P]) for i in range(2)]
        raw = [sb(f"raw{i}", [P, HID]) for i in range(2)]
        hidden = [sb(f"hidden{i}", [P, HM, P]) for i in range(2)]
        result = [sb(f"result{i}", [P, D]) for i in range(2)]
        rows_in, stored = [sem(f"rows_in{i}") for i in range(2)], [sem(f"stored{i}") for i in range(2)]
        bias_in, x_turned, x_read, up_full = sem("bias_in"), sem("x_turned"), sem("x_read"), sem("up_full")
        raw_read, h_turned, gelu_done = sem("raw_read"), sem("h_turned"), sem("gelu_done")
        y_full, y_read = sem("y_full"), sem("y_read")
        FIRST, PAIRS = 5, (TILES - 1 - 5) // 2

        def tile_at(s, pair, lag):
            t = s - lag
            if isinstance(pair, int) and not 0 <= t < TILES:
                return None
            return t + pair * 2, t % 2, t // 2 + pair

        def for_steps(eng, body):
            for s in range(FIRST):
                body(s, 0)
            with eng.Fori(0, PAIRS) as pair:
                for r in range(2):
                    body(FIRST + r, pair)
            for s in range(FIRST + 2 * PAIRS, TILES + 3):
                body(s, 0)

        def weights_of(eng, t):
            return eng.value_load(expert_of[0:1, bass.ds(t, 1)], min_val=0, max_val=EXPERTS - 1)

        with nc.Block() as block:
            @block.sync
            def _(sp):
                def load(at):
                    t, r, _ = at
                    wait_for(sp, x_turned, t - 1)
                    sp.dma_start(rows[r][:, :], rows_dram[bass.ds(t * P, P), :]).then_inc(rows_in[r], 16)

                def body(s, pair):
                    if ahead := tile_at(s, pair, -1):
                        load(ahead)
                    if done := tile_at(s, pair, 3):
                        t, r, _ = done
                        sp.wait_ge(y_read, t + 1)
                        sp.dma_start(results_dram[bass.ds(t * P, P), :], result[r][:, :]).then_inc(stored[r], 16)

                load(tile_at(0, 0, 0))
                for e in range(EXPERTS):
                    sp.dma_start(down[:, e, :, :], a["L1_ffn_exp_W2"][e].rearrange("(m p) n -> p m n", p=P)
                                 ).then_inc(down_in, 16)
                sp.dma_start(bias[:, :].rearrange("p (e m) -> p e m", m=HM),
                             a["L1_ffn_exp_b1"].rearrange("e p m -> p e m")).then_inc(bias_in, 16)
                for_steps(sp, body)
                for r in range(2):
                    sp.wait_ge(stored[r], 16 * ((TILES + 1 - r) // 2))

            @block.tensor
            def _(pe):
                def body(s, pair):
                    if at := tile_at(s, pair, 0):
                        t, r, before = at
                        pe.wait_ge(rows_in[r], (before + 1) * 16)
                        wait_for(pe, x_read, t)
                        for k in range(DK):
                            ins = pe.transpose(c.psum[:, X_BANK, k * P:(k + 1) * P], rows[r][:, k * P:(k + 1) * P],
                                               c.ident[:, :])
                        ins.then_inc(x_turned, 1)
                    if at := tile_at(s, pair, 1):
                        t, r, _ = at
                        e = weights_of(pe, t)
                        pe.wait_ge(x_read, t + 1)
                        for h in range(HALVES):
                            wait_for(pe, raw_read, (t - 1) * HALVES + h + 1)
                            for k in range(DK):
                                ins = pe.matmul(c.psum[:, UP_BANK + h, :], rows_T[r][:, k, :],
                                                up[:, bass.ds(e, 1), k, h * BANK:(h + 1) * BANK].rearrange("p o n -> p (o n)"),
                                                start=k == 0, stop=k == DK - 1)
                            ins.then_inc(up_full, 1)
                    if at := tile_at(s, pair, 2):
                        t, r, _ = at
                        for h in range(HALVES):
                            pe.wait_ge(raw_read, t * HALVES + h + 1)
                            wait_for(pe, gelu_done, (t - 1) * HM + (h + 1) * PER)
                            for m in range(PER):
                                ins = pe.transpose(c.psum[:, TURN_BANK + h, m * P:(m + 1) * P],
                                                   raw[r][:, (h * PER + m) * P:(h * PER + m + 1) * P], c.ident[:, :])
                            ins.then_inc(h_turned, 1)
                    if at := tile_at(s, pair, 3):
                        t, r, _ = at
                        e = weights_of(pe, t)
                        wait_for(pe, y_read, t - 1)
                        pe.wait_ge(gelu_done, (t + 1) * HM)
                        for m in range(HM):
                            ins = pe.matmul(c.psum[:, DOWN_BANK + r, 0:D], hidden[r][:, m, :],
                                            down[:, bass.ds(e, 1), m, :].rearrange("p o n -> p (o n)"),
                                            start=m == 0, stop=m == HM - 1)
                        ins.then_inc(y_full, 1)

                pe.wait_ge(up_in, 16 * EXPERTS)
                for s in range(3):
                    body(s, 0)
                pe.wait_ge(down_in, 16 * EXPERTS)
                for s in range(3, FIRST):
                    body(s, 0)
                with pe.Fori(0, PAIRS) as pair:
                    for r in range(2):
                        body(FIRST + r, pair)
                for s in range(FIRST + 2 * PAIRS, TILES + 3):
                    body(s, 0)

            @block.vector
            def _(v):
                def body(s, pair):
                    if at := tile_at(s, pair, 0):
                        t, r, _ = at
                        v.wait_ge(x_turned, t + 1)
                        wait_for(v, up_full, (t - 1) * HALVES)
                        v.tensor_copy(rows_T[r][:, :, :].rearrange("p k n -> p (k n)"),
                                      c.psum[:, X_BANK, 0:D]).then_inc(x_read, 1)
                    if at := tile_at(s, pair, 1):
                        t, r, _ = at
                        wait_for(v, h_turned, (t - 1) * HALVES)
                        for h in range(HALVES):
                            v.wait_ge(up_full, t * HALVES + h + 1)
                            v.tensor_copy(raw[r][:, h * BANK:(h + 1) * BANK], c.psum[:, UP_BANK + h, :]).then_inc(raw_read, 1)
                    if at := tile_at(s, pair, 3):
                        t, r, before = at
                        v.wait_ge(y_full, t + 1)
                        wait_for(v, stored[r], before * 16)
                        v.tensor_copy(result[r][:, :], c.psum[:, DOWN_BANK + r, 0:D]).then_inc(y_read, 1)

                for_steps(v, body)

            @block.scalar
            def _(act):
                def body(s, pair):
                    if at := tile_at(s, pair, 2):
                        t, r, _ = at
                        e = weights_of(act, t)
                        wait_for(act, y_full, t - 1)
                        for m in range(HM):
                            if m % PER == 0:
                                act.wait_ge(h_turned, t * HALVES + m // PER + 1)
                            act.activation(hidden[r][:, m, :], c.psum[:, TURN_BANK + m // PER, m % PER * P:(m % PER + 1) * P],
                                           ACT.Gelu, bias=bias[:, bass.ds(e * HM + m, 1)]).then_inc(gelu_done, 1)

                act.wait_ge(bias_in, 16)
                for_steps(act, body)


@staged
def stage_gather(c, share, place, results_dram):
    nc = c.nc
    with nc.sbuf_tensor("gathered", [P, NT, 2, D], F32) as gathered:
        got, added = [c.sem(f"gather_got{t}") for t in range(NT)], c.sem("gather_added")
        with nc.Block() as block:
            @block.gpsimd
            def _(pool):
                for t in range(NT):
                    for x in range(2):
                        pool.indirect_dma_start(gathered[:, t, x, :], None, results_dram[:, :],
                                                bass.IndirectOffsetOnAxis(ap=place[:, x, t:t + 1], axis=0)).then_inc(got[t], 16)

            @block.vector
            def _(v):
                for t in range(NT):
                    v.wait_ge(got[t], 32)
                    for x in range(2):
                        v.scalar_tensor_tensor(c.x_tok[:, t, :], gathered[:, t, x, :], share[:, t, x:x + 1],
                                               c.x_tok[:, t, :], ALU.mult, ALU.add).then_inc(added, 1)
                        v.wait_ge(added, 2 * t + x + 1)


@staged
def stage_gate(c, share, place, expert_of, block_in, h_tok, rows_dram, rows_filled):
    nc, a = c.nc, c.args
    E = EXPERTS
    with ExitStack() as ctx:
        def sb(n, shape, dt=F32):
            return ctx.enter_context(nc.sbuf_tensor(f"gate_{n}", shape, dt))

        def sem(n):
            return c.sem(f"gate_{n}")

        weight_T = sb("weight_T", [E, T])
        gate_w, gate_b, down_b = sb("w", [P, DK, E]), sb("b", [P, E]), sb("down_b", [E, D])
        logits, top = sb("logits", [P, NT, E]), sb("top", [P, NT, 8])
        at, at_f = sb("at", [P, NT, 8], U32), sb("at_f", [P, NT, 8])
        number = sb("number", [P, TILES])
        less = sb("less", [P, E, E])
        tri, ones = sb("tri", [P, P], BF16), sb("ones", [P, P], BF16)
        weight = sb("weight", [P, NT, E])
        both = sb("both", [P, NT, E], BF16)
        earlier = sb("earlier", [P, NT + 1, E], BF16)
        over = sb("over", [P, E, NT])
        count, tiles_of, last, first = sb("count", [P, E]), sb("tiles_of", [P, E]), sb("last", [P, E]), sb("first", [P, E])
        part, rank_at, picked = sb("part", [P, E, E]), sb("rank_at", [P, NT, E]), sb("picked", [P, NT, E])
        place_f, past, owner = sb("place_f", [P, 2, NT]), sb("past", [P, TILES, E]), sb("owner", [P, TILES])
        lead, ratio = sb("lead", [P, NT]), sb("ratio", [P, NT])
        pick = sb("pick", [P, 2, NT, E])
        s_in, s_full, s_dve, s_exp = sem("in"), sem("full"), sem("dve"), sem("exp")
        s_number, s_turned, s_out, s_bias = sem("number"), sem("turned"), sem("out"), sem("bias")
        s_bias_full, s_twice = sem("bias_full"), sem("twice")
        s_ranked, s_placed, s_sent = sem("ranked"), sem("placed"), sem("sent")
        LOGIT_BANK, RANK_BANK = 7, 3
        MASKS_DONE = 3 * NT + 10
        with nc.Block() as block:
            @block.sync
            def _(sp):
                sp.dma_start(gate_w[:, :, :], a["L1_ffn_gate_W"].rearrange("(k p) e -> p k e", p=P)).then_inc(s_in, 16)
                sp.dma_start(gate_b[:, :], a["L1_ffn_gate_b"].partition_broadcast(P)).then_inc(s_in, 16)
                sp.dma_start(down_b[:, :], a["L1_ffn_exp_b2"]).then_inc(s_in, 16)
                sp.wait_ge(s_in, 48)

            @block.gpsimd
            def _(pool):
                pool.iota(number[:, :], [[1, TILES]], base=0, channel_multiplier=0,
                          allow_small_or_imprecise_dtypes=True).then_inc(s_number, 1)
                pool.iota(less[:, :, :], [[1, E], [-1, E]], base=0, channel_multiplier=0,
                          allow_small_or_imprecise_dtypes=True).then_inc(s_number, 1)
                pool.memset(ones[:, :], 1.0).then_inc(s_number, 1)
                pool.wait_ge(s_number, 3)
                pool.affine_select(out=tri[:, :], in_=ones[:, :], compare_op=ALU.is_gt, fill=0.0, base=0,
                                   pattern=[[1, P]], channel_multiplier=-1).then_inc(s_number, 1)
                for t in range(NT):
                    pool.tensor_tensor(c.x_tok[:, t, :], c.x_tok[:, t, :], block_in[:, t, :], ALU.add).then_inc(s_twice, 1)
                pool.wait_ge(s_placed, 1)
                pool.wait_ge(rows_filled, 16 * 3)
                for t in range(NT):
                    for x in range(2):
                        pool.indirect_dma_start(rows_dram[:, :], bass.IndirectOffsetOnAxis(ap=place[:, x, t:t + 1], axis=0),
                                                h_tok[:, t, :], None).then_inc(s_sent, 16)
                pool.wait_ge(s_sent, 16 * 2 * NT)

            @block.tensor
            def _(pe):
                pe.wait_ge(s_in, 48)
                for t in range(NT):
                    for k in range(DK):
                        ins = pe.matmul(c.psum[:, LOGIT_BANK, t * E:(t + 1) * E], c.xT[:, k, t * P:(t + 1) * P],
                                        gate_w[:, k, :], start=k == 0, stop=k == DK - 1)
                ins.then_inc(s_full, 1)
                pe.wait_ge(s_number, 4)
                pe.wait_ge(s_dve, MASKS_DONE)
                flat = both[:, :, :].rearrange("p t e -> p (t e)")
                pe.matmul(c.psum[:, RANK_BANK, 0:NT * E], tri[:, :], flat, start=True, stop=False)
                pe.matmul(c.psum[:, RANK_BANK, 0:NT * E], ones[:, :],
                          earlier[:, 0:NT, :].rearrange("p t e -> p (t e)"), start=False, stop=True)
                pe.matmul(c.psum[:, RANK_BANK, NT * E:(NT + 1) * E], ones[:, :], earlier[:, NT, :],
                          start=True, stop=True).then_inc(s_ranked, 1)
                pe.wait_ge(s_placed, 2)
                for t in range(NT):
                    ins = pe.transpose(c.psum[0:E, t // QT, t % QT * P:(t % QT + 1) * P], weight[:, t, :], c.ident[:, :])
                    ins.then_inc(s_turned, 1)
                for t in range(NT):
                    pe.wait_ge(s_out, t // QT + 1)
                    wait_for(pe, s_bias, t - 3)
                    pe.matmul(c.psum[:, 4 + t % 4, 0:D], weight_T[:, t * P:(t + 1) * P], down_b[:, :],
                              start=True, stop=True).then_inc(s_bias_full, 1)

            @block.scalar
            def _(act):
                act.wait_ge(s_dve, 2 * NT + 3)
                act.activation(ratio[:, :], lead[:, :], ACT.Exp).then_inc(s_exp, 1)
                for q in range(NT // QT):
                    act.wait_ge(s_turned, QT * (q + 1))
                    act.activation(weight_T[:, q * SEQ:(q + 1) * SEQ], c.psum[0:E, q, :], ACT.Copy).then_inc(s_out, 1)

            @block.vector
            def _(v):
                done = 0

                def step(ins, wait=True):
                    nonlocal done
                    ins.then_inc(s_dve, 1)
                    done += 1
                    if wait:
                        v.wait_ge(s_dve, done)

                v.wait_ge(s_in, 48)
                v.wait_ge(s_full, 1)
                step(v.tensor_tensor(logits[:, :, :], c.psum[:, LOGIT_BANK, 0:NT * E].rearrange("p (t e) -> p t e", e=E),
                                     gate_b[:, :].unsqueeze(1).to_broadcast([P, NT, E]), ALU.add))
                for t in range(NT):
                    step(v.max(top[:, t, :], logits[:, t, :]), wait=t == NT - 1)
                for t in range(NT):
                    step(v.max_index(at[:, t, :], top[:, t, :], logits[:, t, :]), wait=t == NT - 1)
                step(v.tensor_copy(at_f[:, :, :], at[:, :, :]))
                step(v.tensor_tensor(lead[:, :], top[:, :, 1], top[:, :, 0], ALU.subtract))
                v.wait_ge(s_exp, 1)
                step(v.tensor_scalar(lead[:, :], ratio[:, :], 1.0, None, ALU.add))
                step(v.reciprocal(share[:, :, 0], lead[:, :]))
                step(v.tensor_tensor(share[:, :, 1], ratio[:, :], share[:, :, 0], ALU.mult))
                v.wait_ge(s_number, 4)
                for x in range(2):
                    numbers = number[:, 0:E].unsqueeze(1).to_broadcast([P, NT, E])
                    step(v.tensor_tensor(pick[:, x, :, :], numbers, at_f[:, :, x:x + 1].to_broadcast([P, NT, E]), ALU.is_equal),
                         wait=x == 1)
                step(v.tensor_tensor(both[:, :, :], pick[:, 0, :, :], pick[:, 1, :, :], ALU.add), wait=False)
                step(v.tensor_scalar(earlier[:, 0, :], number[:, 0:E], 0.0, None, ALU.mult))
                for t in range(NT):
                    step(v.tensor_tensor(earlier[:, t + 1, :], earlier[:, t, :], both[:, t, :], ALU.add))
                assert done == MASKS_DONE, done
                v.wait_ge(s_ranked, 1)
                step(v.tensor_scalar(count[:, :], c.psum[:, RANK_BANK, NT * E:(NT + 1) * E], 1.0 / P, None, ALU.mult))
                step(v.tensor_tensor(over[:, :, :], count[:, :].unsqueeze(2).to_broadcast([P, E, NT]),
                                     number[:, 0:NT].unsqueeze(1).to_broadcast([P, E, NT]), ALU.is_gt))
                step(v.tensor_reduce(tiles_of[:, :], over[:, :, :], axis=AX_X, op=ALU.add))
                step(v.scalar_tensor_tensor(part[:, :, :], less[:, :, :], 0.0,
                                            tiles_of[:, :].unsqueeze(1).to_broadcast([P, E, E]), ALU.is_ge, ALU.mult))
                step(v.tensor_reduce(last[:, :], part[:, :, :], axis=AX_X, op=ALU.add))
                step(v.tensor_tensor(first[:, :], last[:, :], tiles_of[:, :], ALU.subtract))
                step(v.scalar_tensor_tensor(rank_at[:, :, :], first[:, :].unsqueeze(1).to_broadcast([P, NT, E]), float(P),
                                            c.psum[:, RANK_BANK, 0:NT * E].rearrange("p (t e) -> p t e", e=E),
                                            ALU.mult, ALU.add))
                for x in range(2):
                    step(v.tensor_tensor(picked[:, :, :], pick[:, x, :, :], rank_at[:, :, :], ALU.mult))
                    step(v.tensor_reduce(place_f[:, x, :], picked[:, :, :], axis=AX_X, op=ALU.add))
                v.tensor_copy(place[:, :, :], place_f[:, :, :]).then_inc(s_placed, 1)
                step(v.tensor_tensor(past[:, :, :], last[:, :].unsqueeze(1).to_broadcast([P, TILES, E]),
                                     number[:, :].unsqueeze(2).to_broadcast([P, TILES, E]), ALU.is_le))
                step(v.tensor_reduce(owner[:, :], past[:, :, :], axis=AX_X, op=ALU.add))
                step(v.tensor_scalar(expert_of[:, :], owner[:, :], float(E - 1), None, ALU.min), wait=False)
                for x in range(2):
                    step(v.tensor_tensor(pick[:, x, :, :], pick[:, x, :, :], share[:, :, x:x + 1].to_broadcast([P, NT, E]),
                                         ALU.mult), wait=x == 1)
                v.tensor_tensor(weight[:, :, :], pick[:, 0, :, :], pick[:, 1, :, :], ALU.add).then_inc(s_placed, 1)
                for t in range(NT):
                    v.wait_ge(s_bias_full, t + 1)
                    v.wait_ge(s_twice, t + 1)
                    v.tensor_tensor(c.x_tok[:, t, :], c.psum[:, 4 + t % 4, 0:D], c.x_tok[:, t, :], ALU.add).then_inc(s_bias, 1)


def build(nc, args, out):
    with ExitStack() as ctx:
        c = Core(nc, ctx, args, out)
        a = args
        rows_dram = c.dram("expert_rows", (TILES * P, D))
        rows_filled = ctx.enter_context(nc.semaphore("rows_filled"))
        stage_load(c, rows_dram, rows_filled)
        stage_norm(c, "x0", c.x_tok, NT, dstT=c.xT)
        q_dram = c.dram("q_parts", (2, BATCH * D, SEQ))
        k_self = c.dram("k_parts_self", (2, BATCH * D, SEQ))
        k_cross = c.dram("k_parts_cross", (2, BATCH * D, CTX_SEQ))
        v_self = c.dram("v_self", (NG, P, SEQ // P, GD))
        v_cross = c.dram("v_cross", (NG, P, CTX_SEQ // P, GD))

        def self_attention(name, wq, wk, wv, bq, bk, bv, wo, bo):
            stage_project(c, f"{name}_qkv", c.xT, P, T, split=((wq, bq, q_dram), (wk, bk, k_self)),
                          values=(wv, v_self))
            attend(name, k_self, v_self, bv, SEQ, True, wo, bo)

        def cross_attention(name, wq, wk, wv, bq, bk, bv, wo, bo):
            stage_project(c, f"{name}_q", c.xT, P, T, split=((wq, bq, q_dram),))
            with nc.sbuf_tensor(f"{name}_ctx", [CP, 2, CT], F32) as ctx_T:
                stage_fetch(c, f"{name}_ctx_in", [(ctx_T[:, k, :], a["ctxT"][k * CP:(k + 1) * CP, :]) for k in range(2)])
                stage_project(c, f"{name}_kv", ctx_T, CP, CT, split=((wk, bk, k_cross),), values=(wv, v_cross))
            attend(name, k_cross, v_cross, bv, CTX_SEQ, False, wo, bo)

        def attend(name, k_dram, v_dram, bv, keys, causal, wo, bo):
            with nc.sbuf_tensor(f"{name}_o_tok", [P, NT, D], F32) as o_tok:
                stage_attention(c, name, q_dram, k_dram, v_dram, bv, o_tok, keys, causal)
                stage_output(c, f"{name}_out", o_tok, wo, bo)

        w, b = a["L0_attn_w_attn"], a["L0_attn_b_attn"]
        self_attention("a0", w[:, 0:D], w[:, D:2 * D], w[:, 2 * D:], b[0:D], b[D:2 * D], b[2 * D:],
                       a["L0_attn_w_proj"], a["L0_attn_b_proj"])
        stage_norm(c, "n0", c.x_tok, NT, layernorm=True, dstT=c.xT)
        cross_attention("c0", *(a[f"L0_xattn_{x}"] for x in ("Wq", "Wk", "Wv", "bq", "bk", "bv", "Wo", "bo")))
        soft_moe(c)
        stage_norm(c, "n2", c.x_tok, NT, layernorm=True, dstT=c.xT)
        w = a["L1_attn_w_qkv"]
        self_attention("a1", w[:, 0:D], w[:, D:2 * D], w[:, 2 * D:], None, None, None, a["L1_attn_w_o"], None)
        stage_norm(c, "n3", c.x_tok, NT, layernorm=True, dstT=c.xT)
        cross_attention("c1", *(a[f"L1_xattn_{x}"] for x in ("wq", "wk", "wv", "bq", "bk", "bv", "wo", "bo")))
        stage_norm(c, "n4", c.x_tok, NT, layernorm=True, affine=(a["L1_ffn_ln1_g"], a["L1_ffn_ln1_b"]), dstT=c.xT)
        block_in = c.keep("block_in", [P, NT, D])
        stage_fetch(c, "block_in", [(block_in[:, :, :], c.x_tok[:, :, :])])
        self_attention("a2", *(a[f"L1_ffn_{x}"] for x in ("Wq", "Wk", "Wv", "bq", "bk", "bv", "Wp", "bp")))
        token_moe(c, block_in, rows_dram, rows_filled)
        stage_norm(c, "n6", c.x_tok, NT, layernorm=True, out=out)


TRANSPOSED = ("L0_attn_w_attn", "L0_attn_w_proj", "L0_xattn_Wq", "L0_xattn_Wk", "L0_xattn_Wv", "L0_xattn_Wo")


def kernel(**inputs):
    import concourse.bacc as bacc
    from concourse.bass_utils import run_bass_kernel_spmd

    nc = bacc.Bacc("TRN2", target_bir_lowering=False, num_devices=1)
    arrays, args = {}, {}
    for name, value in inputs.items():
        a = np.asarray(value)
        if name in TRANSPOSED:
            a = a.T
        if name == "ctx_768":
            name, a = "ctxT", a.reshape(CT, CTX_D).T
        if name in ("L0_ffn_b1", "L1_ffn_exp_b1"):
            a = a.reshape(EXPERTS, HM, P).transpose(0, 2, 1)
        a = np.ascontiguousarray(a)
        arrays[f"in_{name}"] = a
        args[name] = nc.dram_tensor(f"in_{name}", a.shape, mybir.dt.from_np(a.dtype), kind="ExternalInput").ap()
    out = nc.dram_tensor("out", (BATCH, SEQ, D), F32, kind="ExternalOutput").ap()
    build(nc, args, out)
    r = run_bass_kernel_spmd(nc, [arrays], core_ids=[0])
    return r.results[0]["out"]
```

```python
from contextlib import ExitStack, contextmanager

import concourse.bass as bass
from concourse import mybir
import numpy as np

F32 = mybir.dt.float32
F32R = mybir.dt.float32r
BF16 = mybir.dt.bfloat16
U32 = mybir.dt.uint32
ALU = mybir.AluOpType
ACT = mybir.ActivationFunctionType
AX_X = mybir.AxisListType.X

P = 128
BATCH, SEQ, D = 4, 512, 256
T = BATCH * SEQ
NT = T // P
QT = SEQ // P
DK = D // P
CTX_SEQ, CTX_D = 1024, 192
CP = CTX_D // 2
CT = BATCH * CTX_SEQ
HEADS, HD = 16, 16
GH = 4
GROUPS = HEADS // GH
GD = GH * HD
NG = BATCH * GROUPS
EXPERTS, SLOTS, HID = 8, 128, 1024
HM = HID // P
TILES = 2 * T // P + EXPERTS - 1
BANK = 512
NEG_BIG = -1.0e30
LN_EPS = 1e-5
SHIFT_ROW = 96
SHIFT_END = SHIFT_ROW + 3
STACK = P


def wait_for(eng, sem, count):
    if isinstance(count, int) and count <= 0:
        return
    eng.wait_ge(sem, count)


class Core:

    def __init__(self, nc, ctx, args, out):
        self.nc, self.ctx, self.args, self.out = nc, ctx, args, out
        self.slot_stored = [ctx.enter_context(nc.semaphore(f"slot_stored{i}")) for i in range(8)]
        self.slot_count = [0] * 8
        self.psum = ctx.enter_context(nc.psum_tensor("psum", [P, 8, BANK], F32))

    def sem(self, name):
        sem = self.stage_ctx.enter_context(self.nc.semaphore(name))
        self.stage_sems.append(sem)
        return sem

    @contextmanager
    def stage(self):
        self.stage_sems = []
        with ExitStack() as self.stage_ctx:
            yield
            with self.nc.Block() as block:
                @block.gpsimd
                def _(pool):
                    for sem in self.stage_sems:
                        pool.sem_clear(sem)

    def keep(self, name, shape, dt=F32):
        return self.ctx.enter_context(self.nc.sbuf_tensor(name, shape, dt))

    def dram(self, name, shape, dt=F32):
        return self.nc.dram_tensor(name, shape, dt, kind="Internal").ap()


def staged(build_stage):
    def run(c, *args, **named):
        with c.stage():
            build_stage(c, *args, **named)
    return run


@staged
def stage_load(c):
    nc = c.nc
    c.x_tok = c.keep("x_tok", [P, NT, D])
    c.xT = c.keep("xT", [P, DK, T])
    c.rows = c.keep("rows", [P, NT, D])
    c.wo, c.bo = c.keep("wo", [P, DK, D]), c.keep("bo", [P, D])
    c.ident = c.keep("ident", [P, P])
    c.ident_bf = c.keep("ident_bf", [P, P], BF16)
    c.mask_qk = c.keep("mask_qk", [P, P], BF16)
    c.mask_kq = c.keep("mask_kq", [P, P], BF16)
    c.eps = c.keep("eps", [P, 1])
    c.early_shift = [c.keep(f"early_shift{i}", [P, GH * QT, 3], BF16) for i in range(EARLY)]
    loaded, filled, made = c.sem("x_loaded"), c.sem("const_filled"), c.sem("const_made")
    with nc.Block() as block:
        @block.sync
        def _(sp):
            sp.dma_start(c.x_tok[:, :, :], c.args["x"].rearrange("b (q p) d -> p (b q) d", p=P)).then_inc(loaded, 16)
            sp.wait_ge(loaded, 16)

        @block.gpsimd
        def _(pool):
            for t in (c.ident, c.ident_bf, c.mask_qk, c.mask_kq):
                pool.memset(t[:, :], 0.0).then_inc(filled, 1)
            pool.memset(c.eps[:, :], LN_EPS).then_inc(made, 1)
            pool.wait_ge(filled, 4)
            for t in (c.ident, c.ident_bf):
                pool.affine_select(out=t[:, :], in_=t[:, :], compare_op=ALU.not_equal, fill=1.0, base=0,
                                   pattern=[[-1, P]], channel_multiplier=1).then_inc(made, 1)
            pool.affine_select(out=c.mask_qk[:, :], in_=c.mask_qk[:, :], compare_op=ALU.is_ge, fill=NEG_BIG,
                               base=0, pattern=[[-1, P]], channel_multiplier=1).then_inc(made, 1)
            pool.affine_select(out=c.mask_kq[:, :], in_=c.mask_kq[:, :], compare_op=ALU.is_ge, fill=NEG_BIG,
                               base=0, pattern=[[1, P]], channel_multiplier=-1).then_inc(made, 1)
            pool.wait_ge(made, 5)


@staged
def stage_fetch(c, name, pairs):
    loaded = c.sem(name)
    with c.nc.Block() as block:
        @block.sync
        def _(sp):
            for dst, src in pairs:
                sp.dma_start(dst, src).then_inc(loaded, 16)
            sp.wait_ge(loaded, 16 * len(pairs))


@staged
def stage_norm(c, name, src, tiles, layernorm=False, affine=None, rms=None, keep_tok=None, dstT=None, out=None):
    nc = c.nc
    with ExitStack() as ctx:
        def sb(n, shape, dt=F32):
            return ctx.enter_context(nc.sbuf_tensor(f"{name}_{n}", shape, dt))

        stats = sb("stats", [P, tiles, 6])
        mean_var = sb("mean_var", [P, 2, tiles, 2])
        root = sb("root", [P, 2, tiles])
        rstd = sb("rstd", [P, 2, tiles])
        squares = sb("squares", [P, 2, D])
        gain = sb("gain", [P, D])
        bias = sb("bias", [P, D])
        if keep_tok is None and (affine or rms):
            keep_tok = sb("rows", [P, tiles, D])
        coef_in, dve, rooted = c.sem(f"{name}_coef_in"), c.sem(f"{name}_dve"), c.sem(f"{name}_rooted")
        rows_ready, turned, evacuated = c.sem(f"{name}_rows_ready"), c.sem(f"{name}_turned"), c.sem(f"{name}_evacuated")
        stored = c.sem(f"{name}_stored")
        passes = int(layernorm) + int(affine is not None)
        rows = keep_tok if (affine or rms) else src
        coefs = list(affine or ()) + ([rms] if rms else [])

        with nc.Block() as block:
            @block.sync
            def _(sp):
                for tile, ap in zip((gain, bias), coefs):
                    sp.dma_start(tile[:, :], ap.partition_broadcast(P)).then_inc(coef_in, 16)
                if coefs:
                    sp.wait_ge(coef_in, 16 * len(coefs))
                if out is not None:
                    for b in range(tiles // QT):
                        sp.wait_ge(rows_ready, QT * (b + 1))
                        sp.dma_start(out[b].rearrange("(q p) d -> p q d", p=P),
                                     rows[:, b * QT:(b + 1) * QT, :]).then_inc(stored, 16)
                    sp.wait_ge(stored, 16 * (tiles // QT))

            @block.vector
            def _(v):
                done = 0

                def step(ins, wait=True):
                    nonlocal done
                    ins.then_inc(dve, 1)
                    done += 1
                    if wait:
                        v.wait_ge(dve, done)

                def statistics(n, which):
                    for t in range(tiles):
                        step(v.bn_stats(stats[:, t, :], which[:, t, :]), wait=t == tiles - 1)
                    for t in range(tiles):
                        step(v.bn_aggr(mean_var[:, n, t, :], stats[:, t, :]), wait=t == tiles - 1)
                    v.wait_ge(rooted, n + 1)
                    step(v.reciprocal(rstd[:, n, :], root[:, n, :]))

                n = 0
                if layernorm:
                    statistics(n, src)
                    for t in range(tiles):
                        ins = v.tensor_scalar(src[:, t, :], src[:, t, :], mean_var[:, n, t, 0:1], rstd[:, n, t:t + 1],
                                              ALU.subtract, ALU.mult)
                        if affine or rms:
                            step(ins, wait=t == tiles - 1)
                        else:
                            ins.then_inc(rows_ready, 1)
                    n += 1
                if affine:
                    statistics(n, src)
                    v.wait_ge(coef_in, 32)
                    for t in range(tiles):
                        step(v.tensor_scalar(rows[:, t, :], src[:, t, :], mean_var[:, n, t, 0:1], rstd[:, n, t:t + 1],
                                             ALU.subtract, ALU.mult), wait=t == tiles - 1)
                    for t in range(tiles):
                        step(v.tensor_tensor(rows[:, t, :], rows[:, t, :], gain[:, :], ALU.mult), wait=t == tiles - 1)
                    for t in range(tiles):
                        v.tensor_tensor(rows[:, t, :], rows[:, t, :], bias[:, :], ALU.add).then_inc(rows_ready, 1)
                if rms:
                    v.wait_ge(rooted, n + 1)
                    step(v.tensor_scalar(root[:, n, :], root[:, n, :], 1e-12, None, ALU.max))
                    step(v.reciprocal(rstd[:, n, :], root[:, n, :]))
                    step(v.tensor_scalar(rstd[:, n, :], rstd[:, n, :], float(D) ** 0.5, None, ALU.mult))
                    v.wait_ge(coef_in, 16)
                    for t in range(tiles):
                        v.scalar_tensor_tensor(rows[:, t, :], src[:, t, :], rstd[:, n, t:t + 1], gain[:, :],
                                               ALU.mult, ALU.mult).then_inc(rows_ready, 1)

            if dstT is not None:
                @block.tensor
                def _(pe):
                    if not (layernorm or affine or rms):
                        pass
                    else:
                        pe.wait_ge(rows_ready, tiles)
                    for t in range(0, tiles, QT):
                        for k in range(DK):
                            u = t // QT * DK + k
                            wait_for(pe, evacuated, u - 7)
                            for q in range(QT):
                                ins = pe.transpose(c.psum[:, u % 8, q * P:(q + 1) * P],
                                                   rows[:, t + q, k * P:(k + 1) * P], c.ident[:, :])
                            ins.then_inc(turned, 1)

            @block.scalar
            def _(act):
                squared = 0
                n = 0
                for _ in range(passes):
                    act.wait_ge(dve, 2 * tiles + n * (3 * tiles + 1))
                    act.activation(root[:, n, :], mean_var[:, n, :, 1], ACT.Sqrt, bias=c.eps[:, :]).then_inc(rooted, 1)
                    n += 1
                if rms:
                    if layernorm:
                        act.wait_ge(dve, 3 * tiles + 1)
                    for t in range(tiles):
                        if t >= 2:
                            act.wait_ge(evacuated, t - 1)
                        act.activation(squares[:, t % 2, :], src[:, t, :], ACT.Square,
                                       accum_out=root[:, n, t:t + 1]).then_inc(evacuated, 1)
                    act.wait_ge(evacuated, tiles)
                    act.activation(rstd[:, n, :], root[:, n, :], ACT.Sqrt).then_inc(evacuated, 1)
                    act.wait_ge(evacuated, tiles + 1)
                    act.activation(root[:, n, :], rstd[:, n, :], ACT.Copy).then_inc(rooted, 1)
                    squared = tiles + 1
                if dstT is not None:
                    for u in range(tiles // QT * DK):
                        act.wait_ge(turned, u + 1)
                        act.activation(dstT[:, u % DK, u // DK * SEQ:u // DK * SEQ + SEQ], c.psum[:, u % 8, :],
                                       ACT.Copy).then_inc(evacuated, 1)
                    act.wait_ge(evacuated, squared + tiles // QT * DK)


EARLY = 2
SHIFT_STEPS = 6


def max_units(keys, causal):
    return [(j, qt, k0, (qt + 1) * P if causal else BANK)
            for j in range(GH) for qt in range(QT) for k0 in range(0, keys, BANK)]


def load_stacks(sp, q, k, n, q_dram, k_dram, loaded):
    for blk, (qp, kp) in enumerate(((0, 0), (0, 1), (1, 0), (1, 1))):
        at = slice(HD * blk, HD * (blk + 1))
        sp.dma_start(q[at, :, :].bitcast(F32),
                     q_dram[qp, bass.ds(n * GD, GD), :].rearrange("(j d) t -> d j t", d=HD)).then_inc(loaded, 16)
        sp.dma_start(k[at, :, :].bitcast(F32),
                     k_dram[kp, bass.ds(n * GD, GD), :].rearrange("(j d) t -> d j t", d=HD)).then_inc(loaded, 16)


def shift_step(v, s_shift, at, k, max_parts, row_max, rest, shift):
    if k:
        v.wait_ge(s_shift, at + k)
    if k == 0:
        ins = v.tensor_reduce(row_max[:, :], max_parts[:, :].rearrange("p (u k) -> p u k", u=GH * QT),
                              axis=AX_X, op=ALU.max)
    elif k == 1:
        ins = v.tensor_scalar(shift[:, :, 0], row_max[:, :], -1.0, None, ALU.mult)
    elif k == 2:
        ins = v.scalar_tensor_tensor(rest[:, 0, :], row_max[:, :], -1.0, shift[:, :, 0], ALU.mult, ALU.subtract)
    elif k == 3:
        ins = v.tensor_copy(shift[:, :, 1], rest[:, 0, :])
    elif k == 4:
        ins = v.tensor_tensor(rest[:, 1, :], rest[:, 0, :], shift[:, :, 1], ALU.subtract)
    else:
        ins = v.tensor_copy(shift[:, :, 2], rest[:, 1, :])
    ins.then_inc(s_shift, 1)


@staged
def stage_between(c, name, front=None, layernorm=False, affine=None, rms=None, copy_to=None, rows_to=None,
                  project=None, context=None, early=None, out=None, prefetch=()):
    nc, a = c.nc, c.args
    with ExitStack() as ctx:
        def sb(n, shape, dt=F32):
            return ctx.enter_context(nc.sbuf_tensor(f"{name}_{n}", shape, dt))

        def sem(n):
            return c.sem(f"{name}_{n}")

        CHUNKS = NT // QT
        rows = rows_to if (affine or rms) else c.x_tok
        passes = (["plain"] if layernorm else []) + (["affine"] if affine else [])
        normed = bool(passes or rms)
        TURN_BANK, FRONT_BANK, JOB_BANK = 0, 2, 4
        HELD = 4 if front and front[0] == "combine" else 8
        if front and front[0] == "output":
            _, o_tok, biased_output = front
            oT = sb("oT", [P, 2, DK, P])
        if front and front[0] == "gather":
            _, share, place, results_dram = front
            gathered = sb("gathered", [P, NT, 2, D])
            got = [sem(f"got{t}") for t in range(NT)]
        if normed:
            stats, mean_var = sb("stats", [P, NT, 6]), sb("mean_var", [P, 2, NT, 2])
            root, rstd = sb("root", [P, 2, NT]), sb("rstd", [P, 2, NT])
        coefs = list(affine or ()) + ([rms] if rms else [])
        coef = [sb(f"coef{i}", [P, D]) for i in range(len(coefs))]
        squares = sb("squares", [P, 2, D]) if rms else None

        jobs, w_loads, no_bias = [], [], []
        jobs_before = [0] * (CHUNKS + 1)

        def add_jobs(n, what, src, rows_of, tiles, chunk, per):
            split, values = what
            for i, (w, b, dst) in enumerate(split):
                for m in range(DK):
                    jobs.append(("split", src, rows_of, tiles[i][0], tiles[i][1], dst, m, chunk * BANK, per))
            if values:
                for h in range(2):
                    jobs.append(("value", src, rows_of, tiles[-1][0], None, values[1], h, chunk * BANK, per))

        def weight_tiles(n, what, rows_of):
            split, values = what
            tiles = []
            for i, (w, b, _) in enumerate(split):
                tiles.append((sb(f"{n}_w{i}", [rows_of, 2, D]), sb(f"{n}_b{i}", [P, DK])))
                w_loads.append((tiles[-1][0][:, :, :], w.rearrange("(k p) n -> p k n", p=rows_of), False))
                if b is not None:
                    w_loads.append((tiles[-1][1][:, :], b.rearrange("(k p) -> p k", p=P), True))
                else:
                    no_bias.append(tiles[-1][1])
            if values:
                tiles.append((sb(f"{n}_wv", [rows_of, 2, D]), None))
                w_loads.append((tiles[-1][0][:, :, :], values[0].rearrange("(k p) n -> p k n", p=rows_of), False))
            return tiles

        if project:
            own_tiles = weight_tiles("own", project, P)
            w_own = len(w_loads)
            if context:
                ctx_T = sb("ctx_T", [CP, 2, CT])
                context_tiles = weight_tiles("context", context, CP)
                for k in range(2):
                    w_loads.append((ctx_T[:, k, :], a["ctxT"][k * CP:(k + 1) * CP, :], False))
            for n in range(CHUNKS):
                add_jobs(n, project, c.xT, P, own_tiles, n, SEQ)
                if context:
                    per_batch = CTX_SEQ // BANK
                    for chunk in range(n * per_batch, (n + 1) * per_batch):
                        add_jobs(n, context, ctx_T, CP, context_tiles, chunk, CTX_SEQ)
                jobs_before[n + 1] = len(jobs)
        if project:
            held = sb("held", [P, HELD, 2, BANK])

        JOB_BANKS = 3 if early else 4
        UNIT_BANKS = (2, 3, 7)
        unit_after = []
        if early:
            q_dram, k_dram, keys, causal = early
            units = max_units(keys, causal)
            U = len(units)
            first_job = jobs_before[CHUNKS - 2]
            unit_after = [first_job + w * (len(jobs) - first_job) // (EARLY * U) for w in range(EARLY * U)]
            qs = [sb(f"early_q{i}", [4 * HD, GH, SEQ], F32R) for i in range(EARLY)]
            ks = [sb(f"early_k{i}", [4 * HD, GH, keys], F32R) for i in range(EARLY)]
            max_parts = [sb(f"early_max{i}", [P, U]) for i in range(EARLY)]
            row_max, rest = sb("early_row_max", [P, GH * QT]), sb("early_rest", [P, 2, GH * QT])
        s_qk = [sem(f"early_in{i}") for i in range(EARLY)]
        unit_full, unit_read, s_shift = sem("early_full"), sem("early_read"), sem("early_shift")

        coef_in, w_in, ctx_in = sem("coef_in"), sem("w_in"), sem("ctx_in")
        zeroed, biased, copied = sem("zeroed"), sem("biased"), sem("copied")
        o_turned, o_read, projected, added = sem("o_turned"), sem("o_read"), sem("projected"), sem("added")
        measured, aggregated, rooted, inverted = sem("measured"), sem("aggregated"), sem("rooted"), sem("inverted")
        plain_done, rows_ready, squared, scaled = sem("plain_done"), sem("rows_ready"), sem("squared"), sem("scaled")
        turned, xT_ready = sem("turned"), sem("xT_ready")
        bank_full, head_done, bank_read = sem("bank_full"), sem("head_done"), sem("bank_read")
        stored, base = c.slot_stored, list(c.slot_count)
        halves, out_stored = sem("halves"), sem("out_stored")

        with nc.Block() as block:
            @block.sync
            def _(sp):
                for tile, ap in zip(coef, coefs):
                    sp.dma_start(tile[:, :], ap.partition_broadcast(P)).then_inc(coef_in, 16)
                for i, (dst, src, columns) in enumerate(w_loads):
                    sp.dma_start(dst, src, allow_slow_non_contiguous=columns).then_inc(w_in if i < w_own else ctx_in, 16)
                for dst, src, sem_of in prefetch:
                    sp.dma_start(dst, src).then_inc(sem_of, 16)
                for u, (kind, _, _, _, _, dst, part, first, per) in enumerate(jobs):
                    if early and u == jobs_before[1] + 4:
                        for x in range(jobs_before[1]):
                            sp.wait_ge(stored[x % HELD], base[x % HELD] + 16 * (x // HELD + 1))
                        for i in range(EARLY):
                            load_stacks(sp, qs[i], ks[i], i, q_dram, k_dram, s_qk[i])
                    sp.wait_ge(bank_read, u + 1)
                    b, at = first // per, first % per
                    if kind == "split":
                        row = b * D + part * P
                        sp.dma_start(dst[:, row:row + P, at:at + BANK].rearrange("a p t -> p a t"),
                                     held[:, u % HELD, :, :]).then_inc(stored[u % HELD], 16)
                    else:
                        kt = at // P + 2 * part
                        sp.dma_start(dst[b * GROUPS:(b + 1) * GROUPS, :, kt:kt + 2, :].rearrange("g p t d -> p g (t d)"),
                                     held[:, u % HELD, 0, :].rearrange("p (g m) -> p g m", g=GROUPS)
                                     ).then_inc(stored[u % HELD], 16)
                if out is not None:
                    for n in range(CHUNKS):
                        sp.wait_ge(rows_ready, QT * (n + 1))
                        sp.dma_start(out[n].rearrange("(q p) d -> p q d", p=P),
                                     rows[:, n * QT:(n + 1) * QT, :]).then_inc(out_stored, 16)
                    sp.wait_ge(out_stored, 16 * CHUNKS)
                for s in range(HELD):
                    c.slot_count[s] += 16 * len(range(s, len(jobs), HELD))
                    wait_for(sp, stored[s], c.slot_count[s])

            add_bias = bool(front and front[0] == "output" and biased_output)

            @block.gpsimd
            def _(pool):
                for tile in no_bias:
                    pool.memset(tile[:, :], 0.0).then_inc(zeroed, 1)
                if front and front[0] == "gather":
                    for t in range(NT):
                        for x in range(2):
                            pool.indirect_dma_start(gathered[:, t, x, :], None, results_dram[:, :],
                                                    bass.IndirectOffsetOnAxis(ap=place[:, x, t:t + 1], axis=0)
                                                    ).then_inc(got[t], 16)
                if add_bias:
                    for t in range(NT):
                        pool.tensor_tensor(c.x_tok[:, t, :], c.x_tok[:, t, :], c.bo[:, :], ALU.add).then_inc(biased, 1)
                if copy_to is not None:
                    for t in range(NT):
                        pool.wait_ge(plain_done, t // QT * QT + QT)
                        pool.tensor_copy(copy_to[:, t, :], c.x_tok[:, t, :]).then_inc(copied, 1)

            @block.tensor
            def _(pe):
                def output_of(n):
                    def turn(t):
                        wait_for(pe, o_read, t - 1)
                        for k in range(DK):
                            ins = pe.transpose(c.psum[:, TURN_BANK + t % 2, k * P:(k + 1) * P],
                                               o_tok[:, t, k * P:(k + 1) * P], c.ident[:, :])
                        ins.then_inc(o_turned, 1)

                    wait_for(pe, xT_ready, (n - 1) * DK)
                    turn(n * QT)
                    for t in range(n * QT, n * QT + QT):
                        if t + 1 < n * QT + QT:
                            turn(t + 1)
                        pe.wait_ge(o_read, t + 1)
                        wait_for(pe, added, t - 1)
                        for k in range(DK):
                            ins = pe.matmul(c.psum[:, FRONT_BANK + t % 2, 0:D], oT[:, t % 2, k, :], c.wo[:, k, :],
                                            start=k == 0, stop=k == DK - 1)
                        ins.then_inc(projected, 1)

                def combine_of(n):
                    for t in range(n * QT, n * QT + QT):
                        wait_for(pe, added, t - 1)
                        for e in range(EXPERTS):
                            ins = pe.matmul(c.psum[:, FRONT_BANK + t % 2, 0:D], front[1][:, e, t, :],
                                            front[2][:, e, t // QT, :], start=e == 0, stop=e == EXPERTS - 1)
                        ins.then_inc(projected, 1)

                def turn_rows(n):
                    if normed:
                        pe.wait_ge(rows_ready, QT * (n + 1))
                    for k in range(DK):
                        wait_for(pe, xT_ready, (n - 1) * DK + k + 1)
                        for q in range(QT):
                            ins = pe.transpose(c.psum[:, TURN_BANK + k, q * P:(q + 1) * P],
                                               rows[:, n * QT + q, k * P:(k + 1) * P], c.ident[:, :])
                        ins.then_inc(turned, 1)

                def maximum_scores(w):
                    i, (j, qt, k0, width) = w // U, units[w % U]
                    if w % U == 0:
                        pe.wait_ge(s_qk[i], 128)
                    if w == 0 and front:
                        pe.wait_ge(added, NT)
                    wait_for(pe, unit_read, w - 2)
                    bank = UNIT_BANKS[w % 3]
                    ins = pe.matmul(c.psum[:, bank, 0:width], qs[i][:, j, qt * P:(qt + 1) * P],
                                    ks[i][:, j, k0:k0 + width], start=True, stop=not causal)
                    if causal:
                        ins = pe.matmul(c.psum[:, bank, qt * P:(qt + 1) * P], c.ident_bf[:, :],
                                        c.mask_qk[:, :], start=False, stop=True)
                    ins.then_inc(unit_full, 1)

                def products(first, end):
                    for u in range(first, end):
                        kind, src, _, w, _, _, part, token, _ = jobs[u]
                        if src is not c.xT and u == jobs_before[0] + DK:
                            pe.wait_ge(ctx_in, 16 * (len(w_loads) - w_own))
                        wait_for(pe, bank_read, u - JOB_BANKS + 1)
                        bank = JOB_BANK + u % JOB_BANKS
                        for half in range(1 if kind == "split" else 2):
                            for k in range(2):
                                if kind == "split":
                                    ins = pe.matmul(c.psum[:, bank, :], w[:, k, part * P:(part + 1) * P],
                                                    src[:, k, token:token + BANK], start=k == 0, stop=k == 1)
                                else:
                                    t = token + (2 * part + half) * P
                                    ins = pe.matmul(c.psum[:, bank, half * D:(half + 1) * D], src[:, k, t:t + P],
                                                    w[:, k, :], start=k == 0, stop=k == 1)
                        ins.then_inc(bank_full, 1)
                        for x in range(len(unit_after)):
                            if unit_after[x] == u:
                                maximum_scores(x)

                for n in range(CHUNKS + 1):
                    if n < CHUNKS and front and front[0] != "gather":
                        (output_of if front[0] == "output" else combine_of)(n)
                    if n and out is None:
                        turn_rows(n - 1)
                        if project:
                            if n == 1:
                                pe.wait_ge(w_in, 16 * w_own)
                            pe.wait_ge(xT_ready, DK * n)
                            products(jobs_before[n - 1], jobs_before[n])

            @block.scalar
            def _(act):
                def heads(first, end):
                    for u in range(first, end):
                        kind, _, _, _, b, _, part, _, _ = jobs[u]
                        if kind == "split":
                            act.wait_ge(bank_full, u + 1)
                            if u >= HELD:
                                act.wait_ge(stored[u % HELD], base[u % HELD] + 16 * (u // HELD))
                            act.activation(held[:, u % HELD, 0, :].bitcast(F32R), c.psum[:, JOB_BANK + u % JOB_BANKS, :],
                                           ACT.Identity, bias=b[:, part:part + 1]).then_inc(head_done, 1)

                def output_turned(tiles):
                    for t in tiles:
                        act.wait_ge(o_turned, t + 1)
                        wait_for(act, projected, t - 1)
                        act.activation(oT[:, t % 2, :, :],
                                       c.psum[:, TURN_BANK + t % 2, 0:DK * P].rearrange("p (k n) -> p k n", k=DK),
                                       ACT.Copy).then_inc(o_read, 1)

                def rows_turned(n):
                    for k in range(DK):
                        act.wait_ge(turned, DK * n + k + 1)
                        act.activation(c.xT[:, k, n * SEQ:(n + 1) * SEQ], c.psum[:, TURN_BANK + k, :],
                                       ACT.Copy).then_inc(xT_ready, 1)

                def roots(n):
                    own = slice(n * QT, n * QT + QT)
                    for i in range(len(passes)):
                        act.wait_ge(aggregated, QT * (n * len(passes) + i + 1))
                        act.activation(root[:, i, own], mean_var[:, i, own, 1], ACT.Sqrt,
                                       bias=c.eps[:, :]).then_inc(rooted, 1)
                    if rms:
                        if layernorm:
                            act.wait_ge(plain_done, QT * (n + 1))
                        for t in range(n * QT, n * QT + QT):
                            wait_for(act, squared, t - 1)
                            act.activation(squares[:, t % 2, :], c.x_tok[:, t, :], ACT.Square,
                                           accum_out=rstd[:, 1, t:t + 1]).then_inc(squared, 1)
                        act.wait_ge(squared, QT * (n + 1))
                        act.activation(root[:, 1, own], rstd[:, 1, own], ACT.Sqrt).then_inc(rooted, 1)

                AHEAD = 2
                has_output = bool(front and front[0] == "output")
                for n in range(CHUNKS + 1):
                    if has_output and n < CHUNKS:
                        output_turned(range(n * QT + (AHEAD if n == 1 else 0), (n + 1) * QT))
                    if has_output and n == 0:
                        output_turned(range(QT, QT + AHEAD))
                    if n and out is None:
                        rows_turned(n - 1)
                    if n < CHUNKS:
                        roots(n)
                    if project:
                        if n == 0:
                            act.wait_ge(w_in, 16 * w_own)
                            wait_for(act, zeroed, len(no_bias))
                        else:
                            heads(jobs_before[n - 1], jobs_before[n])

            @block.vector
            def _(v):
                inverts = 0
                heads = 0

                def small(ins):
                    nonlocal inverts
                    ins.then_inc(inverted, 1)
                    inverts += 1
                    v.wait_ge(inverted, inverts)

                def norms(n):
                    own = slice(n * QT, n * QT + QT)
                    tiles = range(n * QT, n * QT + QT)
                    for i, kind in enumerate(passes):
                        seq = n * len(passes) + i
                        if front and i == 0:
                            v.wait_ge(added, QT * (n + 1))
                        for t in tiles:
                            v.bn_stats(stats[:, t, :], c.x_tok[:, t, :]).then_inc(measured, 1)
                        v.wait_ge(measured, QT * (seq + 1))
                        for t in tiles:
                            v.bn_aggr(mean_var[:, i, t, :], stats[:, t, :]).then_inc(aggregated, 1)
                        v.wait_ge(aggregated, QT * (seq + 1))
                        v.wait_ge(rooted, n * (len(passes) + bool(rms)) + i + 1)
                        small(v.reciprocal(rstd[:, i, own], root[:, i, own]))
                        if kind == "plain":
                            for t in tiles:
                                v.tensor_scalar(c.x_tok[:, t, :], c.x_tok[:, t, :], mean_var[:, i, t, 0:1],
                                                rstd[:, i, t:t + 1], ALU.subtract, ALU.mult
                                                ).then_inc(plain_done if affine or rms else rows_ready, 1)
                            if affine or rms:
                                v.wait_ge(plain_done, QT * (n + 1))
                        else:
                            if n == 0:
                                v.wait_ge(coef_in, 32)
                            for t in tiles:
                                v.scalar_tensor_tensor(rows[:, t, :], c.x_tok[:, t, :], mean_var[:, i, t, 0:1],
                                                       coef[0][:, :], ALU.subtract, ALU.mult).then_inc(scaled, 1)
                            v.wait_ge(scaled, QT * (n + 1))
                            for t in tiles:
                                v.scalar_tensor_tensor(rows[:, t, :], rows[:, t, :], rstd[:, i, t:t + 1],
                                                       coef[1][:, :], ALU.mult, ALU.add).then_inc(rows_ready, 1)
                    if rms:
                        v.wait_ge(rooted, (n + 1) * (len(passes) + 1))
                        small(v.tensor_scalar(root[:, 1, own], root[:, 1, own], 1e-12, None, ALU.max))
                        small(v.reciprocal(rstd[:, 1, own], root[:, 1, own]))
                        small(v.tensor_scalar(rstd[:, 1, own], rstd[:, 1, own], float(D) ** 0.5, None, ALU.mult))
                        if n == 0:
                            v.wait_ge(coef_in, 16)
                        for t in tiles:
                            v.scalar_tensor_tensor(rows[:, t, :], c.x_tok[:, t, :], rstd[:, 1, t:t + 1], coef[0][:, :],
                                                   ALU.mult, ALU.mult).then_inc(rows_ready, 1)

                def maximum(w):
                    i, width = w // U, units[w % U][3]
                    v.wait_ge(unit_full, w + 1)
                    v.reduce_max(max_parts[i][:, w % U:w % U + 1], c.psum[:, UNIT_BANKS[w % 3], 0:width],
                                 axis=AX_X).then_inc(unit_read, 1)
                    if w % U == U - 1:
                        v.wait_ge(unit_read, w + 1)
                        for k in range(SHIFT_STEPS):
                            shift_step(v, s_shift, SHIFT_STEPS * i, k, max_parts[i], row_max, rest, c.early_shift[i])
                        v.wait_ge(s_shift, SHIFT_STEPS * (i + 1))

                def tails(first, end):
                    nonlocal heads
                    for u in range(first, end):
                        kind, _, _, _, b, _, part, _, _ = jobs[u]
                        bank = c.psum[:, JOB_BANK + u % JOB_BANKS, :]
                        if kind == "split":
                            heads += 1
                            v.wait_ge(head_done, heads)
                            v.scalar_tensor_tensor(held[:, u % HELD, 1, :].bitcast(F32R), bank, b[:, part:part + 1],
                                                   held[:, u % HELD, 0, :], ALU.add, ALU.subtract).then_inc(bank_read, 1)
                        else:
                            v.wait_ge(bank_full, u + 1)
                            if u >= HELD:
                                v.wait_ge(stored[u % HELD], base[u % HELD] + 16 * (u // HELD))
                            v.tensor_copy(held[:, u % HELD, 0, :].rearrange("p (g t d) -> p t g d", g=GROUPS, t=2),
                                          bank.rearrange("p (t g d) -> p t g d", t=2, g=GROUPS)).then_inc(bank_read, 1)
                        for x in range(len(unit_after)):
                            if unit_after[x] == u:
                                maximum(x)

                def add_front(n):
                    tiles = range(n * QT, n * QT + QT)
                    if front[0] == "gather":
                        for x in range(2):
                            for t in tiles:
                                if x == 0:
                                    v.wait_ge(got[t], 32)
                                else:
                                    v.wait_ge(halves, t + 1)
                                v.scalar_tensor_tensor(c.x_tok[:, t, :], gathered[:, t, x, :], share[:, t, x:x + 1],
                                                       c.x_tok[:, t, :], ALU.mult, ALU.add
                                                       ).then_inc(added if x else halves, 1)
                        return
                    for t in tiles:
                        v.wait_ge(projected, t + 1)
                        if add_bias:
                            v.wait_ge(biased, t + 1)
                        v.tensor_tensor(c.x_tok[:, t, :], c.psum[:, FRONT_BANK + t % 2, 0:D], c.x_tok[:, t, :],
                                        ALU.add).then_inc(added, 1)

                for n in range(CHUNKS + 1):
                    if n < CHUNKS:
                        if front:
                            add_front(n)
                        if normed:
                            norms(n)
                    if project:
                        if n == 0:
                            v.wait_ge(w_in, 16 * w_own)
                            wait_for(v, zeroed, len(no_bias))
                        else:
                            tails(jobs_before[n - 1], jobs_before[n])


def attention_plan(KT, units, causal):
    def queries(t):
        return SEQ - t * P if causal else SEQ

    slots = [(t, h) for t in range(KT) for h in range(2)]
    load = [2 * queries(t) + (queries(t) if h else 0) for t, h in slots]
    cost = [unit[3] + P for unit in units]
    plan, u = [], 0
    shift_slots = (3, 5) if causal else (4, 6)
    for s, (t, h) in enumerate(slots):
        while u < len(units) and sum(cost[:u]) * sum(load) <= sum(load[:s]) * sum(cost):
            plan.append(("unit", 2, u))
            if u < SHIFT_STEPS:
                plan.append(("chain", 1, u))
            u += 1
        if s in shift_slots:
            plan.append(("shift", 1, shift_slots.index(s)))
        plan.append(("scores", 0, s))
        if h == 1:
            plan += [("values", 0, t - 1)] if t else [("values", -1, KT - 1), ("drain", -1, 0)]
        if s == 4:
            plan.append(("turn", -1, 0))
    return plan + [("unit", 2, v) for v in range(u, len(units))]


@staged
def stage_attention(c, name, q_dram, k_dram, v_dram, v_bias, o_tok, keys, causal, w_out, b_out):
    nc = c.nc
    KT = keys // P
    units = max_units(keys, causal)
    U = len(units)
    scale = 1.0 / float(HD) ** 0.5
    NB = 4
    PV_BANK, RING = 6, (4, 5, 7)
    PAIRS = 2 * KT + 2
    plan = attention_plan(KT, units, causal)
    ring_uses = [x for x in plan if x[0] in ("unit", "turn")]

    def exists(n, event):
        return (EARLY if event[0] in ("unit", "chain") else 0) <= n + event[1] < NG

    def pair_use(n, like, event):
        own = [x for x in plan if x[0] in ("scores", "shift") and exists(like, x)].index(event)
        return own if like < 0 else 2 + PAIRS * n + own

    def pair_banks(like, event):
        return 2 * (pair_use(like, like, event) % 2)

    def bank_before(n, event):
        at = ring_uses.index(event)
        for body in (n, n - 1, n - 2):
            same = [x for i, x in enumerate(ring_uses) if i % 3 == at % 3 and (body < n or i < at)]
            same = [x for x in same if exists(body, x)]
            if same:
                what, ahead, index = same[-1]
                return what, ahead + body - n, index
        return None

    with ExitStack() as ctx:
        def sb(n, shape, dt=F32):
            return ctx.enter_context(nc.sbuf_tensor(f"{name}_{n}", shape, dt))

        qs = [sb(f"q{i}", [STACK, GH, SEQ], F32R) for i in range(NB)]
        ks = [sb(f"k{i}", [STACK, GH, keys], F32R) for i in range(NB)]
        v_raw = [sb(f"v_raw{i}", [P, KT, GD]) for i in range(2)]
        v_aug = [sb(f"v_aug{i}", [P, KT, GH, 32]) for i in range(2)]
        bias = sb("v_bias", [P, D])
        probs = [sb(f"p{i}", [P, GH, SEQ]) for i in range(2)]
        max_parts = [sb(f"max_parts{i}", [P, U]) for i in range(2)]
        row_max = sb("row_max", [P, GH * QT])
        rest = sb("rest", [P, 2, GH * QT])
        shift = sb("shift", [P, GH * QT, 3], BF16)
        o_sum = sb("o_sum", [P, SEQ])
        recip = sb("recip", [P, QT * GH])
        s_set, s_key_set = c.sem(f"{name}_set"), c.sem(f"{name}_key_set")
        FILLS = (1, 4, 3, 6)
        s_bias, s_out_in = c.sem(f"{name}_v_bias"), c.sem(f"{name}_out_in")
        s_qk = [c.sem(f"{name}_qk_in{i}") for i in range(NB)]
        s_vin = [c.sem(f"{name}_v_in{i}") for i in range(2)]
        s_vaug = c.sem(f"{name}_v_aug")
        s_unit_full, s_unit_read = c.sem(f"{name}_unit_full"), c.sem(f"{name}_unit_read")
        s_shift = c.sem(f"{name}_shift")
        s_pair_full, s_pair_read = c.sem(f"{name}_pair_full"), c.sem(f"{name}_pair_read")
        s_pv = c.sem(f"{name}_pv")
        s_osum, s_turn, s_norm = c.sem(f"{name}_o_sum"), c.sem(f"{name}_turn"), c.sem(f"{name}_norm")

        def first_query(t):
            return t * P if causal else 0

        def ring_bank(event):
            return RING[ring_uses.index(event) % 3]

        with nc.Block() as block:
            def for_groups(eng, body):
                for r in range(GROUPS):
                    body(r, 0, r, r)
                with eng.Fori(1, BATCH - 1) as b:
                    for r in range(GROUPS):
                        body(b * GROUPS + r, b, r, GROUPS + r)
                for r in range(GROUPS):
                    body((BATCH - 1) * GROUPS + r, BATCH - 1, r, (BATCH - 1) * GROUPS + r)

            def run_plan(eng, handlers):
                def body(n, b, r, like):
                    for event in plan:
                        what, ahead, index = event
                        if what in handlers and exists(like, event):
                            g = (r + ahead) % GROUPS
                            batch = b + (r + ahead - g) // GROUPS
                            handlers[what](n + ahead, batch, g, index, n, like, event)

                body(-1, -1, 3, -1)
                for_groups(eng, body)
                body(NG, BATCH, 0, NG)

            @block.sync
            def _(sp):
                def body(n, b, r, like):
                    if not isinstance(n, int) or n >= NB:
                        sp.wait_ge(s_pair_full, 2 + PAIRS * (n - NB + 1))
                    load_stacks(sp, qs[r], ks[r], n, q_dram, k_dram, s_qk[r])
                    wait_for(sp, s_vaug, n - 1)
                    sp.dma_start(v_raw[r % 2][:, :, :], v_dram[bass.ds(n, 1), :, :, :].rearrange("o p t d -> p (o t) d")
                                 ).then_inc(s_vin[r % 2], 16)

                if v_bias is not None:
                    sp.dma_start(bias[:, :], v_bias.partition_broadcast(P)).then_inc(s_bias, 16)
                for_groups(sp, body)
                sp.dma_start(c.wo[:, :, :], w_out.rearrange("(k p) n -> p k n", p=P)).then_inc(s_out_in, 16)
                if b_out is not None:
                    sp.dma_start(c.bo[:, :], b_out.partition_broadcast(P)).then_inc(s_out_in, 16)
                sp.wait_ge(s_out_in, 16 * (1 + (b_out is not None)))

            @block.gpsimd
            def _(pool):
                steps = 0
                if v_bias is None:
                    pool.memset(bias[:, :], 0.0).then_inc(s_bias, 1)
                pool.wait_ge(s_bias, 1 if v_bias is None else 16)

                def fill(ap, value):
                    nonlocal steps
                    pool.memset(ap, value).then_inc(s_set, 1)
                    steps += 1
                    pool.wait_ge(s_set, steps)

                def fill_queries(i):
                    fill(qs[i][64:STACK, :, :].bitcast(F32), 0.0)

                fill_queries(0)
                fill(v_aug[0][:, :, :, :], 1.0)
                fill_queries(2)

                def body(n, b, r, like):
                    pool.wait_ge(s_vin[r % 2], 16 * (b * (GROUPS // 2) + r // 2 + 1))
                    wait_for(pool, s_pv, KT * (n - 1))
                    own = bias[:, r * GD:(r + 1) * GD].rearrange("p (j d) -> p j d", d=HD).unsqueeze(1)
                    pool.tensor_tensor(v_aug[r % 2][:, :, :, 0:HD],
                                       v_raw[r % 2][:, :, :].rearrange("p t (j d) -> p t j d", d=HD),
                                       own.to_broadcast([P, KT, GH, HD]), ALU.add).then_inc(s_vaug, 1)
                    if like == 0:
                        pool.wait_ge(s_vaug, 1)
                        fill_queries(1)
                        fill(v_aug[1][:, :, :, :], 1.0)
                        fill_queries(3)

                for_groups(pool, body)

            @block.tensor
            def _(pe):
                def wait_bank(n, like, event):
                    found = bank_before(like, event)
                    if found is None:
                        return
                    what, ahead, index = found
                    if what == "unit":
                        pe.wait_ge(s_unit_read, (n + ahead - EARLY) * U + index + 1)
                    else:
                        pe.wait_ge(s_norm, 2 * (n + ahead + 1))

                def unit(g, b, r, u, n, like, event):
                    if u == 0:
                        if like + 2 < NB:
                            pe.wait_ge(s_set, FILLS[like + 2])
                            pe.wait_ge(s_key_set, like + 3)
                        pe.wait_ge(s_qk[r], 128 * (b + 1))
                    wait_bank(n, like, event)
                    j, qt, k0, width = units[u]
                    bank = ring_bank(event)
                    ins = pe.matmul(c.psum[:, bank, 0:width], qs[r][0:SHIFT_ROW, j, qt * P:(qt + 1) * P],
                                    ks[r][0:SHIFT_ROW, j, k0:k0 + width], start=True, stop=not causal)
                    if causal:
                        ins = pe.matmul(c.psum[:, bank, qt * P:(qt + 1) * P], c.ident_bf[:, :],
                                        c.mask_qk[:, :], start=False, stop=True)
                    ins.then_inc(s_unit_full, 1)

                def shift_rows(g, b, r, h, n, like, event):
                    early = like + 1 < EARLY
                    source = c.early_shift[like + 1] if early else shift
                    if h == 0 and not early:
                        pe.wait_ge(s_shift, SHIFT_STEPS * (g - EARLY + 1))
                    use = pair_use(n, like, event)
                    wait_for(pe, s_pair_read, use - 1)
                    for j in range(2 * h, 2 * h + 2):
                        bank = pair_banks(like, event) + j % 2
                        for qt in range(QT):
                            ins = pe.matmul(c.psum[SHIFT_ROW:SHIFT_END, bank, qt * P:(qt + 1) * P],
                                            source[:, j * QT + qt, :], c.ident_bf[:, :], start=True, stop=True)
                    ins.then_inc(s_pair_full, 1)

                def scores(g, b, r, s, n, like, event):
                    t, h = s // 2, s % 2
                    if s == 0 and like < EARLY:
                        pe.wait_ge(s_set, FILLS[like])
                        pe.wait_ge(s_key_set, like + 1)
                        pe.wait_ge(s_qk[r], 128 * (b + 1))
                    pe.wait_ge(s_pair_read, pair_use(n, like, event) - 1)
                    q0 = first_query(t)
                    for j in range(2 * h, 2 * h + 2):
                        bank = pair_banks(like, event) + j % 2
                        ins = pe.matmul(c.psum[:, bank, q0:SEQ], ks[r][0:STACK, j, t * P:(t + 1) * P],
                                        qs[r][0:STACK, j, q0:SEQ], start=True, stop=not causal)
                        if causal:
                            ins = pe.matmul(c.psum[:, bank, q0:q0 + P], c.ident_bf[:, :], c.mask_kq[:, :],
                                            start=False, stop=True)
                    ins.then_inc(s_pair_full, 1)

                def values(g, b, r, t, n, like, event):
                    pe.wait_ge(s_pair_read, pair_use(g, like + event[1], ("scores", 0, 2 * t + 1)) + 1)
                    if t == 0:
                        pe.wait_ge(s_vaug, g + 1)
                        wait_for(pe, s_osum, g)
                    q0 = first_query(t)
                    for j in range(GH):
                        ins = pe.matmul(c.psum[32 * j:32 * j + 32, PV_BANK, q0:SEQ], v_aug[r % 2][:, t, j, :],
                                        probs[t % 2][:, j, q0:SEQ], start=t == 0, stop=t == KT - 1)
                    ins.then_inc(s_pv, 1)

                def turn(g, b, r, _, n, like, event):
                    pe.wait_ge(s_osum, g + 1)
                    wait_bank(n, like, event)
                    for qt in range(QT):
                        ins = pe.transpose(c.psum[:, ring_bank(event), qt * P:(qt + 1) * P],
                                           o_sum[:, qt * P:(qt + 1) * P], c.ident[:, :])
                    ins.then_inc(s_turn, 1)

                run_plan(pe, {"unit": unit, "shift": shift_rows, "scores": scores, "values": values, "turn": turn})

            @block.scalar
            def _(act):
                def shift_rows(g, b, r, h, n, like, event):
                    if h == 0 and like + 1 < EARLY:
                        act.wait_ge(s_set, FILLS[like + 1])
                    act.wait_ge(s_pair_full, pair_use(n, like, event) + 1)
                    first = pair_banks(like, event)
                    act.activation(qs[r][SHIFT_ROW:SHIFT_END, 2 * h:2 * h + 2, :],
                                   c.psum[SHIFT_ROW:SHIFT_END, first:first + 2, :], ACT.Copy).then_inc(s_pair_read, 1)

                def exps(g, b, r, s, n, like, event):
                    t, h = s // 2, s % 2
                    q0 = first_query(t)
                    first = pair_banks(like, event)
                    act.wait_ge(s_pair_full, pair_use(n, like, event) + 1)
                    wait_for(act, s_pv, KT * g + t - 1)
                    act.activation(probs[t % 2][:, 2 * h:2 * h + 2, q0:SEQ],
                                   c.psum[:, first:first + 2, q0:SEQ], ACT.Exp,
                                   scale=scale).then_inc(s_pair_read, 1)

                def drain_outputs(g, b, r, _, n, like, event):
                    act.wait_ge(s_pv, KT * (g + 1))
                    wait_for(act, s_turn, g)
                    act.activation(o_sum[:, :], c.psum[:, PV_BANK, :], ACT.Copy).then_inc(s_osum, 1)

                run_plan(act, {"shift": shift_rows, "scores": exps, "drain": drain_outputs})

            @block.vector
            def _(v):
                def unit(g, b, r, u, n, like, event):
                    v.wait_ge(s_unit_full, (g - EARLY) * U + u + 1)
                    if u == 0:
                        if like + 2 >= EARLY + 2:
                            v.wait_ge(s_shift, SHIFT_STEPS * (g - 2 - EARLY) + 1)
                    v.reduce_max(max_parts[r % 2][:, u:u + 1], c.psum[:, ring_bank(event), 0:units[u][3]],
                                 axis=AX_X).then_inc(s_unit_read, 1)

                def chain(g, b, r, k, n, like, event):
                    if k == 0:
                        v.wait_ge(s_unit_read, U * (g - EARLY + 1))
                    if k == 1:
                        v.wait_ge(s_pair_full, pair_use(n - 1, like - 1, ("shift", 1, 1)) + 1)
                    shift_step(v, s_shift, SHIFT_STEPS * (g - EARLY), k, max_parts[r % 2], row_max, rest, shift)

                def normalise(g, b, r, _, n, like, event):
                    v.wait_ge(s_turn, g + 1)
                    turned = c.psum[:, ring_bank(event), :].rearrange("p (a c) -> p a c", c=32)
                    wait_for(v, s_norm, 2 * g)
                    v.reciprocal(recip[:, :].unsqueeze(2), turned[:, :, HD:HD + 1]).then_inc(s_norm, 1)
                    v.wait_ge(s_norm, 2 * g + 1)
                    dst = o_tok[:, bass.ds(b * QT, QT), r * GD:(r + 1) * GD].rearrange("p q (j d) -> p q j d", d=HD)
                    v.tensor_tensor(dst, turned[:, :, 0:HD].rearrange("p (q j) d -> p q j d", j=GH),
                                    recip[:, :].rearrange("p (q j) -> p q j", j=GH).unsqueeze(3)
                                    .to_broadcast([P, QT, GH, HD]), ALU.mult).then_inc(s_norm, 1)

                for i in range(NB):
                    v.memset(ks[i][64:STACK, :, :].bitcast(F32), 1.0).then_inc(s_key_set, 1)
                run_plan(v, {"unit": unit, "chain": chain, "turn": normalise})




@staged
def stage_experts(c, name, w1, b1, w2, b2, tokens_of, eo):
    nc = c.nc
    with ExitStack() as ctx:
        def sb(n, shape, dt=F32):
            return ctx.enter_context(nc.sbuf_tensor(f"{name}_{n}", shape, dt))

        up = [sb(f"up{i}", [P, DK, HID]) for i in range(2)]
        down = [sb(f"down{i}", [P, HM, D]) for i in range(2)]
        up_bias = [sb(f"up_bias{i}", [P, HM]) for i in range(2)]
        down_bias = [sb(f"down_bias{i}", [P, D]) for i in range(2)]
        hidden = sb("hidden", [P, HM, BANK])
        w_in = [c.sem(f"{name}_w_in{i}") for i in range(2)]
        s_up, s_gelu = c.sem(f"{name}_up"), c.sem(f"{name}_gelu")
        s_down, s_read = c.sem(f"{name}_down"), c.sem(f"{name}_read")
        per_load = 16 * 4
        tiles = BANK // P
        UP_BANKS = 4

        with nc.Block() as block:
            def for_experts(eng, body):
                for r in range(2):
                    body(r, 0, r)
                with eng.Fori(1, EXPERTS // 2) as pair:
                    for r in range(2):
                        body(pair * 2 + r, pair, r)

            @block.sync
            def _(sp):
                def body(e, pair, r):
                    wait_for(sp, s_down, tiles * (e - 1))
                    one = bass.ds(e, 1)
                    sp.dma_start(up[r][:, :, :], w1[one, :, :].rearrange("o (k p) n -> p (o k) n", p=P)).then_inc(w_in[r], 16)
                    sp.dma_start(up_bias[r][:, :], b1[one, :, :].rearrange("o p m -> p (o m)")).then_inc(w_in[r], 16)
                    sp.dma_start(down[r][:, :, :], w2[one, :, :].rearrange("o (m p) n -> p (o m) n", p=P)).then_inc(w_in[r], 16)
                    wait_for(sp, s_read, tiles * (e - 1))
                    sp.dma_start(down_bias[r][:, :], b2[one, :].rearrange("o n -> (o n)").partition_broadcast(P)
                                 ).then_inc(w_in[r], 16)

                for_experts(sp, body)

            @block.tensor
            def _(pe):
                def body(e, pair, r):
                    pe.wait_ge(w_in[r], (pair + 1) * per_load)
                    for m in range(HM):
                        wait_for(pe, s_gelu, e * HM + m - UP_BANKS + 1)
                        for k in range(DK):
                            ins = pe.matmul(c.psum[:, m % UP_BANKS, :], up[r][:, k, m * P:(m + 1) * P],
                                            tokens_of(e, k), start=k == 0, stop=k == DK - 1)
                        ins.then_inc(s_up, 1)
                    for t in range(tiles):
                        wait_for(pe, s_read, (e - 1) * tiles + t + 1)
                        for m in range(HM):
                            if t == 0:
                                pe.wait_ge(s_gelu, e * HM + m + 1)
                            ins = pe.matmul(c.psum[:, 4 + t, 0:D], hidden[:, m, t * P:(t + 1) * P],
                                            down[r][:, m, :], start=m == 0, stop=m == HM - 1)
                        ins.then_inc(s_down, 1)

                for_experts(pe, body)

            @block.scalar
            def _(act):
                def body(e, pair, r):
                    act.wait_ge(w_in[r], (pair + 1) * per_load)
                    wait_for(act, s_down, e * tiles)
                    for m in range(HM):
                        act.wait_ge(s_up, e * HM + m + 1)
                        act.activation(hidden[:, m, :], c.psum[:, m % UP_BANKS, :], ACT.Gelu,
                                       bias=up_bias[r][:, m:m + 1]).then_inc(s_gelu, 1)

                for_experts(act, body)

            @block.vector
            def _(v):
                def body(e, pair, r):
                    v.wait_ge(w_in[r], (pair + 1) * per_load)
                    for t in range(tiles):
                        v.wait_ge(s_down, e * tiles + t + 1)
                        v.tensor_tensor(eo[:, bass.ds(e, 1), t, :], c.psum[:, 4 + t, 0:D].unsqueeze(1),
                                        down_bias[r][:, :].unsqueeze(1), ALU.add).then_inc(s_read, 1)

                for_experts(v, body)


def soft_moe(c, name, before, after):
    nc, a = c.nc, c.args
    ES = EXPERTS * SLOTS
    with ExitStack() as ctx:
        def keep(n, shape):
            return ctx.enter_context(nc.sbuf_tensor(f"soft_{n}", shape, F32))

        slots_T = keep("slots_T", [P, EXPERTS, DK, BATCH * SLOTS])
        combine = keep("combine", [P, EXPERTS, NT, P])
        with nc.sbuf_tensor("soft_slot_T", [P, DK, ES], F32) as slot_T:
            with nc.sbuf_tensor("soft_embeds", [P, EXPERTS, D], F32) as embeds:
                stage_fetch(c, "soft_embeds_in", [(embeds[:, :, :], a["L0_ffn_slot_embeds"].rearrange("e s d -> s e d"))])
                stage_norm(c, "slot", embeds, EXPERTS, rms=a["L0_ffn_slot_norm_gamma"], dstT=slot_T)
            stage_between(c, f"{name}_in", rms=a["L0_ffn_norm_gamma"], rows_to=c.rows, **before)
            stage_soft_routes(c, c.rows, slot_T, slots_T, combine)
        outputs = slots_T[:, :, :, :].rearrange("p e k (h n) -> p e (k h) n", n=D)
        stage_experts(c, "soft_experts", a["L0_ffn_w1"], a["L0_ffn_b1"], a["L0_ffn_w2"], a["L0_ffn_b2"],
                      lambda e, k: slots_T[:, bass.ds(e, 1), k, :].rearrange("p o n -> p (o n)"), eo=outputs)
        stage_between(c, f"{name}_out", front=("combine", combine, outputs), **after)


@staged
def stage_soft_routes(c, h_tok, slot_T, slots_T, combine):
    nc = c.nc
    with ExitStack() as ctx:
        def sb(n, shape, dt=F32):
            return ctx.enter_context(nc.sbuf_tensor(f"route_{n}", shape, dt))

        def sem(n):
            return c.sem(f"route_{n}")

        jobs = []
        for b in range(BATCH):
            jobs += [("dispatch", b, e) for e in range(EXPERTS)] + [("combine", b, q) for q in range(QT)]
            jobs += [("slots", b, k) for k in range(DK)]
        soft = [i for i, job in enumerate(jobs) if job[0] != "slots"]
        place = {i: n for n, i in enumerate(soft)}
        DEEP, TURN_BANK = 3, 6
        probs = sb("probs", [P, DEEP, 2, BANK])
        dispatch = sb("dispatch", [P, QT, EXPERTS * SLOTS])
        logits = sb("logits", [P, EXPERTS, SEQ])
        low, total, inverse = sb("low", [P, len(soft)]), sb("total", [P, len(soft)]), sb("inverse", [P, len(soft)])
        s_full, s_low, s_exp, s_inverse = sem("full"), sem("low"), sem("exp"), sem("inverse")
        s_scaled, s_turned, s_out, s_slots = sem("scaled"), sem("turned"), sem("out"), sem("slots")
        s_kept = sem("kept")

        def banks(i):
            return 2 if jobs[i][0] != "dispatch" else 1

        def dispatches_to(i):
            return sum(job[0] == "dispatch" for job in jobs[:i + 1])

        def scores_of(i):
            kind, _, e = jobs[i]
            return logits[:, e:e + 1, :] if kind == "dispatch" else c.psum[:, 2 * (i % DEEP):2 * (i % DEEP) + 2, :]

        def slots_before(i):
            return sum(job[0] == "slots" for job in jobs[:i])

        with nc.Block() as block:
            @block.tensor
            def _(pe):
                def fill(i):
                    kind, b, n = jobs[i]
                    if i >= DEEP:
                        if jobs[i - DEEP][0] == "dispatch":
                            pe.wait_ge(s_kept, dispatches_to(i - DEEP))
                        elif i - DEEP in place:
                            pe.wait_ge(s_exp, place[i - DEEP] + 1)
                        else:
                            pe.wait_ge(s_slots, slots_before(i - DEEP) + 1)
                    if kind == "slots":
                        pe.wait_ge(s_out, max(place[x] for x in soft if jobs[x][:2] == ("dispatch", b)) + 1)
                    if kind == "combine" and n == 0:
                        pe.wait_ge(s_kept, (b + 1) * EXPERTS)
                    for h in range(banks(i)):
                        bank = c.psum[:, 2 * (i % DEEP) + h, :]
                        if kind == "dispatch":
                            for k in range(DK):
                                ins = pe.matmul(bank, slot_T[:, k, n * SLOTS:(n + 1) * SLOTS],
                                                c.xT[:, k, b * SEQ:(b + 1) * SEQ], start=k == 0, stop=k == DK - 1)
                        elif kind == "combine":
                            for q in range(BANK // P):
                                ins = pe.transpose(bank[:, q * P:(q + 1) * P],
                                                   logits[:, h * (BANK // P) + q, n * P:(n + 1) * P], c.ident[:, :])
                        else:
                            for q in range(QT):
                                ins = pe.matmul(bank, h_tok[:, b * QT + q, n * P:(n + 1) * P],
                                                dispatch[:, q, h * BANK:(h + 1) * BANK], start=q == 0, stop=q == QT - 1)
                    ins.then_inc(s_full, 1)

                def turn(i):
                    n = place[i]
                    pe.wait_ge(s_scaled, n + 1)
                    wait_for(pe, s_out, n)
                    for h in range(banks(i)):
                        for q in range(BANK // P):
                            ins = pe.transpose(c.psum[:, TURN_BANK + h, q * P:(q + 1) * P],
                                               probs[:, n % DEEP, h, q * P:(q + 1) * P], c.ident[:, :])
                    ins.then_inc(s_turned, 1)

                left = list(soft)
                for i in range(len(jobs)):
                    while left and (left[0] <= i - 3 or jobs[i][0] == "slots" and jobs[left[0]][:2] == ("dispatch", jobs[i][1])):
                        turn(left.pop(0))
                    fill(i)
                for i in left:
                    turn(i)

            @block.vector
            def _(v):
                def lows(i):
                    n = place[i]
                    v.wait_ge(s_full, i + 1)
                    kind, b, e = jobs[i]
                    if kind == "dispatch":
                        if b and e == 0:
                            v.wait_ge(s_full, max(x for x in soft if jobs[x][:2] == ("combine", b - 1)) + 1)
                        v.tensor_copy(logits[:, e, :], c.psum[:, 2 * (i % DEEP), :]).then_inc(s_kept, 1)
                        v.wait_ge(s_kept, dispatches_to(i))
                    v.tensor_reduce(low[:, n:n + 1], scores_of(i), axis=mybir.AxisListType.XY, op=ALU.max,
                                    negate=True).then_inc(s_low, 1)

                def scale(i):
                    n = place[i]
                    v.wait_ge(s_exp, n + 1)
                    v.reciprocal(inverse[:, n:n + 1], total[:, n:n + 1]).then_inc(s_inverse, 1)
                    v.wait_ge(s_inverse, n + 1)
                    own = probs[:, n % DEEP, 0:banks(i), :]
                    v.tensor_scalar(own, own, inverse[:, n:n + 1], None, ALU.mult).then_inc(s_scaled, 1)

                for i in range(len(jobs) + 1):
                    if i < len(jobs) and i in place:
                        lows(i)
                    if i >= 1 and i - 1 in place:
                        scale(i - 1)

            @block.scalar
            def _(act):
                def exps(i):
                    n = place[i]
                    act.wait_ge(s_low, n + 1)
                    wait_for(act, s_turned, n - DEEP + 1)
                    act.activation(probs[:, n % DEEP, 0:banks(i), :], scores_of(i),
                                   ACT.Exp, bias=low[:, n:n + 1], accum_out=total[:, n:n + 1]).then_inc(s_exp, 1)

                def evacuate(i):
                    kind, b, x = jobs[i]
                    n = place[i]
                    act.wait_ge(s_turned, n + 1)
                    if kind == "dispatch":
                        act.activation(dispatch[:, :, x * SLOTS:(x + 1) * SLOTS],
                                       c.psum[:, TURN_BANK, :].rearrange("p (q s) -> p q s", q=QT), ACT.Copy).then_inc(s_out, 1)
                    else:
                        act.activation(combine[:, :, b * QT + x, :],
                                       c.psum[:, TURN_BANK:TURN_BANK + 2, :].rearrange("p h (e n) -> p (h e) n", n=P),
                                       ACT.Copy).then_inc(s_out, 1)

                def slots(i):
                    _, b, k = jobs[i]
                    act.wait_ge(s_full, i + 1)
                    pair = 2 * (i % DEEP)
                    act.activation(slots_T[:, :, k, b * SLOTS:(b + 1) * SLOTS],
                                   c.psum[:, pair:pair + 2, :].rearrange("p h (e n) -> p (h e) n", n=SLOTS),
                                   ACT.Copy).then_inc(s_slots, 1)

                for i in range(len(jobs) + 2):
                    if i in place:
                        exps(i)
                    if i - 2 in place:
                        evacuate(i - 2)
                    if i < len(jobs) and i not in place:
                        slots(i)


def token_moe(c, before, block_in, after, rows_dram, rows_filled):
    nc, a = c.nc, c.args
    results_dram = c.dram("expert_results", (TILES * P, D))
    with ExitStack() as ctx:
        def keep(n, shape, dt=F32):
            return ctx.enter_context(nc.sbuf_tensor(f"routed_{n}", shape, dt))

        gate_in = ctx.enter_context(nc.semaphore("routed_gate_in"))
        up_in = ctx.enter_context(nc.semaphore("routed_up_in"))
        down_in = ctx.enter_context(nc.semaphore("routed_down_in"))
        share = keep("share", [P, NT, 2])
        place = keep("place", [P, 2, NT], U32)
        expert_of = keep("expert_of", [P, TILES], U32)
        gate_w, gate_b, down_b = keep("gate_w", [P, DK, EXPERTS]), keep("gate_b", [P, EXPERTS]), keep("b2", [EXPERTS, D])
        gate_loads = [(gate_w[:, :, :], a["L1_ffn_gate_W"].rearrange("(k p) e -> p k e", p=P), gate_in),
                      (gate_b[:, :], a["L1_ffn_gate_b"].partition_broadcast(P), gate_in),
                      (down_b[:, :], a["L1_ffn_exp_b2"], gate_in)]
        with ExitStack() as inner:
            up = inner.enter_context(nc.sbuf_tensor("routed_up", [P, EXPERTS, DK, HID], F32))
            down = inner.enter_context(nc.sbuf_tensor("routed_down", [P, EXPERTS, HM, D], F32))
            up_loads = [(up[:, e, :, :], a["L1_ffn_exp_W1"][e].rearrange("(k p) n -> p k n", p=P), up_in)
                        for e in range(EXPERTS)]
            down_loads = [(down[:, e, :, :], a["L1_ffn_exp_W2"][e].rearrange("(m p) n -> p m n", p=P), down_in)
                          for e in range(EXPERTS)]
            stage_between(c, "gate_in", affine=(a["L1_ffn_ln2_g"], a["L1_ffn_ln2_b"]), rows_to=c.rows,
                          prefetch=gate_loads + up_loads, **before)
            stage_gate(c, gate_w, gate_b, down_b, gate_in, share, place, expert_of, block_in, c.rows,
                       rows_dram, rows_filled, prefetch=down_loads)
            stage_routed_experts(c, up, up_in, down, down_in, expert_of, rows_dram, results_dram)
        stage_between(c, "last", front=("gather", share, place, results_dram), **after)


@staged
def stage_routed_experts(c, up, up_in, down, down_in, expert_of, rows_dram, results_dram):
    nc, a = c.nc, c.args
    HALVES = HID // BANK
    PER = BANK // P
    X_BANK, UP_BANK, TURN_BANK, DOWN_BANK = 0, 1, 3, 5
    with ExitStack() as ctx:
        def sb(n, shape, dt=F32):
            return ctx.enter_context(nc.sbuf_tensor(f"routed_{n}", shape, dt))

        def sem(n):
            return c.sem(f"routed_{n}")

        bias = sb("bias", [P, EXPERTS * HM])
        rows = [sb(f"rows{i}", [P, D]) for i in range(2)]
        rows_T = [sb(f"rows_T{i}", [P, DK, P]) for i in range(2)]
        quarter = [c.rows[:, QT * i:QT * (i + 1), :] for i in range(NT // QT)]
        raw = [x.rearrange("p t d -> p (t d)") for x in quarter[:2]]
        hidden = [x.rearrange("p t (k n) -> p (t k) n", n=P) for x in quarter[2:]]
        result = [sb(f"result{i}", [P, D]) for i in range(2)]
        rows_in, stored = [sem(f"rows_in{i}") for i in range(2)], [sem(f"stored{i}") for i in range(2)]
        bias_in, x_turned, x_read, up_full = sem("bias_in"), sem("x_turned"), sem("x_read"), sem("up_full")
        raw_read, h_turned, gelu_done = sem("raw_read"), sem("h_turned"), sem("gelu_done")
        y_full, y_read = sem("y_full"), sem("y_read")
        FIRST, PAIRS = 5, (TILES - 1 - 5) // 2

        def tile_at(s, pair, lag):
            t = s - lag
            if isinstance(pair, int) and not 0 <= t < TILES:
                return None
            return t + pair * 2, t % 2, t // 2 + pair

        def for_steps(eng, body):
            for s in range(FIRST):
                body(s, 0)
            with eng.Fori(0, PAIRS) as pair:
                for r in range(2):
                    body(FIRST + r, pair)
            for s in range(FIRST + 2 * PAIRS, TILES + 3):
                body(s, 0)

        def weights_of(eng, t):
            return eng.value_load(expert_of[0:1, bass.ds(t, 1)], min_val=0, max_val=EXPERTS - 1)

        with nc.Block() as block:
            @block.sync
            def _(sp):
                def load(at):
                    t, r, _ = at
                    wait_for(sp, x_turned, t - 1)
                    sp.dma_start(rows[r][:, :], rows_dram[bass.ds(t * P, P), :]).then_inc(rows_in[r], 16)

                def body(s, pair):
                    if ahead := tile_at(s, pair, -1):
                        load(ahead)
                    if done := tile_at(s, pair, 3):
                        t, r, _ = done
                        sp.wait_ge(y_read, t + 1)
                        sp.dma_start(results_dram[bass.ds(t * P, P), :], result[r][:, :]).then_inc(stored[r], 16)

                load(tile_at(0, 0, 0))
                sp.dma_start(bias[:, :].rearrange("p (e m) -> p e m", m=HM),
                             a["L1_ffn_exp_b1"].rearrange("e p m -> p e m")).then_inc(bias_in, 16)
                for_steps(sp, body)
                for r in range(2):
                    sp.wait_ge(stored[r], 16 * ((TILES + 1 - r) // 2))

            @block.tensor
            def _(pe):
                def body(s, pair):
                    if at := tile_at(s, pair, 0):
                        t, r, before = at
                        pe.wait_ge(rows_in[r], (before + 1) * 16)
                        wait_for(pe, x_read, t)
                        for k in range(DK):
                            ins = pe.transpose(c.psum[:, X_BANK, k * P:(k + 1) * P], rows[r][:, k * P:(k + 1) * P],
                                               c.ident[:, :])
                        ins.then_inc(x_turned, 1)
                    if at := tile_at(s, pair, 1):
                        t, r, _ = at
                        e = weights_of(pe, t)
                        pe.wait_ge(x_read, t + 1)
                        for h in range(HALVES):
                            wait_for(pe, raw_read, (t - 1) * HALVES + h + 1)
                            for k in range(DK):
                                ins = pe.matmul(c.psum[:, UP_BANK + h, :], rows_T[r][:, k, :],
                                                up[:, bass.ds(e, 1), k, h * BANK:(h + 1) * BANK].rearrange("p o n -> p (o n)"),
                                                start=k == 0, stop=k == DK - 1)
                            ins.then_inc(up_full, 1)
                    if at := tile_at(s, pair, 2):
                        t, r, _ = at
                        for h in range(HALVES):
                            pe.wait_ge(raw_read, t * HALVES + h + 1)
                            wait_for(pe, gelu_done, (t - 1) * HM + (h + 1) * PER)
                            for m in range(PER):
                                ins = pe.transpose(c.psum[:, TURN_BANK + h, m * P:(m + 1) * P],
                                                   raw[r][:, (h * PER + m) * P:(h * PER + m + 1) * P], c.ident[:, :])
                            ins.then_inc(h_turned, 1)
                    if at := tile_at(s, pair, 3):
                        t, r, _ = at
                        e = weights_of(pe, t)
                        wait_for(pe, y_read, t - 1)
                        pe.wait_ge(gelu_done, (t + 1) * HM)
                        for m in range(HM):
                            ins = pe.matmul(c.psum[:, DOWN_BANK + r, 0:D], hidden[r][:, m, :],
                                            down[:, bass.ds(e, 1), m, :].rearrange("p o n -> p (o n)"),
                                            start=m == 0, stop=m == HM - 1)
                        ins.then_inc(y_full, 1)

                pe.wait_ge(up_in, 16 * EXPERTS)
                for s in range(3):
                    body(s, 0)
                pe.wait_ge(down_in, 16 * EXPERTS)
                for s in range(3, FIRST):
                    body(s, 0)
                with pe.Fori(0, PAIRS) as pair:
                    for r in range(2):
                        body(FIRST + r, pair)
                for s in range(FIRST + 2 * PAIRS, TILES + 3):
                    body(s, 0)

            @block.vector
            def _(v):
                def body(s, pair):
                    if at := tile_at(s, pair, 0):
                        t, r, _ = at
                        v.wait_ge(x_turned, t + 1)
                        wait_for(v, up_full, (t - 1) * HALVES)
                        v.tensor_copy(rows_T[r][:, :, :].rearrange("p k n -> p (k n)"),
                                      c.psum[:, X_BANK, 0:D]).then_inc(x_read, 1)
                    if at := tile_at(s, pair, 1):
                        t, r, _ = at
                        wait_for(v, h_turned, (t - 1) * HALVES)
                        for h in range(HALVES):
                            v.wait_ge(up_full, t * HALVES + h + 1)
                            v.tensor_copy(raw[r][:, h * BANK:(h + 1) * BANK], c.psum[:, UP_BANK + h, :]).then_inc(raw_read, 1)
                    if at := tile_at(s, pair, 3):
                        t, r, before = at
                        v.wait_ge(y_full, t + 1)
                        wait_for(v, stored[r], before * 16)
                        v.tensor_copy(result[r][:, :], c.psum[:, DOWN_BANK + r, 0:D]).then_inc(y_read, 1)

                for_steps(v, body)

            @block.scalar
            def _(act):
                def body(s, pair):
                    if at := tile_at(s, pair, 2):
                        t, r, _ = at
                        e = weights_of(act, t)
                        wait_for(act, y_full, t - 1)
                        for m in range(HM):
                            if m % PER == 0:
                                act.wait_ge(h_turned, t * HALVES + m // PER + 1)
                            act.activation(hidden[r][:, m, :], c.psum[:, TURN_BANK + m // PER, m % PER * P:(m % PER + 1) * P],
                                           ACT.Gelu, bias=bias[:, bass.ds(e * HM + m, 1)]).then_inc(gelu_done, 1)

                act.wait_ge(bias_in, 16)
                for_steps(act, body)


@staged
def stage_gate(c, gate_w, gate_b, down_b, gate_in, share, place, expert_of, block_in, h_tok, rows_dram,
               rows_filled, prefetch):
    nc, a = c.nc, c.args
    E = EXPERTS
    with ExitStack() as ctx:
        def sb(n, shape, dt=F32):
            return ctx.enter_context(nc.sbuf_tensor(f"gate_{n}", shape, dt))

        def sem(n):
            return c.sem(f"gate_{n}")

        weight_T = c.xT[0:E, 0, :]
        logits, top = sb("logits", [P, NT, E]), sb("top", [P, NT, 8])
        at, at_f = sb("at", [P, NT, 8], U32), sb("at_f", [P, NT, 8])
        number = sb("number", [P, TILES])
        less = sb("less", [P, E, E])
        tri, ones = sb("tri", [P, P], BF16), sb("ones", [P, P], BF16)
        weight = sb("weight", [P, NT, E])
        both = sb("both", [P, NT, E], BF16)
        earlier = sb("earlier", [P, NT + 1, E], BF16)
        over = sb("over", [P, E, NT])
        count, tiles_of, last, first = sb("count", [P, E]), sb("tiles_of", [P, E]), sb("last", [P, E]), sb("first", [P, E])
        part, rank_at, picked = sb("part", [P, E, E]), sb("rank_at", [P, NT, E]), sb("picked", [P, NT, E])
        place_f, past, owner = sb("place_f", [P, 2, NT]), sb("past", [P, TILES, E]), sb("owner", [P, TILES])
        lead, ratio = sb("lead", [P, NT]), sb("ratio", [P, NT])
        pick = sb("pick", [P, 2, NT, E])
        s_full, s_dve, s_exp = sem("full"), sem("dve"), sem("exp")
        s_number, s_turned, s_out, s_bias = sem("number"), sem("turned"), sem("out"), sem("bias")
        s_bias_full, s_twice = sem("bias_full"), sem("twice")
        s_ranked, s_placed, s_sent = sem("ranked"), sem("placed"), sem("sent")
        LOGIT_BANK, RANK_BANK = 7, 3
        MASKS_DONE = 3 * NT + 10
        with nc.Block() as block:
            @block.sync
            def _(sp):
                for dst, src, sem_of in prefetch:
                    sp.dma_start(dst, src).then_inc(sem_of, 16)

            @block.gpsimd
            def _(pool):
                pool.iota(number[:, :], [[1, TILES]], base=0, channel_multiplier=0,
                          allow_small_or_imprecise_dtypes=True).then_inc(s_number, 1)
                pool.iota(less[:, :, :], [[1, E], [-1, E]], base=0, channel_multiplier=0,
                          allow_small_or_imprecise_dtypes=True).then_inc(s_number, 1)
                pool.memset(ones[:, :], 1.0).then_inc(s_number, 1)
                pool.wait_ge(s_number, 3)
                pool.affine_select(out=tri[:, :], in_=ones[:, :], compare_op=ALU.is_gt, fill=0.0, base=0,
                                   pattern=[[1, P]], channel_multiplier=-1).then_inc(s_number, 1)
                for t in range(NT):
                    pool.tensor_tensor(c.x_tok[:, t, :], c.x_tok[:, t, :], block_in[:, t, :], ALU.add).then_inc(s_twice, 1)
                pool.wait_ge(s_placed, 1)
                pool.wait_ge(rows_filled, 16 * (-(-TILES * P // T)))
                for t in range(NT):
                    for x in range(2):
                        pool.indirect_dma_start(rows_dram[:, :], bass.IndirectOffsetOnAxis(ap=place[:, x, t:t + 1], axis=0),
                                                h_tok[:, t, :], None).then_inc(s_sent, 16)
                pool.wait_ge(s_sent, 16 * 2 * NT)

            @block.tensor
            def _(pe):
                pe.wait_ge(gate_in, 48)
                for t in range(NT):
                    for k in range(DK):
                        ins = pe.matmul(c.psum[:, LOGIT_BANK, t * E:(t + 1) * E], c.xT[:, k, t * P:(t + 1) * P],
                                        gate_w[:, k, :], start=k == 0, stop=k == DK - 1)
                ins.then_inc(s_full, 1)
                pe.wait_ge(s_number, 4)
                pe.wait_ge(s_dve, MASKS_DONE)
                flat = both[:, :, :].rearrange("p t e -> p (t e)")
                pe.matmul(c.psum[:, RANK_BANK, 0:NT * E], tri[:, :], flat, start=True, stop=False)
                pe.matmul(c.psum[:, RANK_BANK, 0:NT * E], ones[:, :],
                          earlier[:, 0:NT, :].rearrange("p t e -> p (t e)"), start=False, stop=True)
                pe.matmul(c.psum[:, RANK_BANK, NT * E:(NT + 1) * E], ones[:, :], earlier[:, NT, :],
                          start=True, stop=True).then_inc(s_ranked, 1)
                pe.wait_ge(s_placed, 2)
                for t in range(NT):
                    ins = pe.transpose(c.psum[0:E, t // QT, t % QT * P:(t % QT + 1) * P], weight[:, t, :], c.ident[:, :])
                    ins.then_inc(s_turned, 1)
                for t in range(NT):
                    pe.wait_ge(s_out, t // QT + 1)
                    wait_for(pe, s_bias, t - 3)
                    pe.matmul(c.psum[:, 4 + t % 4, 0:D], weight_T[:, t * P:(t + 1) * P], down_b[:, :],
                              start=True, stop=True).then_inc(s_bias_full, 1)

            @block.scalar
            def _(act):
                act.wait_ge(s_dve, 2 * NT + 3)
                act.activation(ratio[:, :], lead[:, :], ACT.Exp).then_inc(s_exp, 1)
                for q in range(NT // QT):
                    act.wait_ge(s_turned, QT * (q + 1))
                    act.activation(weight_T[:, q * SEQ:(q + 1) * SEQ], c.psum[0:E, q, :], ACT.Copy).then_inc(s_out, 1)

            @block.vector
            def _(v):
                done = 0

                def step(ins, wait=True):
                    nonlocal done
                    ins.then_inc(s_dve, 1)
                    done += 1
                    if wait:
                        v.wait_ge(s_dve, done)

                v.wait_ge(gate_in, 48)
                v.wait_ge(s_full, 1)
                step(v.tensor_tensor(logits[:, :, :], c.psum[:, LOGIT_BANK, 0:NT * E].rearrange("p (t e) -> p t e", e=E),
                                     gate_b[:, :].unsqueeze(1).to_broadcast([P, NT, E]), ALU.add))
                for t in range(NT):
                    step(v.max(top[:, t, :], logits[:, t, :]), wait=t == NT - 1)
                for t in range(NT):
                    step(v.max_index(at[:, t, :], top[:, t, :], logits[:, t, :]), wait=t == NT - 1)
                step(v.tensor_copy(at_f[:, :, :], at[:, :, :]))
                step(v.tensor_tensor(lead[:, :], top[:, :, 1], top[:, :, 0], ALU.subtract))
                v.wait_ge(s_exp, 1)
                step(v.tensor_scalar(lead[:, :], ratio[:, :], 1.0, None, ALU.add))
                step(v.reciprocal(share[:, :, 0], lead[:, :]))
                step(v.tensor_tensor(share[:, :, 1], ratio[:, :], share[:, :, 0], ALU.mult))
                v.wait_ge(s_number, 4)
                for x in range(2):
                    numbers = number[:, 0:E].unsqueeze(1).to_broadcast([P, NT, E])
                    step(v.tensor_tensor(pick[:, x, :, :], numbers, at_f[:, :, x:x + 1].to_broadcast([P, NT, E]), ALU.is_equal),
                         wait=x == 1)
                step(v.tensor_tensor(both[:, :, :], pick[:, 0, :, :], pick[:, 1, :, :], ALU.add), wait=False)
                step(v.tensor_scalar(earlier[:, 0, :], number[:, 0:E], 0.0, None, ALU.mult))
                for t in range(NT):
                    step(v.tensor_tensor(earlier[:, t + 1, :], earlier[:, t, :], both[:, t, :], ALU.add))
                assert done == MASKS_DONE, done
                v.wait_ge(s_ranked, 1)
                step(v.tensor_scalar(count[:, :], c.psum[:, RANK_BANK, NT * E:(NT + 1) * E], 1.0 / P, None, ALU.mult))
                step(v.tensor_tensor(over[:, :, :], count[:, :].unsqueeze(2).to_broadcast([P, E, NT]),
                                     number[:, 0:NT].unsqueeze(1).to_broadcast([P, E, NT]), ALU.is_gt))
                step(v.tensor_reduce(tiles_of[:, :], over[:, :, :], axis=AX_X, op=ALU.add))
                step(v.scalar_tensor_tensor(part[:, :, :], less[:, :, :], 0.0,
                                            tiles_of[:, :].unsqueeze(1).to_broadcast([P, E, E]), ALU.is_ge, ALU.mult))
                step(v.tensor_reduce(last[:, :], part[:, :, :], axis=AX_X, op=ALU.add))
                step(v.tensor_tensor(first[:, :], last[:, :], tiles_of[:, :], ALU.subtract))
                step(v.scalar_tensor_tensor(rank_at[:, :, :], first[:, :].unsqueeze(1).to_broadcast([P, NT, E]), float(P),
                                            c.psum[:, RANK_BANK, 0:NT * E].rearrange("p (t e) -> p t e", e=E),
                                            ALU.mult, ALU.add))
                for x in range(2):
                    step(v.tensor_tensor(picked[:, :, :], pick[:, x, :, :], rank_at[:, :, :], ALU.mult))
                    step(v.tensor_reduce(place_f[:, x, :], picked[:, :, :], axis=AX_X, op=ALU.add))
                v.tensor_copy(place[:, :, :], place_f[:, :, :]).then_inc(s_placed, 1)
                step(v.tensor_tensor(past[:, :, :], last[:, :].unsqueeze(1).to_broadcast([P, TILES, E]),
                                     number[:, :].unsqueeze(2).to_broadcast([P, TILES, E]), ALU.is_le))
                step(v.tensor_reduce(owner[:, :], past[:, :, :], axis=AX_X, op=ALU.add))
                step(v.tensor_scalar(expert_of[:, :], owner[:, :], float(E - 1), None, ALU.min), wait=False)
                for x in range(2):
                    step(v.tensor_tensor(pick[:, x, :, :], pick[:, x, :, :], share[:, :, x:x + 1].to_broadcast([P, NT, E]),
                                         ALU.mult), wait=x == 1)
                v.tensor_tensor(weight[:, :, :], pick[:, 0, :, :], pick[:, 1, :, :], ALU.add).then_inc(s_placed, 1)
                for t in range(NT):
                    v.wait_ge(s_bias_full, t + 1)
                    v.wait_ge(s_twice, t + 1)
                    v.tensor_tensor(c.x_tok[:, t, :], c.psum[:, 4 + t % 4, 0:D], c.x_tok[:, t, :], ALU.add).then_inc(s_bias, 1)


def build(nc, args, out):
    with ExitStack() as ctx:
        c = Core(nc, ctx, args, out)
        a = args
        stage_load(c)
        q_dram = c.dram("q_parts", (2, BATCH * D, SEQ))
        k_self = c.dram("k_parts_self", (2, BATCH * D, SEQ))
        k_cross = c.dram("k_parts_cross", (2, BATCH * D, CTX_SEQ))
        v_self = c.dram("v_self", (NG, P, SEQ // P, GD))
        v_cross = c.dram("v_cross", (NG, P, CTX_SEQ // P, GD))

        def self_products(wq, wk, wv, bq, bk):
            return dict(project=(((wq, bq, q_dram), (wk, bk, k_self)), (wv, v_self)),
                        early=(q_dram, k_self, SEQ, True))

        def cross_products(wq, wk, wv, bq, bk):
            return dict(project=(((wq, bq, q_dram),), None), context=(((wk, bk, k_cross),), (wv, v_cross)),
                        early=(q_dram, k_cross, CTX_SEQ, False))

        w, bias = a["L0_attn_w_attn"], a["L0_attn_b_attn"]
        stage_between(c, "a0", **self_products(w[:, 0:D], w[:, D:2 * D], w[:, 2 * D:], bias[0:D], bias[D:2 * D]))
        stage_attention(c, "a0", q_dram, k_self, v_self, bias[2 * D:], c.rows, SEQ, True,
                        a["L0_attn_w_proj"], a["L0_attn_b_proj"])
        wq, wk, wv, bq, bk, bv, wo, bo = (a[f"L0_xattn_{x}"] for x in ("Wq", "Wk", "Wv", "bq", "bk", "bv", "Wo", "bo"))
        stage_between(c, "c0", front=("output", c.rows, True), layernorm=True,
                      **cross_products(wq, wk, wv, bq, bk))
        stage_attention(c, "c0", q_dram, k_cross, v_cross, bv, c.rows, CTX_SEQ, False, wo, bo)
        w = a["L1_attn_w_qkv"]
        soft_moe(c, "soft", before=dict(front=("output", c.rows, True), layernorm=True),
                 after=dict(layernorm=True, **self_products(w[:, 0:D], w[:, D:2 * D], w[:, 2 * D:], None, None)))
        stage_attention(c, "a1", q_dram, k_self, v_self, None, c.rows, SEQ, True, a["L1_attn_w_o"], None)
        wq, wk, wv, bq, bk, bv, wo, bo = (a[f"L1_xattn_{x}"] for x in ("wq", "wk", "wv", "bq", "bk", "bv", "wo", "bo"))
        stage_between(c, "c1", front=("output", c.rows, False), layernorm=True,
                      **cross_products(wq, wk, wv, bq, bk))
        stage_attention(c, "c1", q_dram, k_cross, v_cross, bv, c.rows, CTX_SEQ, False, wo, bo)
        rows_dram = c.dram("expert_rows", (TILES * P, D))
        rows_filled = ctx.enter_context(nc.semaphore("rows_filled"))
        x_rows = a["x"].rearrange("b s d -> (b s) d")
        fills = [(rows_dram[at:min(at + T, TILES * P), :], x_rows[0:min(T, TILES * P - at), :], rows_filled)
                 for at in range(0, TILES * P, T)]
        block_in = c.keep("block_in", [P, NT, D])
        wq, wk, wv, bq, bk, bv, wp, bp = (a[f"L1_ffn_{x}"] for x in ("Wq", "Wk", "Wv", "bq", "bk", "bv", "Wp", "bp"))
        stage_between(c, "a2", front=("output", c.rows, True), layernorm=True, copy_to=block_in,
                      affine=(a["L1_ffn_ln1_g"], a["L1_ffn_ln1_b"]), rows_to=c.rows,
                      prefetch=fills, **self_products(wq, wk, wv, bq, bk))
        stage_attention(c, "a2", q_dram, k_self, v_self, bv, c.rows, SEQ, True, wp, bp)
        token_moe(c, dict(front=("output", c.rows, True)), block_in, dict(layernorm=True, out=out),
                  rows_dram, rows_filled)


TRANSPOSED = ("L0_attn_w_attn", "L0_attn_w_proj", "L0_xattn_Wq", "L0_xattn_Wk", "L0_xattn_Wv", "L0_xattn_Wo")


def kernel(**inputs):
    import concourse.bacc as bacc
    from concourse.bass_utils import run_bass_kernel_spmd

    nc = bacc.Bacc("TRN2", target_bir_lowering=False, num_devices=1)
    arrays, args = {}, {}
    for name, value in inputs.items():
        a = np.asarray(value)
        if name in TRANSPOSED:
            a = a.T
        if name == "ctx_768":
            name, a = "ctxT", a.reshape(CT, CTX_D).T
        if name in ("L0_ffn_b1", "L1_ffn_exp_b1"):
            a = a.reshape(EXPERTS, HM, P).transpose(0, 2, 1)
        a = np.ascontiguousarray(a)
        arrays[f"in_{name}"] = a
        args[name] = nc.dram_tensor(f"in_{name}", a.shape, mybir.dt.from_np(a.dtype), kind="ExternalInput").ap()
    out = nc.dram_tensor("out", (BATCH, SEQ, D), F32, kind="ExternalOutput").ap()
    build(nc, args, out)
    r = run_bass_kernel_spmd(nc, [arrays], core_ids=[0])
    return r.results[0]["out"]
```
